# Optimizing a Trainium2 kernel written in Bass

```python
import numpy as np
import jax
import jax.numpy as jnp

def _softmax(x, axis=-1):
    return jax.nn.softmax(x, axis=axis)

def _gelu(x):
    return jax.nn.gelu(x, approximate=True)

def _silu(x):
    return jax.nn.silu(x)

def _sigmoid(x):
    return jax.nn.sigmoid(x)

def _layernorm(x, axis=-1, eps=1e-05):
    m = jnp.mean(x, axis=axis, keepdims=True)
    v = jnp.var(x, axis=axis, keepdims=True)
    return (x - m) / jnp.sqrt(v + eps)

def _scatter_add(tgt, idx, src, axis=0):
    return tgt.at[idx].add(src)

def _segment_sum(src, seg, n):
    return jax.ops.segment_sum(src, seg, n)
kernel_name = 'mk_seq_preln_d1_jaxref_r8_55034d'

def setup_inputs(seed: int=0):
    np.random.seed(seed)
    _w = jnp.asarray

    def _L0_attn_setup():
        import jax, jax.numpy as jnp
        import numpy as np
        HID = 256
        NH = 32
        QLR = 192
        KVLR = 64
        DR = 64
        DN = 128
        DV = 128
        DQK = DN + DR
        EPS = 1e-06
        ROPE_BASE = 10000.0

        def rms_norm(x, w):
            return x * jax.lax.rsqrt(jnp.mean(x * x, axis=-1, keepdims=True) + EPS) * w

        def apply_rope(x, pos):
            d = x.shape[-1]
            inv_freq = 1.0 / ROPE_BASE ** (jnp.arange(0, d, 2, dtype=jnp.float32) / d)
            freqs = pos[:, None].astype(jnp.float32) * inv_freq
            cos = jnp.cos(freqs)[None, :, None, :]
            sin = jnp.sin(freqs)[None, :, None, :]
            x1, x2 = (x[..., :d // 2], x[..., d // 2:])
            return jnp.concatenate([x1 * cos - x2 * sin, x1 * sin + x2 * cos], axis=-1)
        key = jax.random.key(seed)
        ks = jax.random.split(key, 8)
        s = 0.02
        return {'hidden_states': jax.random.normal(ks[0], (1, 256, HID), jnp.float32), 'q_a_w': jax.random.normal(ks[1], (HID, QLR), jnp.float32) * s, 'q_a_ln_w': jnp.ones((QLR,), jnp.float32), 'q_b_w': jax.random.normal(ks[2], (QLR, NH * DQK), jnp.float32) * s, 'kv_a_w': jax.random.normal(ks[3], (HID, KVLR + DR), jnp.float32) * s, 'kv_a_ln_w': jnp.ones((KVLR,), jnp.float32), 'kv_b_w': jax.random.normal(ks[4], (KVLR, NH * (DN + DV)), jnp.float32) * s, 'o_w': jax.random.normal(ks[5], (NH * DV, HID), jnp.float32) * s}
    _L0_attn_in = _L0_attn_setup()

    def _L0_ffn_setup():
        import jax, jax.numpy as jnp
        import numpy as np
        EPS = 1e-05
        ROPE_BASE = 150000.0
        NHEADS = 32
        KVHEADS = 8
        HEAD_DIM = 64
        TOP_K = 4

        def _rms(x, w):
            return x * jax.lax.rsqrt(jnp.mean(x * x, -1, keepdims=True) + EPS) * w

        def _rope(q, k):
            S, hd = (q.shape[1], q.shape[-1])
            half = hd // 2
            inv = 1.0 / ROPE_BASE ** (jnp.arange(half, dtype=jnp.float32) / half)
            ang = jnp.arange(S, dtype=jnp.float32)[:, None] * inv
            cos = jnp.concatenate([jnp.cos(ang), jnp.cos(ang)], -1)[None, :, None, :]
            sin = jnp.concatenate([jnp.sin(ang), jnp.sin(ang)], -1)[None, :, None, :]

            def rot(t):
                t1, t2 = (t[..., :half], t[..., half:])
                return jnp.concatenate([-t2, t1], -1)
            return (q * cos + rot(q) * sin, k * cos + rot(k) * sin)
        key = jax.random.key(seed)
        ks = jax.random.split(key, 12)
        B, S, D, H, E = (1, 128, 256, 256, 16)
        s = 0.02
        return {'x': jax.random.normal(ks[0], (B, S, D), jnp.float32), 'ln_w': jnp.ones((D,), jnp.float32), 'ff_ln_w': jnp.ones((D,), jnp.float32), 'wq': jax.random.normal(ks[1], (D, NHEADS * HEAD_DIM), jnp.float32) * s, 'wk': jax.random.normal(ks[2], (D, KVHEADS * HEAD_DIM), jnp.float32) * s, 'wv': jax.random.normal(ks[3], (D, KVHEADS * HEAD_DIM), jnp.float32) * s, 'wo': jax.random.normal(ks[4], (NHEADS * HEAD_DIM, D), jnp.float32) * s, 'wg': jax.random.normal(ks[5], (D, E), jnp.float32) * s, 'w1': jax.random.normal(ks[6], (E, D, H), jnp.float32) * s, 'w3': jax.random.normal(ks[7], (E, D, H), jnp.float32) * s, 'w2': jax.random.normal(ks[8], (E, H, D), jnp.float32) * s}
    _L0_ffn_in = _L0_ffn_setup()
    _d = {'L0_attn_hidden_states': _L0_attn_in['hidden_states'], 'L0_attn_q_a_w': _L0_attn_in['q_a_w'], 'L0_attn_q_a_ln_w': _L0_attn_in['q_a_ln_w'], 'L0_attn_q_b_w': _L0_attn_in['q_b_w'], 'L0_attn_kv_a_w': _L0_attn_in['kv_a_w'], 'L0_attn_kv_a_ln_w': _L0_attn_in['kv_a_ln_w'], 'L0_attn_kv_b_w': _L0_attn_in['kv_b_w'], 'L0_attn_o_w': _L0_attn_in['o_w'], 'L0_ffn_ln_w': _L0_ffn_in['ln_w'], 'L0_ffn_ff_ln_w': _L0_ffn_in['ff_ln_w'], 'L0_ffn_wq': _L0_ffn_in['wq'], 'L0_ffn_wk': _L0_ffn_in['wk'], 'L0_ffn_wv': _L0_ffn_in['wv'], 'L0_ffn_wo': _L0_ffn_in['wo'], 'L0_ffn_wg': _L0_ffn_in['wg'], 'L0_ffn_w1': _L0_ffn_in['w1'], 'L0_ffn_w3': _L0_ffn_in['w3'], 'L0_ffn_w2': _L0_ffn_in['w2']}
    _x0 = _d['L0_attn_hidden_states']
    _d['L0_attn_hidden_states'] = jax.random.normal(jax.random.fold_in(jax.random.key(seed), 1), (4, 512, 256), dtype=_x0.dtype)
    del _x0
    return _d

def reference(L0_attn_hidden_states, L0_attn_q_a_w, L0_attn_q_a_ln_w, L0_attn_q_b_w, L0_attn_kv_a_w, L0_attn_kv_a_ln_w, L0_attn_kv_b_w, L0_attn_o_w, L0_ffn_ln_w, L0_ffn_ff_ln_w, L0_ffn_wq, L0_ffn_wk, L0_ffn_wv, L0_ffn_wo, L0_ffn_wg, L0_ffn_w1, L0_ffn_w3, L0_ffn_w2):

    def _L0_attn_ref(hidden_states, q_a_w, q_a_ln_w, q_b_w, kv_a_w, kv_a_ln_w, kv_b_w, o_w):
        import jax, jax.numpy as jnp
        import numpy as np
        HID = 256
        NH = 32
        QLR = 192
        KVLR = 64
        DR = 64
        DN = 128
        DV = 128
        DQK = DN + DR
        EPS = 1e-06
        ROPE_BASE = 10000.0

        def rms_norm(x, w):
            return x * jax.lax.rsqrt(jnp.mean(x * x, axis=-1, keepdims=True) + EPS) * w

        def apply_rope(x, pos):
            d = x.shape[-1]
            inv_freq = 1.0 / ROPE_BASE ** (jnp.arange(0, d, 2, dtype=jnp.float32) / d)
            freqs = pos[:, None].astype(jnp.float32) * inv_freq
            cos = jnp.cos(freqs)[None, :, None, :]
            sin = jnp.sin(freqs)[None, :, None, :]
            x1, x2 = (x[..., :d // 2], x[..., d // 2:])
            return jnp.concatenate([x1 * cos - x2 * sin, x1 * sin + x2 * cos], axis=-1)
        B, S, _ = hidden_states.shape
        q = rms_norm(hidden_states @ q_a_w, q_a_ln_w) @ q_b_w
        q = q.reshape(B, S, NH, DQK)
        q_pass, q_rot = (q[..., :DN], q[..., DN:])
        ckv = hidden_states @ kv_a_w
        c_kv, k_rot = (ckv[..., :KVLR], ckv[..., KVLR:])
        kv = rms_norm(c_kv, kv_a_ln_w) @ kv_b_w
        kv = kv.reshape(B, S, NH, DN + DV)
        k_pass, v = (kv[..., :DN], kv[..., DN:])
        pos = jnp.arange(S)
        q_rot = apply_rope(q_rot, pos)
        k_rot = apply_rope(k_rot[:, :, None, :], pos)[:, :, 0, :]
        scale = DQK ** (-0.5)
        scores = (jnp.einsum('bqhd,bkhd->bhqk', q_pass, k_pass) + jnp.einsum('bqhd,bkd->bhqk', q_rot, k_rot)) * scale
        causal = jnp.tril(jnp.ones((S, S), dtype=bool))
        scores = jnp.where(causal[None, None], scores, jnp.finfo(scores.dtype).min)
        p = jax.nn.softmax(scores, axis=-1)
        out = jnp.einsum('bhqk,bkhd->bqhd', p, v).reshape(B, S, NH * DV)
        return out @ o_w

    def _L0_ffn_ref(x, ln_w, ff_ln_w, wq, wk, wv, wo, wg, w1, w3, w2):
        import jax, jax.numpy as jnp
        import numpy as np
        EPS = 1e-05
        ROPE_BASE = 150000.0
        NHEADS = 32
        KVHEADS = 8
        HEAD_DIM = 64
        TOP_K = 4

        def _rms(x, w):
            return x * jax.lax.rsqrt(jnp.mean(x * x, -1, keepdims=True) + EPS) * w

        def _rope(q, k):
            S, hd = (q.shape[1], q.shape[-1])
            half = hd // 2
            inv = 1.0 / ROPE_BASE ** (jnp.arange(half, dtype=jnp.float32) / half)
            ang = jnp.arange(S, dtype=jnp.float32)[:, None] * inv
            cos = jnp.concatenate([jnp.cos(ang), jnp.cos(ang)], -1)[None, :, None, :]
            sin = jnp.concatenate([jnp.sin(ang), jnp.sin(ang)], -1)[None, :, None, :]

            def rot(t):
                t1, t2 = (t[..., :half], t[..., half:])
                return jnp.concatenate([-t2, t1], -1)
            return (q * cos + rot(q) * sin, k * cos + rot(k) * sin)
        B, S, D = x.shape
        h = _rms(x, ln_w)
        q = (h @ wq).reshape(B, S, NHEADS, HEAD_DIM)
        k = (h @ wk).reshape(B, S, KVHEADS, HEAD_DIM)
        v = (h @ wv).reshape(B, S, KVHEADS, HEAD_DIM)
        q, k = _rope(q, k)
        g = NHEADS // KVHEADS
        k = jnp.repeat(k, g, axis=2)
        v = jnp.repeat(v, g, axis=2)
        scores = jnp.einsum('bqhd,bkhd->bhqk', q, k) / np.float32(np.sqrt(HEAD_DIM))
        causal = jnp.tril(jnp.ones((S, S), bool))
        scores = jnp.where(causal[None, None], scores, jnp.float32(-1e+30))
        attn = jax.nn.softmax(scores, -1)
        o = jnp.einsum('bhqk,bkhd->bqhd', attn, v).reshape(B, S, NHEADS * HEAD_DIM)
        x = x + o @ wo
        h = _rms(x, ff_ln_w)
        logits = h @ wg
        topv, topi = jax.lax.top_k(logits, TOP_K)
        gate = jax.nn.softmax(topv, -1)
        bidx = jnp.arange(B)[:, None, None]
        sidx = jnp.arange(S)[None, :, None]
        weights = jnp.zeros_like(logits).at[bidx, sidx, topi].set(gate)
        a = jax.nn.silu(jnp.einsum('bsd,edh->bseh', h, w1)) * jnp.einsum('bsd,edh->bseh', h, w3)
        y = jnp.einsum('bseh,ehd->bsed', a, w2)
        moe = jnp.einsum('bsed,bse->bsd', y, weights)
        return x + moe
    x = L0_attn_hidden_states
    x = x + _L0_attn_ref(_layernorm(x, axis=-1), L0_attn_q_a_w, L0_attn_q_a_ln_w, L0_attn_q_b_w, L0_attn_kv_a_w, L0_attn_kv_a_ln_w, L0_attn_kv_b_w, L0_attn_o_w)
    x = x + _L0_ffn_ref(_layernorm(x, axis=-1), L0_ffn_ln_w, L0_ffn_ff_ln_w, L0_ffn_wq, L0_ffn_wk, L0_ffn_wv, L0_ffn_wo, L0_ffn_wg, L0_ffn_w1, L0_ffn_w3, L0_ffn_w2)
    return x

_drawn_inputs = setup_inputs


def setup_inputs(seed=0):
    import zlib

    import numpy as np

    out = dict(_drawn_inputs(seed))
    spreads = {'L0_attn_q_a_ln_w': (1.0, 0.6),
     'L0_attn_kv_a_ln_w': (1.0, 0.6),
     'L0_ffn_ln_w': (1.0, 0.6),
     'L0_ffn_ff_ln_w': (1.0, 0.6)}
    factors = {'L0_attn_q_a_w': 8.0,
     'L0_attn_q_b_w': 8.0,
     'L0_ffn_wq': 8.0,
     'L0_ffn_wk': 8.0,
     'L0_ffn_wv': 3.291,
     'L0_ffn_wo': 3.317,
     'L0_ffn_wg': 8.0,
     'L0_ffn_w1': 8.0,
     'L0_ffn_w3': 8.0,
     'L0_ffn_w2': 8.0}
    for name, (base, spread) in spreads.items():
        noise = np.random.default_rng([zlib.crc32(name.encode()), seed]).standard_normal(out[name].shape)
        drawn = base * np.exp(spread * noise) if base else spread * noise
        out[name] = jnp.asarray(drawn.astype(out[name].dtype))
    for name, factor in factors.items():
        out[name] = (out[name] * factor).astype(out[name].dtype)
    return out
```

```python
from contextlib import ExitStack

import numpy as np

import concourse.bass as bass
from concourse import mybir

F32 = mybir.dt.float32
F32R = mybir.dt.float32r
U32 = mybir.dt.uint32
ALU = mybir.AluOpType
ACT = mybir.ActivationFunctionType
AX_X = mybir.AxisListType.X

P = 128
B, S, D = 4, 512, 256
NT = S // P
TILES = B * NT
KT = D // P
NH = 32
QLR, KVLR, DR, DN, DV = 192, 64, 64, 128, 128
HD, KVH = 64, 8
E, TOPK, H = 16, 4, 256
HALF = 32
BODY = 8
Q_RING = 5
ROUNDS = NH // BODY
N_ROUNDS = B * ROUNDS
MASKED = -1.0e30
BIG = 3.0e38
LN_EPS, MLA_EPS, FFN_EPS = 1e-5, 1e-6, 1e-5

P_OFF = [0, 128, 384, 768]
P_ALL = 1280
SCORE_UNITS = [[(3, 0)], [(0, 0), (2, 128)], [(1, 0)]]
PT_OFF = [0, 512, 896, 1152]
TRANS_UNITS = [[(0, 0)], [(1, 0), (3, 384)], [(2, 0)]]


def wait_alone(eng, sem, value, passed):
    eng.wait_ge(sem, value)
    eng.sem_inc(passed, 1)


class Sems:

    def __init__(self, nc, ctx, prefix):
        self.nc, self.ctx, self.prefix = nc, ctx, prefix

    def __call__(self, name):
        return self.ctx.enter_context(self.nc.semaphore(f"{self.prefix}_{name}"))


def prepare_latent_weights(nc, sems, hbm, w, ident):
    with ExitStack() as ctx:
        def sb(name, shape, dt=F32):
            return ctx.enter_context(nc.sbuf_tensor("lw_" + name, shape, dt))

        def psum(name):
            return ctx.enter_context(nc.psum_tensor("lw_" + name, [P, 512], F32))

        raw_q1 = [sb(f"raw_q1{u}", [P, 2, DN + DR]) for u in range(2)]
        raw_q2 = [sb(f"raw_q2{u}", [P, 2, DN + DR]) for u in range(2)]
        raw_kv = [sb(f"raw_kv{u}", [KVLR, 2, DN + DV]) for u in range(2)]
        raw_o = [sb(f"raw_o{u}", [P, 2, D]) for u in range(2)]
        q_t = [sb(f"q_t{u}", [P, 2, 2, P]) for u in range(2)]
        kv_t = [sb(f"kv_t{u}", [P, 2, 2, KVLR]) for u in range(2)]
        ps_q = [psum(f"ps_q{u}") for u in range(2)]
        ps_kv = [psum(f"ps_kv{u}") for u in range(2)]
        ps_w = [psum(f"ps_w{u}") for u in range(2)]
        ps_vo = [psum(f"ps_vo{u}") for u in range(2)]

        raw_loaded = [sems(f"raw_loaded{u}") for u in range(2)]
        turned = sems("turned")
        q_turned = sems("q_turned")
        kv_turned = sems("kv_turned")
        multiplied = sems("multiplied")
        hi_done = sems("hi_done")
        lo_done = sems("lo_done")
        PAIRS = NH // 4

        wq_dram = hbm["L0_attn_q_b_w"].rearrange("r (i u h n) -> i u r h n", i=PAIRS, u=2, h=2)
        kvb_dram = hbm["L0_attn_kv_b_w"].rearrange("r (i u h n) -> i u r h n", i=PAIRS, u=2, h=2)
        o_dram = hbm["L0_attn_o_w"].rearrange("(i u h p) n -> i u p h n", i=PAIRS, u=2, h=2)

        def view(t):
            return t[:].rearrange("p (i u h n) -> p i u h n", i=PAIRS, u=2, h=2)

        w1hi, w1lo, w2hi, w2lo = (view(w[n]) for n in ("w1hi", "w1lo", "w2hi", "w2lo"))
        vohi, volo = (w[n][:].rearrange("p (i u) n -> p i u n", u=2) for n in ("vohi", "volo"))
        block = ctx.enter_context(nc.Block())

        @block.sync
        def _(sp):
            with sp.Fori(0, PAIRS) as i:
                done = sp.snap(i * 2)
                for u in range(2):
                    sp.wait_ge(lo_done, done + (u + 1))
                    sp.dma_start(raw_q1[u][:], wq_dram[i, u, 0:P]).then_inc(raw_loaded[u], 16)
                    sp.dma_start(raw_q2[u][0:64], wq_dram[i, u, P:QLR]).then_inc(raw_loaded[u], 16)
                    sp.dma_start(raw_q2[u][64:P], wq_dram[i, u, P:QLR]).then_inc(raw_loaded[u], 16)
                    sp.dma_start(raw_kv[u][:], kvb_dram[i, u]).then_inc(raw_loaded[u], 16)
                    sp.dma_start(raw_o[u][:], o_dram[i, u]).then_inc(raw_loaded[u], 16)

        @block.tensor
        def _(pe):
            with pe.Fori(0, PAIRS) as i:
                base = pe.snap(i * 2)
                loads = pe.snap(i * 80)
                for u in range(2):
                    pe.wait_ge(raw_loaded[u], loads + 80)
                    pe.wait_ge(lo_done, base + (u + 1))
                    for h in range(2):
                        nc.tensor.transpose(ps_q[u][:, 256 * h:256 * h + P], raw_q1[u][:, h, 0:DN], ident[:])
                        nc.tensor.transpose(ps_q[u][:, 256 * h + P:256 * h + 256], raw_q2[u][:, h, 0:DN], ident[:])
                        nc.tensor.transpose(ps_kv[u][:, 128 * h:128 * h + 64], raw_kv[u][:, h, 0:DN], ident[0:64, 0:64])
                        last = nc.tensor.transpose(ps_kv[u][:, 128 * h + 64:128 * h + 128], raw_kv[u][:, h, DN:DN + DV],
                                                   ident[0:64, 0:64])
                    last.then_inc(turned, 1)
                for u in range(2):
                    pe.wait_ge(q_turned, base + (u + 1))
                    pe.wait_ge(kv_turned, base + (u + 1))
                    for h in range(2):
                        for r in range(2):
                            nc.tensor.matmul(ps_w[u][:, 128 * h + 64 * r:128 * h + 64 * r + 64], q_t[u][:, h, r, :],
                                             kv_t[u][:, h, 0, :], start=True, stop=True)
                    for h in range(2):
                        last = nc.tensor.matmul(ps_vo[u][64 * h:64 * h + 64, 0:D], kv_t[u][:, h, 1, :], raw_o[u][:, h, :],
                                                start=True, stop=True)
                    last.then_inc(multiplied, 1)

        @block.scalar
        def _(act):
            with act.Fori(0, PAIRS) as i:
                base = act.snap(i * 2)
                for u in range(2):
                    act.wait_ge(turned, base + (u + 1))
                    nc.scalar.activation(q_t[u][:].rearrange("p h r n -> p (h r n)"), ps_q[u][:], ACT.Copy).then_inc(q_turned, 1)
                for u in range(2):
                    act.wait_ge(multiplied, base + (u + 1))
                    pw = ps_w[u][:, 0:256].rearrange("p (h r c) -> p h r c", h=2, r=2)
                    nc.scalar.activation(w1hi[:, i, u, :, 0:64], pw[:, :, 0, :], ACT.Copy)
                    nc.scalar.activation(w2hi[:, i, u, :, 0:64], pw[:, :, 1, :], ACT.Copy)
                    nc.scalar.activation(w1hi[:, i, u, :, 64:128], raw_q1[u][:, :, DN:DN + DR], ACT.Copy)
                    nc.scalar.activation(w2hi[:, i, u, :, 64:128], raw_q2[u][:, :, DN:DN + DR], ACT.Copy)
                    nc.scalar.activation(vohi[:, i, u, :], ps_vo[u][:, 0:D], ACT.Copy).then_inc(hi_done, 1)

        @block.vector
        def _(dve):
            dve.sem_inc(lo_done, 2)
            with dve.Fori(0, PAIRS) as i:
                base = dve.snap(i * 2)
                for u in range(2):
                    dve.wait_ge(turned, base + (u + 1))
                    nc.vector.tensor_copy(kv_t[u][:].rearrange("p h r n -> p (h r n)"), ps_kv[u][:, 0:256]).then_inc(kv_turned, 1)
                for u in range(2):
                    dve.wait_ge(hi_done, base + (u + 1))
                    pw = ps_w[u][:, 0:256].rearrange("p (h r c) -> p h r c", h=2, r=2)

                    def split(lo, x, hi):
                        return nc.vector.tensor_tensor(lo, x, hi.bitcast(F32), ALU.subtract)

                    split(w1lo[:, i, u, :, 0:64], pw[:, :, 0, :], w1hi[:, i, u, :, 0:64])
                    split(w2lo[:, i, u, :, 0:64], pw[:, :, 1, :], w2hi[:, i, u, :, 0:64])
                    split(w1lo[:, i, u, :, 64:128], raw_q1[u][:, :, DN:DN + DR], w1hi[:, i, u, :, 64:128])
                    split(w2lo[:, i, u, :, 64:128], raw_q2[u][:, :, DN:DN + DR], w2hi[:, i, u, :, 64:128])
                    split(volo[:, i, u, :], ps_vo[u][:, 0:D], vohi[:, i, u, :]).then_inc(lo_done, 1)


def start_constants(nc, sems, hbm, x_res, ident, mask, exponent):
    with ExitStack() as ctx:
        x_loaded, zeroed, made = sems("x_loaded"), sems("zeroed"), sems("made")
        block = ctx.enter_context(nc.Block())

        @block.sync
        def _(sp):
            sp.dma_start(x_res[:], hbm["L0_attn_hidden_states"].rearrange("b (j p) d -> p (b j) d", p=P)).then_inc(x_loaded, 16)
            sp.wait_ge(x_loaded, 16)

        @block.gpsimd
        def _(pool):
            nc.gpsimd.memset(ident[:], 0.0)
            nc.gpsimd.memset(exponent[:], -0.5)
            nc.gpsimd.memset(mask[:], 0.0).then_inc(zeroed, 1)
            pool.wait_ge(zeroed, 1)
            nc.gpsimd.affine_select(out=ident[:], in_=ident[:], compare_op=ALU.not_equal, fill=1.0, base=0,
                                    pattern=[[-1, P]], channel_multiplier=1)
            nc.gpsimd.affine_select(out=mask[:, 384:512], in_=mask[:, 384:512], compare_op=ALU.is_ge, fill=MASKED, base=0,
                                    pattern=[[-1, P]], channel_multiplier=1).then_inc(made, 1)
            pool.wait_ge(made, 1)


def latent_inputs(nc, sems, hbm, x_res, ident, exponent, scratch):
    with ExitStack() as ctx:
        def sb(name, shape, dt=F32):
            return ctx.enter_context(nc.sbuf_tensor("li_" + name, shape, dt))

        W = QLR + KVLR + DR
        wa = sb("wa", [P, KT, W])
        wa_hi, wa_lo = sb("wa_hi", [P, KT, W], F32R), sb("wa_lo", [P, KT, W], F32R)
        ln_w = sb("ln_w", [P, QLR + KVLR])
        rope = sb("rope", [P, 2, NT, DR])
        stats, mv = sb("stats", [P, NT, 6]), sb("mv", [P, NT, 2])
        var_eps, rstd = sb("var_eps", [P, NT]), sb("rstd", [P, NT])
        xn = sb("xn", [P, NT, D])
        xt_hi, xt_lo = sb("xt_hi", [P, NT, D], F32R), sb("xt_lo", [P, NT, D], F32R)
        square = sb("square", [P, NT, QLR + KVLR])
        ms, ms_eps, rms = sb("ms", [P, NT, 2]), sb("ms_eps", [P, NT, 2]), sb("rms", [P, NT, 2])
        qn, kv = sb("qn", [P, NT, 256]), sb("kv", [P, NT, P])
        rot_a, rot_b = sb("rot_a", [P, NT, DR]), sb("rot_b", [P, NT, DR])
        t_hi, t_lo = sb("t_hi", [P, 3, NT, P], F32R), sb("t_lo", [P, 3, NT, P], F32R)
        ps_t = [ctx.enter_context(nc.psum_tensor(f"li_ps_t{u}", [P, 512], F32)) for u in range(NT)]
        ps_p = [ctx.enter_context(nc.psum_tensor(f"li_ps_p{u}", [P, 512], F32)) for u in range(NT)]

        loaded, w_hi, w_lo = sems("loaded"), sems("w_hi"), sems("w_lo")
        bn, mean_var, eps_added, rstd_done, xn_done = (sems(n) for n in ("bn", "mean_var", "eps_added", "rstd_done", "xn_done"))
        xt_turned, xt_hi_done, xt_lo_done, projected = (sems(n) for n in ("xt_turned", "xt_hi_done", "xt_lo_done", "projected"))
        squared, ms_eps_added, rms_done, rotated, normed = (
            sems(n) for n in ("squared", "ms_eps_added", "rms_done", "rotated", "normed"))
        turned, hi_done, lo_done, stored, passed = (sems(n) for n in ("turned", "hi_done", "lo_done", "stored", "passed"))
        block = ctx.enter_context(nc.Block())
        N_LOADS, N_STORES = 6, 7

        @block.sync
        def _(sp):
            sp.dma_start(wa[:, :, 0:QLR], hbm["L0_attn_q_a_w"].rearrange("(k p) n -> p k n", p=P)).then_inc(loaded, 16)
            sp.dma_start(wa[:, :, QLR:W], hbm["L0_attn_kv_a_w"].rearrange("(k p) n -> p k n", p=P)).then_inc(loaded, 16)
            sp.dma_start(ln_w[:, 0:QLR], hbm["L0_attn_q_a_ln_w"].rearrange("(o n) -> o n", o=1).to_broadcast([P, QLR])).then_inc(loaded, 16)
            sp.dma_start(ln_w[:, QLR:], hbm["L0_attn_kv_a_ln_w"].rearrange("(o n) -> o n", o=1).to_broadcast([P, KVLR])).then_inc(loaded, 16)
            for k in range(2):
                sp.dma_start(rope[:, k], hbm["rope_latent"][k].rearrange("(j p) n -> p j n", p=P)).then_inc(loaded, 16)
            with sp.Fori(0, B) as b:
                done = sp.snap(b * NT)
                sp.wait_ge(hi_done, done + NT)
                flat = "p j n -> p (j n)"
                qs, kk = scratch["q_src"][b], scratch["k"][b]
                sp.dma_start(qs[:, 0], t_hi[:, 0].bitcast(F32).rearrange(flat)).then_inc(stored, 16)
                sp.dma_start(qs[0:64, 2], t_hi[0:64, 1].bitcast(F32).rearrange(flat)).then_inc(stored, 16)
                sp.dma_start(kk[:, 0], t_hi[:, 2].bitcast(F32).rearrange(flat)).then_inc(stored, 16)
                sp.wait_ge(lo_done, done + NT)
                sp.dma_start(qs[:, 1], t_lo[:, 0].bitcast(F32).rearrange(flat)).then_inc(stored, 16)
                sp.dma_start(qs[64:P, 2], t_lo[64:P, 1].bitcast(F32).rearrange(flat)).then_inc(stored, 16)
                sp.dma_start(kk[:, 1], t_lo[:, 2].bitcast(F32).rearrange(flat)).then_inc(stored, 16)
                sp.dma_start(scratch["v"][b], kv[:, :, 0:KVLR]).then_inc(stored, 16)
            sp.wait_ge(stored, 16 * N_STORES * (B + 1))

        @block.gpsimd
        def _(pool):
            pool.sem_inc(stored, 16 * N_STORES)
            with pool.Fori(0, B) as b:
                base = pool.snap(b * NT)
                for u in range(NT):
                    wait_alone(pool, mean_var, base + (u + 1), passed)
                    nc.gpsimd.tensor_scalar(var_eps[:, u:u + 1], mv[:, u, 1:2], LN_EPS, 1.0, ALU.add, ALU.mult).then_inc(eps_added, 1)
                    pool.wait_ge(eps_added, base + (u + 1))
                    nc.gpsimd.tensor_tensor(rstd[:, u:u + 1], var_eps[:, u:u + 1], exponent[:], ALU.pow).then_inc(rstd_done, 1)
                for u in range(NT):
                    wait_alone(pool, squared, base + (u + 1), passed)
                    nc.gpsimd.tensor_scalar(ms_eps[:, u, :], ms[:, u, :], MLA_EPS, 1.0, ALU.add, ALU.mult).then_inc(ms_eps_added, 1)
                    pool.wait_ge(ms_eps_added, base + (u + 1))
                    nc.gpsimd.tensor_tensor(rms[:, u, :], ms_eps[:, u, :], exponent[:].to_broadcast([P, 2]), ALU.pow).then_inc(rms_done, 1)

        @block.tensor
        def _(pe):
            pe.wait_ge(w_lo, 1)
            with pe.Fori(0, B) as b:
                base = pe.snap(b * NT)
                for u in range(NT):
                    pe.wait_ge(xn_done, base + (u + 1))
                    for k in range(KT):
                        last = nc.tensor.transpose(ps_t[u][:, P * k:P * k + P], xn[:, u, P * k:P * k + P], ident[:])
                    last.then_inc(xt_turned, 1)
                for u in range(NT):
                    pe.wait_ge(xt_lo_done, base + (u + 1))
                    n = 0
                    for k in range(KT):
                        for x, wt in ((xt_hi, wa_hi), (xt_hi, wa_lo), (xt_lo, wa_hi)):
                            last = nc.tensor.matmul(ps_p[u][:, 0:W], x[:, u, P * k:P * k + P], wt[:, k, :], start=(n == 0), stop=(n == 5))
                            n += 1
                    last.then_inc(projected, 1)
                for u in range(NT):
                    pe.wait_ge(normed, base + (u + 1))
                    nc.tensor.transpose(ps_t[u][:, 0:P], qn[:, u, 0:P], ident[:])
                    nc.tensor.transpose(ps_t[u][:, P:2 * P], qn[:, u, P:2 * P], ident[:])
                    nc.tensor.transpose(ps_t[u][:, 2 * P:3 * P], kv[:, u, :], ident[:]).then_inc(turned, 1)

        @block.scalar
        def _(act):
            act.wait_ge(loaded, 16 * N_LOADS)
            nc.scalar.activation(wa_hi[:], wa[:], ACT.Copy).then_inc(w_hi, 1)
            with act.Fori(0, B) as b:
                base = act.snap(b * NT)
                stores = act.snap(b * (16 * N_STORES))
                for u in range(NT):
                    act.wait_ge(xt_turned, base + (u + 1))
                    nc.scalar.activation(xt_hi[:, u, :], ps_t[u][:, 0:D], ACT.Copy).then_inc(xt_hi_done, 1)
                for u in range(NT):
                    act.wait_ge(projected, base + (u + 1))
                    nc.scalar.activation(square[:, u, 0:QLR], ps_p[u][:, 0:QLR], ACT.Square, scale=float(QLR) ** -0.5,
                                         accum_out=ms[:, u, 0:1])
                    nc.scalar.activation(square[:, u, QLR:], ps_p[u][:, QLR:QLR + KVLR], ACT.Square, scale=float(KVLR) ** -0.5,
                                         accum_out=ms[:, u, 1:2]).then_inc(squared, 1)
                act.wait_ge(stored, stores + 16 * N_STORES)
                for u in range(NT):
                    act.wait_ge(turned, base + (u + 1))
                    nc.scalar.activation(t_hi[:, :, u, :], ps_t[u][:, 0:3 * P].rearrange("p (k n) -> p k n", k=3), ACT.Copy)\
                        .then_inc(hi_done, 1)

        @block.vector
        def _(dve):
            dve.wait_ge(w_hi, 1)
            nc.vector.tensor_tensor(wa_lo[:], wa[:], wa_hi[:].bitcast(F32), ALU.subtract).then_inc(w_lo, 1)
            with dve.Fori(0, B) as b:
                base = dve.snap(b * NT)
                stores = dve.snap(b * (16 * N_STORES))
                xb = x_res[:].rearrange("p (b j) d -> p b j d", b=B)
                for u in range(NT):
                    nc.vector.bn_stats(stats[:, u, :], xb[:, b, u, :]).then_inc(bn, 1)
                for u in range(NT):
                    wait_alone(dve, bn, base + (u + 1), passed)
                    nc.vector.bn_aggr(mv[:, u, :], stats[:, u, :]).then_inc(mean_var, 1)
                for u in range(NT):
                    dve.wait_ge(rstd_done, base + (u + 1))
                    nc.vector.tensor_scalar(xn[:, u, :], xb[:, b, u, :], mv[:, u, 0:1], rstd[:, u:u + 1], ALU.subtract, ALU.mult)\
                        .then_inc(xn_done, 1)
                for u in range(NT):
                    dve.wait_ge(xt_hi_done, base + (u + 1))
                    nc.vector.tensor_tensor(xt_lo[:, u, :], ps_t[u][:, 0:D], xt_hi[:, u, :].bitcast(F32), ALU.subtract)\
                        .then_inc(xt_lo_done, 1)
                dve.wait_ge(stored, stores + 16 * N_STORES)
                for u in range(NT):
                    dve.wait_ge(rms_done, base + (u + 1))
                    q, c, kr = ps_p[u][:, 0:QLR], ps_p[u][:, QLR:QLR + KVLR], ps_p[u][:, QLR + KVLR:W]
                    nc.vector.tensor_tensor(rot_a[:, u, :], kr, rope[:, 0, u, :], ALU.mult)
                    nc.vector.tensor_tensor(rot_b[:, u, :].rearrange("p (t c) -> p t c", t=2),
                                            kr.rearrange("p (t c) -> p t c", t=2)[:, ::-1, :],
                                            rope[:, 1, u, :].rearrange("p (t c) -> p t c", t=2), ALU.mult).then_inc(rotated, 1)
                    nc.vector.scalar_tensor_tensor(out=qn[:, u, 0:P], in0=q[:, 0:P], scalar=rms[:, u, 0:1], in1=ln_w[:, 0:P],
                                                   op0=ALU.mult, op1=ALU.mult)
                    for k in range(2):
                        nc.vector.scalar_tensor_tensor(out=qn[:, u, P + 64 * k:P + 64 * k + 64], in0=q[:, P:QLR],
                                                       scalar=rms[:, u, 0:1], in1=ln_w[:, P:QLR], op0=ALU.mult, op1=ALU.mult)
                    nc.vector.scalar_tensor_tensor(out=kv[:, u, 0:KVLR], in0=c, scalar=rms[:, u, 1:2],
                                                   in1=ln_w[:, QLR:QLR + KVLR], op0=ALU.mult, op1=ALU.mult)
                    dve.wait_ge(rotated, base + (u + 1))
                    nc.vector.tensor_tensor(kv[:, u, KVLR:P], rot_a[:, u, :], rot_b[:, u, :], ALU.add).then_inc(normed, 1)
                for u in range(NT):
                    dve.wait_ge(hi_done, base + (u + 1))
                    nc.vector.tensor_tensor(t_lo[:, :, u, :], ps_t[u][:, 0:3 * P].rearrange("p (k n) -> p k n", k=3),
                                            t_hi[:, :, u, :].bitcast(F32), ALU.subtract).then_inc(lo_done, 1)


class Attention:

    def __init__(self, name, scale, q_slots, width, q_passes, k_slots, s_passes, out_hi, out_lo, scratch, rope):
        self.name, self.scale, self.q_slots, self.width = name, scale, q_slots, width
        self.q_passes, self.k_slots, self.s_passes = q_passes, k_slots, s_passes
        self.out_hi, self.out_lo, self.scratch, self.rope = out_hi, out_lo, scratch, rope


def attention(nc, sems, a, x_res, ident, mask):
    latent = a.width == 128
    with ExitStack() as ctx:
        def sb(name, shape, dt=F32):
            return ctx.enter_context(nc.sbuf_tensor(f"{a.name}_{name}", shape, dt))

        def psum(name):
            return ctx.enter_context(nc.psum_tensor(f"{a.name}_{name}", [P, 512], F32))

        q_src = sb("q_src", [P, a.q_slots, S], F32R)
        keys = [sb(f"keys{c}", [P, a.k_slots, S], F32R) for c in range(2)]
        values = [sb(f"values{c}", [P, NT, HD]) for c in range(2)]
        qt_hi, qt_lo = sb("qt_hi", [P, BODY, S], F32R), sb("qt_lo", [P, BODY, S], F32R)
        q_tok = [sb(f"q_tok{r}", [P, 4, P]) for r in range(Q_RING)]
        rot_a = [sb(f"rot_a{r}", [P, 4, DR]) for r in range(2)]
        rot_b = [sb(f"rot_b{r}", [P, 4, DR]) for r in range(2)]
        rope = sb("rope", [P, 2, NT, DR])
        probs = [sb(f"probs{r}", [P, P_ALL]) for r in range(2)]
        probs_t = [sb(f"probs_t{r}", [P, P_ALL]) for r in range(2)]
        neg_max = [sb(f"neg_max{r}", [P, NT]) for r in range(2)]
        total = [sb(f"total{r}", [P, NT]) for r in range(2)]
        inverse = [sb(f"inverse{r}", [P, NT]) for r in range(2)]
        ot_hi = [sb(f"ot_hi{r}", [P, S], F32R) for r in range(2)]
        ot_lo = [sb(f"ot_lo{r}", [P, S], F32R) for r in range(2)]
        ps_s = [psum(f"ps_s{r}") for r in range(2)]
        ps_t = [psum(f"ps_t{r}") for r in range(2)]
        ps_v, ps_q, ps_qt, ps_o = psum("ps_v"), psum("ps_q"), psum("ps_qt"), psum("ps_o")

        rope_loaded, q_src_loaded, passed = sems("rope_loaded"), sems("q_src_loaded"), sems("passed")
        k_loaded = [sems(f"k_loaded{c}") for c in range(2)]
        v_loaded = [sems(f"v_loaded{c}") for c in range(2)]
        scored, masked = sems("scored"), sems("masked")
        exped, inverted, scaled = sems("exped"), sems("inverted"), sems("scaled")
        turned, t_act, t_dve = sems("turned"), sems("t_act"), sems("t_dve")
        valued, o_hi_done, o_lo_done = sems("valued"), sems("o_hi_done"), sems("o_lo_done")
        out_done, added = sems("out_done"), sems("added")
        q_done, rope_read, nope_done, rope_added = sems("q_done"), sems("rope_read"), sems("nope_done"), sems("rope_added")
        q_turned, q_hi_done, q_lo_done = sems("q_turned"), sems("q_hi_done"), sems("q_lo_done")
        q_bank_read = nope_done if latent else rope_read
        block = ctx.enter_context(nc.Block())

        q_weights = [(slot, wt.rearrange("p (r c n) -> p r c n", r=ROUNDS, c=2)) for slot, wt in a.q_passes]
        out_w = [t[:].rearrange("p (r m) n -> p r m n", r=ROUNDS) for t in (a.out_hi, a.out_lo)]
        UQ = BODY

        def wait_q_tok(eng, u, unit):
            if u >= Q_RING:
                eng.wait_ge(q_turned, unit + (u - Q_RING + 1))
            elif not isinstance(unit, int):
                eng.wait_ge(q_turned, unit)

        @block.sync
        def _(sp):
            for k in range(2):
                sp.dma_start(rope[:, k], a.rope[k].rearrange("(j p) n -> p j n", p=P)).then_inc(rope_loaded, 16)
            sp.dma_start(q_src[:].bitcast(F32), a.scratch["q_src"][0]).then_inc(q_src_loaded, 16)

            def load_kv(c, b, r):
                kk, vv = (a.scratch["k"][b], a.scratch["v"][b]) if latent else \
                    (a.scratch["k"][b, r, c], a.scratch["v"][b, r, c])
                return kk, vv

            for c in range(2):
                kk, vv = load_kv(c, 0, 0)
                sp.dma_start(keys[c][:].bitcast(F32), kk).then_inc(k_loaded[c], 16)
                sp.dma_start(values[c][:], vv).then_inc(v_loaded[c], 16)

            def reload(done, b, r):
                for c in range(2):
                    kk, vv = load_kv(c, b, r)
                    sp.wait_ge(scored, done * 3 + 12 * (c + 1))
                    sp.dma_start(keys[c][:].bitcast(F32), kk).then_inc(k_loaded[c], 16)
                    sp.wait_ge(valued, done + 4 * (c + 1))
                    sp.dma_start(values[c][:], vv).then_inc(v_loaded[c], 16)

            with sp.Fori(0, B) as b:
                next_b = sp.snap((b + 1) & (B - 1))
                with sp.Fori(0, ROUNDS - 1) as r:
                    reload(sp.snap(b * (BODY * ROUNDS) + r * BODY), b, sp.snap(r + 1))
                done = sp.snap(b * (BODY * ROUNDS))
                wait_alone(sp, q_done, done + BODY * ROUNDS, passed)
                sp.dma_start(q_src[:].bitcast(F32), a.scratch["q_src"][next_b]).then_inc(q_src_loaded, 16)
                reload(sp.snap(b * (BODY * ROUNDS) + (ROUNDS - 1) * BODY), next_b, 0)
            sp.wait_ge(q_src_loaded, 16 * (B + 1))
            for c in range(2):
                sp.wait_ge(k_loaded[c], 16 * (N_ROUNDS + 1))
                sp.wait_ge(v_loaded[c], 16 * (N_ROUNDS + 1))

        @block.gpsimd
        def _(pool):
            pool.sem_inc(rope_added, 2)

            def rope_add(u, unit):
                pool.wait_ge(rope_read, unit + (u + 1) + (0 if latent else 1))
                wait_q_tok(pool, u, unit)
                if latent:
                    last = nc.gpsimd.tensor_tensor(q_tok[u % Q_RING][:, :, 64:P], rot_a[u % 2][:], rot_b[u % 2][:], ALU.add)
                else:
                    def twice(t):
                        return t[:].rearrange("p h (o n) -> p h o n", o=1).to_broadcast([P, 4, 2, HD])
                    last = nc.gpsimd.tensor_tensor(q_tok[u % Q_RING][:].rearrange("p h (o n) -> p h o n", o=2),
                                                   twice(rot_a[u % 2]), twice(rot_b[u % 2]), ALU.add)
                last.then_inc(rope_added, 1)

            for u in range(UQ):
                rope_add(u, 0)
            with pool.Fori(0, N_ROUNDS) as i:
                unit = pool.snap(i * UQ + UQ)
                heads = pool.snap(i * BODY)
                for k in range(BODY):
                    rope_add(k, unit)
                    wait_alone(pool, inverted, heads + (k + 1), passed)
                    for q in (3, 0, 2, 1):
                        n = P * (q + 1)
                        pr = probs[k % 2][:, P_OFF[q]:P_OFF[q] + n]
                        last = nc.gpsimd.tensor_scalar(pr, pr, inverse[k % 2][:, q:q + 1], 1.0, ALU.mult, ALU.mult)
                    last.then_inc(scaled, 1)

        @block.tensor
        def _(pe):
            def project(u, unit, nxt, loads):
                if loads is not None:
                    pe.wait_ge(q_src_loaded, loads)
                pe.wait_ge(q_bank_read, unit + (u + 1))
                for n, (slot, wt) in enumerate(q_weights):
                    last = nc.tensor.matmul(ps_q[:, 0:4 * a.width], q_src[:, slot, P * (u % 4):P * (u % 4) + P],
                                            wt[:, nxt, u // 4, :], start=(n == 0), stop=(n == len(q_weights) - 1))
                last.then_inc(q_done, 1)

            def turn_queries(u, unit):
                pe.wait_ge(rope_added, unit + (u + 1) + 2)
                if latent:
                    pe.wait_ge(nope_done, unit + (u + 1) + 1)
                pe.wait_ge(q_lo_done, unit + (u + 1))
                for h in range(4):
                    last = nc.tensor.transpose(ps_qt[:, P * h:P * h + P], q_tok[u % Q_RING][:, h, :], ident[:])
                last.then_inc(q_turned, 1)

            def scores(k, heads4, unit, rounds16):
                if k % 4 == 0:
                    pe.wait_ge(q_lo_done, unit + (k + 4 + 1 - UQ))
                    pe.wait_ge(k_loaded[k // 4], rounds16 + 16)
                for n, tiles in enumerate(SCORE_UNITS):
                    pe.wait_ge(masked, heads4 + (4 * k + 3 + n))
                    for q, col in tiles:
                        nk = P * (q + 1)
                        for m, (which, slot) in enumerate(a.s_passes):
                            qt = (qt_hi, qt_lo)[which]
                            last = nc.tensor.matmul(ps_s[(3 * k + n) % 2][:, col:col + nk], qt[:, k, P * q:P * q + P],
                                                    keys[k // 4][:, slot, 0:nk], start=(m == 0), stop=(m == len(a.s_passes) - 1))
                    last.then_inc(scored, 1)

            def turn_probs(k, heads, heads2):
                pe.wait_ge(scaled, heads + (k + 1))
                for n, blocks in enumerate(TRANS_UNITS):
                    if n == 0:
                        pe.wait_ge(t_dve, heads + (k + 1))
                    else:
                        pe.wait_ge(t_act, heads2 + (2 * k + n))
                    for j, col in blocks:
                        for q in range(j, NT):
                            last = nc.tensor.transpose(ps_t[(3 * k + n) % 2][:, col + P * (q - j):col + P * (q - j) + P],
                                                       probs[k % 2][:, P_OFF[q] + P * j:P_OFF[q] + P * j + P], ident[:])
                    last.then_inc(turned, 1)

            def apply(k, heads, heads2, pairs, rounds16):
                if k % 4 == 0:
                    pe.wait_ge(v_loaded[k // 4], rounds16 + 16)
                if k % 2 == 0:
                    pe.wait_ge(o_lo_done, pairs + (k // 2 + 1))
                pe.wait_ge(t_act, heads2 + (2 * k + 3))
                pe.wait_ge(t_dve, heads + (k + 2))
                row = 64 * (k % 2)
                for j in range(NT):
                    n = S - P * j
                    last = nc.tensor.matmul(ps_v[row:row + 64, P * j:S], values[k // 4][:, j, :],
                                            probs_t[k % 2][:, PT_OFF[j]:PT_OFF[j] + n], start=(j == 0), stop=(j == NT - 1))
                last.then_inc(valued, 1)

            def project_out(c, half, r, pairs):
                pe.wait_ge(o_lo_done, pairs + (2 * c + 2 + 1))
                pe.wait_ge(added, pairs + (2 * c + half + 1))
                for t in range(2):
                    j = 2 * half + t
                    n = 0
                    for e in range(2):
                        for ot, wt in ((ot_hi, 0), (ot_hi, 1), (ot_lo, 0)):
                            last = nc.tensor.matmul(ps_o[:, D * t:D * t + D], ot[e][:, P * j:P * j + P],
                                                    out_w[wt][:, r, 2 * c + e, :], start=(n == 0), stop=(n == 5))
                            n += 1
                last.then_inc(out_done, 1)

            for u in range(UQ):
                project(u, 0, 0, 16 if u == 0 else None)
                if u:
                    turn_queries(u - 1, 0)
            turn_queries(UQ - 1, 0)
            with pe.Fori(0, N_ROUNDS) as i:
                r = pe.snap(i & (ROUNDS - 1))
                nxt = pe.snap((i + 1) & (ROUNDS - 1))
                loads = pe.snap((((i + 1) >> 2) + 1) * 16)
                heads = pe.snap(i * BODY)
                unit = pe.snap(i * UQ + UQ)
                heads2 = pe.snap(i * (2 * BODY))
                heads4 = pe.snap(i * (4 * BODY))
                pairs = pe.snap(i * (BODY // 2))
                rounds16 = pe.snap(i * 16)
                for k in range(BODY):
                    scores(k, heads4, unit, rounds16)
                    if k >= 1:
                        turn_probs(k - 1, heads, heads2)
                    project(k, unit, nxt, loads if k == 0 else None)
                    if k >= 4:
                        turn_queries(k - 4, unit)
                    if k in (5, 6):
                        project_out(0, k - 5, r, pairs)
                    if k >= 1:
                        apply(k - 1, heads, heads2, pairs, rounds16)
                k = BODY
                turn_probs(k - 1, heads, heads2)
                turn_queries(4, unit)
                turn_queries(5, unit)
                apply(k - 1, heads, heads2, pairs, rounds16)
                turn_queries(6, unit)
                project_out(1, 0, r, pairs)
                turn_queries(7, unit)
                project_out(1, 1, r, pairs)

        @block.scalar
        def _(act):
            act.sem_inc(t_act, 1)

            def copy_nope(u, unit):
                if latent:
                    act.wait_ge(rope_read, unit + (u + 1))
                    wait_q_tok(act, u, unit)
                    nc.scalar.activation(q_tok[u % Q_RING][:, :, 0:64], ps_q[:].rearrange("p (h n) -> p h n", h=4)[:, :, 0:64],
                                         ACT.Copy).then_inc(nope_done, 1)

            def queries_hi(u, unit):
                act.wait_ge(q_turned, unit + (u + 1))
                h = 4 * (u // 4)
                nc.scalar.activation(qt_hi[:, h:h + 4, P * (u % 4):P * (u % 4) + P], ps_qt[:].rearrange("p (h n) -> p h n", h=4),
                                     ACT.Copy).then_inc(q_hi_done, 1)

            def exps(k, tiles_done):
                for n, q in enumerate((3, 0, 2, 1)):
                    act.wait_ge(masked, tiles_done + (4 * k + n + 1 + 4))
                    pr = probs[k % 2][:, P_OFF[q]:P_OFF[q] + P * (q + 1)]
                    last = nc.scalar.activation(pr, pr, ACT.Exp, scale=-1.0, bias=neg_max[k % 2][:, q:q + 1],
                                                accum_out=total[k % 2][:, q:q + 1])
                last.then_inc(exped, 1)

            def copy_turned(k, heads3):
                for n in (0, 2):
                    act.wait_ge(turned, heads3 + (3 * k + n + 1))
                    j = TRANS_UNITS[n][0][0]
                    m = S - P * j
                    nc.scalar.activation(probs_t[k % 2][:, PT_OFF[j]:PT_OFF[j] + m], ps_t[(3 * k + n) % 2][:, 0:m], ACT.Copy)\
                        .then_inc(t_act, 1)

            def values_hi(m, heads, pairs):
                act.wait_ge(valued, heads + (2 * m + 2))
                act.wait_ge(out_done, pairs + (m // 2 * 2 + 2))
                nc.scalar.activation(ot_hi[m % 2][:], ps_v[:], ACT.Copy).then_inc(o_hi_done, 1)

            for u in range(UQ):
                copy_nope(u, 0)
                if u:
                    queries_hi(u - 1, 0)
            queries_hi(UQ - 1, 0)
            with act.Fori(0, N_ROUNDS) as i:
                heads = act.snap(i * BODY)
                unit = act.snap(i * UQ + UQ)
                heads3 = act.snap(i * (3 * BODY))
                tiles_done = act.snap(i * (4 * BODY))
                pairs = act.snap(i * (BODY // 2))
                for k in range(BODY):
                    exps(k, tiles_done)
                    if k >= 1:
                        copy_turned(k - 1, heads3)
                    copy_nope(k, unit)
                    if k >= 4:
                        queries_hi(k - 4, unit)
                    if k >= 2 and k % 2 == 0:
                        values_hi(k // 2 - 1, heads, pairs)
                copy_turned(BODY - 1, heads3)
                queries_hi(4, unit)
                queries_hi(5, unit)
                values_hi(3, heads, pairs)
                queries_hi(6, unit)
                queries_hi(7, unit)

        @block.vector
        def _(dve):
            dve.sem_inc(masked, 4)
            dve.sem_inc(t_dve, 1)
            dve.sem_inc(o_lo_done, 1)
            dve.sem_inc(added, 1)
            dve.sem_inc(q_lo_done, 1)
            dve.sem_inc(out_done, 2)
            dve.sem_inc(q_bank_read, 1)
            dve.wait_ge(rope_loaded, 32)

            def rotate(u, unit):
                dve.wait_ge(q_done, unit + (u + 1))
                dve.wait_ge(rope_added, unit + (u + 1))
                x = ps_q[:, 0:4 * a.width].rearrange("p (h n) -> p h n", h=4)[:, :, a.width - DR:a.width]
                j = u % 4
                nc.vector.tensor_tensor(rot_a[u % 2][:], x, rope[:, 0, j:j + 1, :].to_broadcast([P, 4, DR]), ALU.mult)
                swapped = x.rearrange("p h (t c) -> p h t c", t=2)[:, :, ::-1, :]
                sines = rope[:, 1, j:j + 1, :].rearrange("p o (t c) -> p o t c", t=2).to_broadcast([P, 4, 2, HALF])
                nc.vector.tensor_tensor(rot_b[u % 2][:].rearrange("p h (t c) -> p h t c", t=2), swapped, sines, ALU.mult)\
                    .then_inc(rope_read, 1)

            def queries_lo(u, unit):
                dve.wait_ge(q_hi_done, unit + (u + 1))
                h = 4 * (u // 4)
                cols = slice(P * (u % 4), P * (u % 4) + P)
                nc.vector.tensor_tensor(qt_lo[:, h:h + 4, cols], ps_qt[:].rearrange("p (h n) -> p h n", h=4),
                                        qt_hi[:, h:h + 4, cols].bitcast(F32), ALU.subtract).then_inc(q_lo_done, 1)

            def mask_and_max(k, heads3, free):
                if free is not None:
                    dve.wait_ge(turned, free)
                for n, tiles in enumerate(SCORE_UNITS):
                    wait_alone(dve, scored, heads3 + (3 * k + n + 1), passed)
                    for q, col in tiles:
                        nk = P * (q + 1)
                        last = nc.vector.tensor_tensor_reduce(
                            out=probs[k % 2][:, P_OFF[q]:P_OFF[q] + nk], in0=ps_s[(3 * k + n) % 2][:, col:col + nk],
                            in1=mask[:, 512 - nk:512], scale=-a.scale, scalar=BIG, op0=ALU.add, op1=ALU.min,
                            accum_out=neg_max[k % 2][:, q:q + 1])
                        last.then_inc(masked, 1)

            def invert(k, heads):
                dve.wait_ge(exped, heads + (k + 1))
                nc.vector.reciprocal(inverse[k % 2][:], total[k % 2][:]).then_inc(inverted, 1)

            def copy_turned(k, heads3):
                dve.wait_ge(turned, heads3 + (3 * k + 2))
                o = probs_t[k % 2][:, PT_OFF[1]:PT_OFF[1] + 384]
                nc.vector.tensor_copy(o, ps_t[(3 * k + 1) % 2][:, 0:384])
                nc.vector.tensor_copy(probs_t[k % 2][:, PT_OFF[3]:PT_OFF[3] + P], ps_t[(3 * k + 1) % 2][:, 384:512]).then_inc(t_dve, 1)

            def values_lo(m, pairs):
                dve.wait_ge(o_hi_done, pairs + (m + 1))
                nc.vector.tensor_tensor(ot_lo[m % 2][:], ps_v[:], ot_hi[m % 2][:].bitcast(F32), ALU.subtract).then_inc(o_lo_done, 1)

            def add_out(c, half, b, pairs):
                dve.wait_ge(out_done, pairs + (2 * c + half + 1 + 2))
                xb = x_res[:].rearrange("p (b g t) d -> p b g (t d)", b=B, g=2)[:, b, half, :]
                nc.vector.tensor_tensor(xb, ps_o[:], xb, ALU.add).then_inc(added, 1)

            for u in range(UQ):
                rotate(u, 0)
                if u:
                    queries_lo(u - 1, 0)
            queries_lo(UQ - 1, 0)
            with dve.Fori(0, N_ROUNDS) as i:
                b = dve.snap((i >> 2) & (B - 1))
                heads = dve.snap(i * BODY)
                unit = dve.snap(i * UQ + UQ)
                heads3 = dve.snap(i * (3 * BODY))
                pairs = dve.snap(i * (BODY // 2))
                for k in range(BODY):
                    mask_and_max(k, heads3, heads3 + 3 * (k - 1) if k >= 2 else None)
                    if k >= 1:
                        copy_turned(k - 1, heads3)
                    rotate(k, unit)
                    invert(k, heads)
                    if k >= 4:
                        queries_lo(k - 4, unit)
                    if k in (5, 6):
                        add_out(0, k - 5, b, pairs)
                    if k >= 2 and k % 2 == 0:
                        values_lo(k // 2 - 1, pairs)
                copy_turned(BODY - 1, heads3)
                queries_lo(4, unit)
                queries_lo(5, unit)
                values_lo(3, pairs)
                queries_lo(6, unit)
                add_out(1, 0, b, pairs)
                queries_lo(7, unit)
                add_out(1, 1, b, pairs)


def split_ffn_weights(nc, sems, hbm, w, wkv):
    with ExitStack() as ctx:
        raw = [ctx.enter_context(nc.sbuf_tensor(f"fw_raw{u}", [P, 2048], F32)) for u in range(3)]
        loaded = [sems(f"raw_loaded{u}") for u in range(3)]
        hi_done, lo_done = sems("hi_done"), sems("lo_done")
        wq = hbm["L0_ffn_wq"].rearrange("(k p) n -> k p n", p=P)
        wk = hbm["L0_ffn_wk"].rearrange("(k p) n -> k p n", p=P)
        wv = hbm["L0_ffn_wv"].rearrange("(k p) n -> k p n", p=P)
        wo = hbm["L0_ffn_wo"].rearrange("(m p) n -> p m n", p=P)
        jobs = [([(wk[k], 0, 512), (wv[k], 512, 1024)], wkv[0][:, k, :], wkv[1][:, k, :]) for k in range(KT)]
        jobs += [([(wq[k], 0, 2048)], w["wq_hi"][:, k, :], w["wq_lo"][:, k, :]) for k in range(KT)]
        for k in range(2):
            jobs.append(([(wo[:, 8 * k:8 * k + 8, :], 0, 2048)],
                         *(w[n][:].rearrange("p (k m) n -> p k (m n)", k=2)[:, k] for n in ("wo_hi", "wo_lo"))))
        block = ctx.enter_context(nc.Block())

        @block.sync
        def _(sp):
            for n, (parts, _, _) in enumerate(jobs):
                if n >= 3:
                    sp.wait_ge(lo_done, n - 2)
                for src, c0, c1 in parts:
                    dst = raw[n % 3][:, c0:c1]
                    if len(src.shape) == 3:
                        dst = dst.rearrange("p (m n) -> p m n", n=D)
                    sp.dma_start(dst, src).then_inc(loaded[n % 3], 16)

        @block.scalar
        def _(act):
            seen = [0, 0, 0]
            for n, (parts, hi, _) in enumerate(jobs):
                seen[n % 3] += 16 * len(parts)
                act.wait_ge(loaded[n % 3], seen[n % 3])
                nc.scalar.activation(hi, raw[n % 3][:, 0:parts[-1][2]], ACT.Copy).then_inc(hi_done, 1)

        @block.vector
        def _(dve):
            for n, (parts, hi, lo) in enumerate(jobs):
                dve.wait_ge(hi_done, n + 1)
                nc.vector.tensor_tensor(lo, raw[n % 3][:, 0:parts[-1][2]], hi.bitcast(F32), ALU.subtract).then_inc(lo_done, 1)


def ffn_inputs(nc, sems, hbm, x_res, ident, exponent, wkv, scratch):
    with ExitStack() as ctx:
        def sb(name, shape, dt=F32):
            return ctx.enter_context(nc.sbuf_tensor("fi_" + name, shape, dt))

        U = 2
        ROUNDS_IN = TILES // U
        ln_w = sb("ln_w", [P, D])
        rope = sb("rope", [P, 2, NT, DR])
        stats, mv = sb("stats", [P, U, 6]), sb("mv", [P, U, 2])
        var_eps, rstd = sb("var_eps", [P, U]), sb("rstd", [P, U])
        square, ms, ms_eps, rms = sb("square", [P, U, D]), sb("ms", [P, U]), sb("ms_eps", [P, U]), sb("rms", [P, U])
        h = sb("h", [P, U, D])
        ht_hi, ht_lo = sb("ht_hi", [P, U, KT, P], F32R), sb("ht_lo", [P, U, KT, P], F32R)
        rot_a, rot_b = sb("rot_a", [P, U, KVH, DR]), sb("rot_b", [P, U, KVH, DR])
        k_tok, v_tok = sb("k_tok", [P, U, KVH, 2, HD]), sb("v_tok", [P, U, KVH, HD])
        k_stack = sb("k_stack", [P, U, KVH, P], F32R)
        ps_t = [ctx.enter_context(nc.psum_tensor(f"fi_ps_t{u}", [P, 512], F32)) for u in range(U)]
        ps_k = [ctx.enter_context(nc.psum_tensor(f"fi_ps_k{u}", [P, 512], F32)) for u in range(U)]
        ps_v = [ctx.enter_context(nc.psum_tensor(f"fi_ps_v{u}", [P, 512], F32)) for u in range(U)]
        ps_kt = [ctx.enter_context(nc.psum_tensor(f"fi_ps_kt{g}", [P, 512], F32)) for g in range(2)]

        loaded, x_saved, bn, mean_var, eps_added, rstd_done = (
            sems(n) for n in ("loaded", "x_saved", "bn", "mean_var", "eps_added", "rstd_done"))
        xi_done, squared, ms_eps_added, rms_done, h_done = (
            sems(n) for n in ("xi_done", "squared", "ms_eps_added", "rms_done", "h_done"))
        turned, hi_done, lo_done, projected, rotated, added = (
            sems(n) for n in ("turned", "hi_done", "lo_done", "projected", "rotated", "added"))
        v_done, k_turned, k_hi_done, k_lo_done, stored, passed = (
            sems(n) for n in ("v_done", "k_turned", "k_hi_done", "k_lo_done", "stored", "passed"))
        block = ctx.enter_context(nc.Block())
        N_STORES = 4 * U

        @block.sync
        def _(sp):
            sp.dma_start(scratch["x1"], x_res[:]).then_inc(x_saved, 16)
            sp.dma_start(ln_w[:], hbm["L0_ffn_ln_w"].rearrange("(o n) -> o n", o=1).to_broadcast([P, D])).then_inc(loaded, 16)
            for k in range(2):
                sp.dma_start(rope[:, k], hbm["rope_ffn"][k].rearrange("(j p) n -> p j n", p=P)).then_inc(loaded, 16)
            with sp.Fori(0, B) as b:
                with sp.Fori(0, NT // U) as x:
                    done = sp.snap(b * NT + x * U)
                    for u in range(U):
                        qs = scratch["q_src"][b].rearrange("p k (x u n) -> p k x u n", x=2, u=2)[:, :, x, u, :]
                        kk = scratch["k"][b].rearrange("g p (x u n) -> p g x u n", x=2, u=2)[:, :, x, u, :]
                        vv = scratch["v"][b].rearrange("g p (x u) n -> p g x u n", x=2)[:, :, x, u, :]
                        sp.wait_ge(lo_done, done + (u + 1))
                        sp.dma_start(qs[:, 0:2], ht_hi[:, u].bitcast(F32)).then_inc(stored, 16)
                        sp.dma_start(qs[:, 2:4], ht_lo[:, u].bitcast(F32)).then_inc(stored, 16)
                        sp.wait_ge(v_done, done + (u + 1))
                        sp.dma_start(vv, v_tok[:, u]).then_inc(stored, 16)
                        sp.wait_ge(k_lo_done, done * 2 + (2 * (u + 1) + 2))
                        sp.dma_start(kk, k_stack[:, u].bitcast(F32)).then_inc(stored, 16)
            sp.wait_ge(stored, 16 * N_STORES * (ROUNDS_IN + 1))

        @block.gpsimd
        def _(pool):
            pool.sem_inc(stored, 16 * N_STORES)
            with pool.Fori(0, ROUNDS_IN) as i:
                base = pool.snap(i * U)
                for u in range(U):
                    wait_alone(pool, mean_var, base + (u + 1), passed)
                    nc.gpsimd.tensor_scalar(var_eps[:, u:u + 1], mv[:, u, 1:2], LN_EPS, 1.0, ALU.add, ALU.mult).then_inc(eps_added, 1)
                    pool.wait_ge(eps_added, base + (u + 1))
                    nc.gpsimd.tensor_tensor(rstd[:, u:u + 1], var_eps[:, u:u + 1], exponent[:], ALU.pow).then_inc(rstd_done, 1)
                for u in range(U):
                    wait_alone(pool, squared, base + (u + 1), passed)
                    nc.gpsimd.tensor_scalar(ms_eps[:, u:u + 1], ms[:, u:u + 1], FFN_EPS, 1.0, ALU.add, ALU.mult).then_inc(ms_eps_added, 1)
                    pool.wait_ge(ms_eps_added, base + (u + 1))
                    nc.gpsimd.tensor_tensor(rms[:, u:u + 1], ms_eps[:, u:u + 1], exponent[:], ALU.pow).then_inc(rms_done, 1)
                for u in range(U):
                    pool.wait_ge(rotated, base + (u + 1))

                    def twice(t):
                        return t[:, u].rearrange("p g (o n) -> p g o n", o=1).to_broadcast([P, KVH, 2, HD])
                    nc.gpsimd.tensor_tensor(k_tok[:, u], twice(rot_a), twice(rot_b), ALU.add).then_inc(added, 1)

        @block.tensor
        def _(pe):
            with pe.Fori(0, ROUNDS_IN) as i:
                base = pe.snap(i * U)
                halves = pe.snap(i * (2 * U))
                for u in range(U):
                    pe.wait_ge(h_done, base + (u + 1))
                    for k in range(KT):
                        last = nc.tensor.transpose(ps_t[u][:, P * k:P * k + P], h[:, u, P * k:P * k + P], ident[:])
                    last.then_inc(turned, 1)
                for u in range(U):
                    pe.wait_ge(lo_done, base + (u + 1))
                    for ps, c0 in ((ps_k[u], 0), (ps_v[u], 512)):
                        n = 0
                        for k in range(KT):
                            for x, wt in ((ht_hi, 0), (ht_hi, 1), (ht_lo, 0)):
                                last = nc.tensor.matmul(ps[:], x[:, u, k, :], wkv[wt][:, k, c0:c0 + 512], start=(n == 0), stop=(n == 5))
                                n += 1
                    last.then_inc(projected, 1)
                for u in range(U):
                    pe.wait_ge(added, base + (u + 1))
                    for g in range(2):
                        pe.wait_ge(k_lo_done, halves + (2 * u + g + 1))
                        for n in range(4):
                            last = nc.tensor.transpose(ps_kt[g][:, P * n:P * n + P],
                                                       k_tok[:, u, 4 * g + n].rearrange("p o n -> p (o n)"), ident[:])
                        last.then_inc(k_turned, 1)

        @block.scalar
        def _(act):
            with act.Fori(0, ROUNDS_IN) as i:
                base = act.snap(i * U)
                halves = act.snap(i * (2 * U))
                stores = act.snap(i * (16 * N_STORES))
                xr = x_res[:].rearrange("p (i u) d -> p i u d", u=U)
                for u in range(U):
                    act.wait_ge(xi_done, base + (u + 1))
                    nc.scalar.activation(square[:, u, :], xr[:, i, u, :], ACT.Square, scale=float(D) ** -0.5,
                                         accum_out=ms[:, u:u + 1]).then_inc(squared, 1)
                act.wait_ge(stored, stores + 16 * N_STORES)
                for u in range(U):
                    act.wait_ge(turned, base + (u + 1))
                    nc.scalar.activation(ht_hi[:, u].rearrange("p k n -> p (k n)"), ps_t[u][:, 0:D], ACT.Copy).then_inc(hi_done, 1)
                for u in range(U):
                    act.wait_ge(projected, base + (u + 1))
                    nc.scalar.activation(v_tok[:, u].rearrange("p g n -> p (g n)"), ps_v[u][:], ACT.Copy).then_inc(v_done, 1)
                for u in range(U):
                    for g in range(2):
                        act.wait_ge(k_turned, halves + (2 * u + g + 1))
                        nc.scalar.activation(k_stack[:, u, 4 * g:4 * g + 4].rearrange("p g n -> p (g n)"), ps_kt[g][:], ACT.Copy)\
                            .then_inc(k_hi_done, 1)

        @block.vector
        def _(dve):
            dve.sem_inc(k_lo_done, 2)
            dve.wait_ge(loaded, 48)
            dve.wait_ge(x_saved, 16)
            with dve.Fori(0, ROUNDS_IN) as i:
                base = dve.snap(i * U)
                halves = dve.snap(i * (2 * U))
                stores = dve.snap(i * (16 * N_STORES))
                x = dve.snap(i & 1)
                xr = x_res[:].rearrange("p (i u) d -> p i u d", u=U)
                table = rope[:].rearrange("p s (x u) n -> p s x u n", x=2)
                for u in range(U):
                    nc.vector.bn_stats(stats[:, u, :], xr[:, i, u, :]).then_inc(bn, 1)
                for u in range(U):
                    wait_alone(dve, bn, base + (u + 1), passed)
                    nc.vector.bn_aggr(mv[:, u, :], stats[:, u, :]).then_inc(mean_var, 1)
                for u in range(U):
                    dve.wait_ge(rstd_done, base + (u + 1))
                    nc.vector.tensor_scalar(xr[:, i, u, :], xr[:, i, u, :], mv[:, u, 0:1], rstd[:, u:u + 1], ALU.subtract, ALU.mult)\
                        .then_inc(xi_done, 1)
                for u in range(U):
                    dve.wait_ge(rms_done, base + (u + 1))
                    dve.wait_ge(xi_done, base + (u + 1))
                    nc.vector.scalar_tensor_tensor(out=h[:, u, :], in0=xr[:, i, u, :], scalar=rms[:, u:u + 1], in1=ln_w[:],
                                                   op0=ALU.mult, op1=ALU.mult).then_inc(h_done, 1)
                dve.wait_ge(stored, stores + 16 * N_STORES)
                for u in range(U):
                    dve.wait_ge(hi_done, base + (u + 1))
                    nc.vector.tensor_tensor(ht_lo[:, u].rearrange("p k n -> p (k n)"), ps_t[u][:, 0:D],
                                            ht_hi[:, u].bitcast(F32).rearrange("p k n -> p (k n)"), ALU.subtract).then_inc(lo_done, 1)
                for u in range(U):
                    dve.wait_ge(projected, base + (u + 1))
                    k3 = ps_k[u][:].rearrange("p (g n) -> p g n", g=KVH)
                    nc.vector.tensor_tensor(rot_a[:, u], k3, table[:, 0, x, u:u + 1, :].to_broadcast([P, KVH, DR]), ALU.mult)
                    nc.vector.tensor_tensor(rot_b[:, u].rearrange("p g (t c) -> p g t c", t=2),
                                            k3.rearrange("p g (t c) -> p g t c", t=2)[:, :, ::-1, :],
                                            table[:, 1, x, u:u + 1, :].rearrange("p o (t c) -> p o t c", t=2).to_broadcast([P, KVH, 2, HALF]),
                                            ALU.mult).then_inc(rotated, 1)
                for u in range(U):
                    for g in range(2):
                        dve.wait_ge(k_hi_done, halves + (2 * u + g + 1))
                        ks = k_stack[64:P, u, 4 * g:4 * g + 4].rearrange("p g n -> p (g n)")
                        nc.vector.tensor_tensor(ks, ps_kt[g][64:P, :], ks.bitcast(F32), ALU.subtract).then_inc(k_lo_done, 1)


def route(nc, sems, hbm, x_res, ident, exponent, gates, h_t, scratch):
    with ExitStack() as ctx:
        def sb(name, shape, dt=F32):
            return ctx.enter_context(nc.sbuf_tensor("rt_" + name, shape, dt))

        U = NT
        ff_w, wg, numbers = sb("ff_w", [P, D]), sb("wg", [P, KT, E]), sb("numbers", [P, E])
        x1 = sb("x1", [P, TILES, D])
        square, ms, ms_eps, rms = sb("square", [P, U, D]), sb("ms", [P, U]), sb("ms_eps", [P, U]), sb("rms", [P, U])
        h, h_now = sb("h", [P, U, D]), sb("h_now", [P, U, D])
        logits, top, index = sb("logits", [P, U, E]), sb("top", [P, U, 8]), sb("index", [P, U, 8], U32)
        index_f, neg, e4, esum, einv, g4 = (sb(n, s) for n, s in (
            ("index_f", [P, U, TOPK]), ("neg", [P, U]), ("e4", [P, U, TOPK]), ("esum", [P, U]), ("einv", [P, U]), ("g4", [P, U, TOPK])))
        hot = sb("hot", [P, U, E, TOPK])
        ps_t = [ctx.enter_context(nc.psum_tensor(f"rt_ps_t{u}", [P, 512], F32)) for u in range(U)]
        ps_l = [ctx.enter_context(nc.psum_tensor(f"rt_ps_l{u}", [P, 512], F32)) for u in range(U)]
        names = ("loaded", "squared", "ms_eps_added", "rms_done", "h_done", "turned", "copied", "copied_all", "routed",
                 "logits_out", "top_done", "index_done", "index_cast", "neg_done", "exped", "inverted", "g4_done", "hot_done",
                 "numbered", "gated", "passed")
        (loaded, squared, ms_eps_added, rms_done, h_done, turned, copied, copied_all, routed, logits_out, top_done,
         index_done, index_cast, neg_done, exped, inverted, g4_done, hot_done, numbered, gated, passed) = (sems(n) for n in names)
        block = ctx.enter_context(nc.Block())

        @block.sync
        def _(sp):
            sp.dma_start(ff_w[:], hbm["L0_ffn_ff_ln_w"].rearrange("(o n) -> o n", o=1).to_broadcast([P, D])).then_inc(loaded, 16)
            sp.dma_start(wg[:], hbm["L0_ffn_wg"].rearrange("(k p) n -> p k n", p=P)).then_inc(loaded, 16)
            sp.dma_start(x1[:], scratch["x1"]).then_inc(loaded, 16)
            sp.wait_ge(loaded, 48)

        @block.gpsimd
        def _(pool):
            nc.gpsimd.iota(numbers[:], pattern=[[1, E]], base=0, channel_multiplier=0,
                           allow_small_or_imprecise_dtypes=True).then_inc(numbered, 1)
            with pool.Fori(0, TILES // U) as i:
                base = pool.snap(i * U)
                for u in range(U):
                    wait_alone(pool, squared, base + (u + 1), passed)
                    nc.gpsimd.tensor_scalar(ms_eps[:, u:u + 1], ms[:, u:u + 1], FFN_EPS, 1.0, ALU.add, ALU.mult).then_inc(ms_eps_added, 1)
                    pool.wait_ge(ms_eps_added, base + (u + 1))
                    nc.gpsimd.tensor_tensor(rms[:, u:u + 1], ms_eps[:, u:u + 1], exponent[:], ALU.pow).then_inc(rms_done, 1)

        @block.tensor
        def _(pe):
            pe.wait_ge(loaded, 48)
            with pe.Fori(0, TILES // U) as i:
                base = pe.snap(i * U)
                for u in range(U):
                    pe.wait_ge(h_done, base + (u + 1))
                    for k in range(KT):
                        last = nc.tensor.transpose(ps_t[u][:, P * k:P * k + P], h[:, u, P * k:P * k + P], ident[:])
                    last.then_inc(turned, 1)
                for u in range(U):
                    pe.wait_ge(copied, base + (u + 1))
                    for k in range(KT):
                        last = nc.tensor.matmul(ps_l[u][:, 0:E], h_now[:, u, P * k:P * k + P], wg[:, k, :], start=(k == 0), stop=(k == KT - 1))
                    last.then_inc(routed, 1)

        @block.scalar
        def _(act):
            with act.Fori(0, TILES // U) as i:
                base = act.snap(i * U)
                xr = x_res[:].rearrange("p (i u) d -> p i u d", u=U)
                ht = h_t[:].rearrange("p k (i u n) -> p k i u n", u=U, n=P)
                for u in range(U):
                    nc.scalar.activation(square[:, u, :], xr[:, i, u, :], ACT.Square, scale=float(D) ** -0.5,
                                         accum_out=ms[:, u:u + 1]).then_inc(squared, 1)
                for u in range(U):
                    act.wait_ge(turned, base + (u + 1))
                    nc.scalar.activation(h_now[:, u, :], ps_t[u][:, 0:D], ACT.Copy).then_inc(copied, 1)
                    nc.scalar.activation(ht[:, :, i, u, :], ps_t[u][:, 0:D].rearrange("p (k n) -> p k n", k=KT), ACT.Copy)\
                        .then_inc(copied_all, 1)
                for u in range(U):
                    act.wait_ge(neg_done, base + (u + 1))
                    nc.scalar.activation(e4[:, u, :], top[:, u, 0:TOPK], ACT.Exp, bias=neg[:, u:u + 1],
                                         accum_out=esum[:, u:u + 1]).then_inc(exped, 1)

        @block.vector
        def _(dve):
            dve.wait_ge(loaded, 48)
            dve.wait_ge(numbered, 1)
            with dve.Fori(0, TILES // U) as i:
                base = dve.snap(i * U)
                base4 = dve.snap(i * (U * TOPK))
                xr = x_res[:].rearrange("p (i u) d -> p i u d", u=U)
                x1r = x1[:].rearrange("p (i u) d -> p i u d", u=U)
                gt = gates[:].rearrange("p (i u) e -> p i u e", u=U)
                for u in range(U):
                    dve.wait_ge(rms_done, base + (u + 1))
                    nc.vector.scalar_tensor_tensor(out=h[:, u, :], in0=xr[:, i, u, :], scalar=rms[:, u:u + 1], in1=ff_w[:],
                                                   op0=ALU.mult, op1=ALU.mult).then_inc(h_done, 1)
                for u in range(U):
                    dve.wait_ge(h_done, base + (u + 1))
                    nc.vector.tensor_tensor(xr[:, i, u, :], xr[:, i, u, :], x1r[:, i, u, :], ALU.add)
                for u in range(U):
                    dve.wait_ge(routed, base + (u + 1))
                    nc.vector.tensor_copy(logits[:, u, :], ps_l[u][:, 0:E]).then_inc(logits_out, 1)
                for u in range(U):
                    wait_alone(dve, logits_out, base + (u + 1), passed)
                    nc.vector.max(top[:, u, :], logits[:, u, :]).then_inc(top_done, 1)
                for u in range(U):
                    dve.wait_ge(top_done, base + (u + 1))
                    nc.vector.tensor_scalar(neg[:, u:u + 1], top[:, u, 0:1], -1.0, None, ALU.mult).then_inc(neg_done, 1)
                    nc.vector.max_index(index[:, u, :], top[:, u, :], logits[:, u, :]).then_inc(index_done, 1)
                for u in range(U):
                    dve.wait_ge(index_done, base + (u + 1))
                    nc.vector.tensor_copy(index_f[:, u, :], index[:, u, 0:TOPK]).then_inc(index_cast, 1)
                for u in range(U):
                    dve.wait_ge(exped, base + (u + 1))
                    nc.vector.reciprocal(einv[:, u:u + 1], esum[:, u:u + 1]).then_inc(inverted, 1)
                for u in range(U):
                    dve.wait_ge(inverted, base + (u + 1))
                    nc.vector.tensor_scalar(g4[:, u, :], e4[:, u, :], einv[:, u:u + 1], None, ALU.mult).then_inc(g4_done, 1)
                for u in range(U):
                    dve.wait_ge(g4_done, base + (u + 1))
                    dve.wait_ge(index_cast, base + (u + 1))
                    for k in range(TOPK):
                        nc.vector.tensor_scalar(hot[:, u, :, k], numbers[:], index_f[:, u, k:k + 1], g4[:, u, k:k + 1],
                                                ALU.is_equal, ALU.mult).then_inc(hot_done, 1)
                for u in range(U):
                    dve.wait_ge(hot_done, base4 + TOPK * (u + 1))
                    nc.vector.tensor_reduce(gt[:, i, u, :], hot[:, u], AX_X, ALU.add).then_inc(gated, 1)


def experts_dense(nc, sems, hbm, x_res, ident, gates, h_t, out):
    with ExitStack() as ctx:
        def sb(name, shape, dt=F32):
            return ctx.enter_context(nc.sbuf_tensor("ex_" + name, shape, dt))

        U = 2
        w13 = [sb(f"w13_{u}", [P, KT, 2 * H]) for u in range(U)]
        w2 = [sb(f"w2_{u}", [P, KT, D]) for u in range(U)]
        g_act = [sb(f"g_act{r}", [P, H]) for r in range(2)]
        a = [sb(f"a{r}", [P, H]) for r in range(2)]
        a_t = [sb(f"a_t{r}", [P, H]) for r in range(2)]
        ps_gu, ps_at, ps_y = ([ctx.enter_context(nc.psum_tensor(f"ex_{n}{r}", [P, 512], F32)) for r in range(2)]
                              for n in ("ps_gu", "ps_at", "ps_y"))
        loaded = [sems(f"loaded{u}") for u in range(U)]
        up, silued, mixed, turned, copied, down, added, stored = (
            sems(n) for n in ("up", "silued", "mixed", "turned", "copied", "down", "added", "stored"))
        block = ctx.enter_context(nc.Block())
        N = TILES
        ROUNDS_E = E // U

        @block.sync
        def _(sp):
            with sp.Fori(0, ROUNDS_E) as i:
                done = sp.snap(i * (N * U))
                for u in range(U):
                    sp.wait_ge(down, done + (N * u + 1))
                    for n, name in enumerate(("L0_ffn_w1", "L0_ffn_w3")):
                        src = hbm[name].rearrange("(i u) (k p) h -> i u p k h", u=U, p=P)[i, u]
                        sp.dma_start(w13[u][:, :, H * n:H * n + H], src).then_inc(loaded[u], 16)
                    src = hbm["L0_ffn_w2"].rearrange("(i u) (k p) h -> i u p k h", u=U, p=P)[i, u]
                    sp.dma_start(w2[u][:], src).then_inc(loaded[u], 16)
            sp.wait_ge(added, N * E + 2)
            sp.dma_start(out.rearrange("b (j p) d -> p (b j) d", p=P), x_res[:]).then_inc(stored, 16)
            sp.wait_ge(stored, 16)

        @block.tensor
        def _(pe):
            with pe.Fori(0, ROUNDS_E) as i:
                base = pe.snap(i * (N * U))
                loads = pe.snap(i * 48)

                def gate_up(s):
                    u, t = s // N, s % N
                    if t == 0:
                        pe.wait_ge(loaded[u], loads + 48)
                    pe.wait_ge(mixed, base + (s + 1))
                    for k in range(KT):
                        last = nc.tensor.matmul(ps_gu[s % 2][:], h_t[:, k, P * t:P * t + P], w13[u][:, k, :], start=(k == 0), stop=(k == KT - 1))
                    last.then_inc(up, 1)

                def turn(s):
                    pe.wait_ge(mixed, base + (s + 1 + 2))
                    pe.wait_ge(copied, base + (s + 1))
                    for k in range(KT):
                        last = nc.tensor.transpose(ps_at[s % 2][:, P * k:P * k + P], a[s % 2][:, P * k:P * k + P], ident[:])
                    last.then_inc(turned, 1)

                def project(s):
                    pe.wait_ge(copied, base + (s + 1 + 2))
                    pe.wait_ge(added, base + (s + 1))
                    for k in range(KT):
                        last = nc.tensor.matmul(ps_y[s % 2][:, 0:D], a_t[s % 2][:, P * k:P * k + P], w2[s // N][:, k, :],
                                                start=(k == 0), stop=(k == KT - 1))
                    last.then_inc(down, 1)

                for s in range(N * U + 2):
                    if s < N * U:
                        gate_up(s)
                    if 1 <= s <= N * U:
                        turn(s - 1)
                    if s >= 2:
                        project(s - 2)

        @block.scalar
        def _(act):
            with act.Fori(0, ROUNDS_E) as i:
                base = act.snap(i * (N * U))
                for s in range(N * U + 1):
                    if s < N * U:
                        act.wait_ge(up, base + (s + 1))
                        nc.scalar.activation(g_act[s % 2][:], ps_gu[s % 2][:, 0:H], ACT.Silu).then_inc(silued, 1)
                    if s >= 1:
                        act.wait_ge(turned, base + s)
                        nc.scalar.activation(a_t[(s - 1) % 2][:], ps_at[(s - 1) % 2][:, 0:H], ACT.Copy).then_inc(copied, 1)

        @block.vector
        def _(dve):
            dve.sem_inc(mixed, 2)
            dve.sem_inc(copied, 2)
            dve.sem_inc(added, 2)
            dve.sem_inc(down, N + 1)
            with dve.Fori(0, ROUNDS_E) as i:
                base = dve.snap(i * (N * U))
                for s in range(N * U + 2):
                    if s < N * U:
                        dve.wait_ge(silued, base + (s + 1))
                        nc.vector.tensor_tensor(a[s % 2][:], ps_gu[s % 2][:, H:2 * H], g_act[s % 2][:], ALU.mult).then_inc(mixed, 1)
                    if s >= 2:
                        u, t = (s - 2) // N, (s - 2) % N
                        dve.wait_ge(down, base + (s - 1 + N + 1))
                        gt = gates[:].rearrange("p t (i u) -> p t i u", u=U)[:, t, i, u:u + 1]
                        nc.vector.scalar_tensor_tensor(out=x_res[:, t, :], in0=ps_y[s % 2][:, 0:D], scalar=gt, in1=x_res[:, t, :],
                                                       op0=ALU.mult, op1=ALU.add).then_inc(added, 1)


def build(nc, hbm, out, upto=9):
    with ExitStack() as ctx:
        def sb(name, shape, dt=F32, c=ctx):
            return c.enter_context(nc.sbuf_tensor(name, shape, dt))

        def dram(name, shape):
            return nc.dram_tensor("scratch_" + name, shape, F32, kind="Internal").ap()

        x_res = sb("x_res", [P, TILES, D])
        ident, mask, exponent = sb("ident", [P, P]), sb("mask", [P, S]), sb("exponent", [P, 1])
        start_constants(nc, Sems(nc, ctx, "sc"), hbm, x_res, ident, mask, exponent)

        with ExitStack() as layer:
            w = {n: sb(n, [P, NH * P], F32R, layer) for n in ("w1hi", "w1lo", "w2hi", "w2lo")}
            w |= {n: sb(n, [P, NH // 2, D], F32R, layer) for n in ("vohi", "volo")}
            latent_scratch = {"q_src": dram("lq", [B, P, 3, S]), "k": dram("lk", [B, P, 2, S]), "v": dram("lv", [B, P, NT, KVLR])}
            prepare_latent_weights(nc, Sems(nc, ctx, "lw"), hbm, w, ident)
            latent_inputs(nc, Sems(nc, ctx, "li"), hbm, x_res, ident, exponent, latent_scratch)
            q_passes = [(0, w["w1hi"][:]), (0, w["w1lo"][:]), (1, w["w1hi"][:]), (2, w["w2hi"][:]), (2, w["w2lo"][:])]
            latent = Attention("la", float(DN + DR) ** -0.5, 3, P, q_passes, 2, [(0, 0), (0, 1), (1, 0)],
                               w["vohi"], w["volo"], latent_scratch, hbm["rope_latent"])
            attention(nc, Sems(nc, ctx, "la"), latent, x_res, ident, mask)
        if upto >= 2:
            with ExitStack() as layer:
                w = {n: sb(n, [P, KT, NH * HD], F32R, layer) for n in ("wq_hi", "wq_lo")}
                w |= {n: sb(n, [P, NH // 2, D], F32R, layer) for n in ("wo_hi", "wo_lo")}
                ffn_scratch = {"q_src": dram("fq", [B, P, 4, S]), "k": dram("fk", [B, KVH, P, S]),
                               "v": dram("fv", [B, KVH, P, NT, HD]), "x1": dram("x1", [P, TILES, D])}
                with ExitStack() as part:
                    wkv = [sb(n, [P, KT, 2 * KVH * HD], F32R, part) for n in ("wkv_hi", "wkv_lo")]
                    split_ffn_weights(nc, Sems(nc, ctx, "fw"), hbm, w, wkv)
                    ffn_inputs(nc, Sems(nc, ctx, "fi"), hbm, x_res, ident, exponent, wkv, ffn_scratch)
                q_passes = [p for k in range(KT) for p in ((k, w["wq_hi"][:, k, :]), (k, w["wq_lo"][:, k, :]), (2 + k, w["wq_hi"][:, k, :]))]
                views = dict(ffn_scratch, k=ffn_scratch["k"].rearrange("b (r c) p (o s) -> b r c p o s", r=ROUNDS, o=1),
                             v=ffn_scratch["v"].rearrange("b (r c) p j n -> b r c p j n", r=ROUNDS))
                grouped = Attention("ga", float(HD) ** -0.5, 4, HD, q_passes, 1, [(0, 0), (1, 0)],
                                    w["wo_hi"], w["wo_lo"], views, hbm["rope_ffn"])
                attention(nc, Sems(nc, ctx, "ga"), grouped, x_res, ident, mask)
        if upto >= 3:
            h_t, gates = sb("h_t", [P, KT, B * S]), sb("gates", [P, TILES, E])
            route(nc, Sems(nc, ctx, "rt"), hbm, x_res, ident, exponent, gates, h_t, ffn_scratch)
            experts_dense(nc, Sems(nc, ctx, "ex"), hbm, x_res, ident, gates, h_t, out)
        else:
            stored = ctx.enter_context(nc.semaphore("stored"))
            block = ctx.enter_context(nc.Block())

            @block.sync
            def _(sp):
                sp.dma_start(out.rearrange("b (j p) d -> p (b j) d", p=P), x_res[:]).then_inc(stored, 16)
                sp.wait_ge(stored, 16)


_INS = ["L0_attn_hidden_states", "L0_attn_q_a_w", "L0_attn_q_a_ln_w", "L0_attn_q_b_w", "L0_attn_kv_a_w", "L0_attn_kv_a_ln_w",
        "L0_attn_kv_b_w", "L0_attn_o_w", "L0_ffn_ln_w", "L0_ffn_ff_ln_w", "L0_ffn_wq", "L0_ffn_wk", "L0_ffn_wv", "L0_ffn_wo",
        "L0_ffn_wg", "L0_ffn_w1", "L0_ffn_w3", "L0_ffn_w2"]


def rope_table(base):
    half = np.arange(HALF, dtype=np.float32) / np.float32(HALF)
    angle = np.arange(S, dtype=np.float32)[:, None] * (np.float32(1.0) / np.float32(base) ** half)
    cos, sin = np.cos(angle), np.sin(angle)
    return np.stack([np.concatenate([cos, cos], 1), np.concatenate([-sin, sin], 1)]).astype(np.float32)


def kernel(**inputs):
    import concourse.bacc as bacc
    from concourse.bass_utils import run_bass_kernel_spmd

    nc = bacc.Bacc("TRN2", target_bir_lowering=False, num_devices=1)
    arrays = {n: np.ascontiguousarray(inputs[n]) for n in _INS}
    arrays |= {"rope_latent": rope_table(10000.0), "rope_ffn": rope_table(150000.0)}
    hbm = {n: nc.dram_tensor("in_" + n, a.shape, mybir.dt.from_np(a.dtype), kind="ExternalInput").ap() for n, a in arrays.items()}
    out = nc.dram_tensor("out_x", (B, S, D), F32, kind="ExternalOutput").ap()
    build(nc, hbm, out)
    r = run_bass_kernel_spmd(nc, [{"in_" + n: a for n, a in arrays.items()}], core_ids=[0])
    return r.results[0]["out_x"]
```

```python
from contextlib import ExitStack

import numpy as np

import concourse.bass as bass
from concourse import mybir

F32 = mybir.dt.float32
F32R = mybir.dt.float32r
U32 = mybir.dt.uint32
ALU = mybir.AluOpType
ACT = mybir.ActivationFunctionType
AX_X = mybir.AxisListType.X

P = 128
B, S, D = 4, 512, 256
NT = S // P
TILES = B * NT
KT = D // P
NH = 32
QLR, KVLR, DR, DN, DV = 192, 64, 64, 128, 128
HD, KVH = 64, 8
E, TOPK, H = 16, 4, 256
HALF = 32
BODY = 8
Q_RING = 2
ROUNDS = NH // BODY
N_ROUNDS = B * ROUNDS
MASKED = -1.0e30
BIG = 3.0e38
LN_EPS, MLA_EPS, FFN_EPS = 1e-5, 1e-6, 1e-5

P_OFF = [0, 128, 384, 768]
P_ALL = 1280
SCORE_UNITS = [[(3, 0)], [(0, 0), (2, 128)], [(1, 0)]]
PT_OFF = [0, 512, 896, 1152]
TRANS_UNITS = [[(0, 0)], [(1, 0), (3, 384)], [(2, 0)]]


def wait_alone(eng, sem, value, passed):
    eng.wait_ge(sem, value)
    eng.sem_inc(passed, 1)


class Sems:

    def __init__(self, nc, ctx, prefix):
        self.nc, self.ctx, self.prefix = nc, ctx, prefix

    def __call__(self, name):
        return self.ctx.enter_context(self.nc.semaphore(f"{self.prefix}_{name}"))


def prepare_latent_weights(nc, sems, hbm, w, ident):
    with ExitStack() as ctx:
        def sb(name, shape, dt=F32):
            return ctx.enter_context(nc.sbuf_tensor("lw_" + name, shape, dt))

        def psum(name):
            return ctx.enter_context(nc.psum_tensor("lw_" + name, [P, 512], F32))

        raw_q1 = [sb(f"raw_q1{u}", [P, 2, DN + DR]) for u in range(2)]
        raw_q2 = [sb(f"raw_q2{u}", [P, 2, DN + DR]) for u in range(2)]
        raw_kv = [sb(f"raw_kv{u}", [KVLR, 2, DN + DV]) for u in range(2)]
        raw_o = [sb(f"raw_o{u}", [P, 2, D]) for u in range(2)]
        q_t = [sb(f"q_t{u}", [P, 2, 2, P]) for u in range(2)]
        kv_t = [sb(f"kv_t{u}", [P, 2, 2, KVLR]) for u in range(2)]
        ps_q = [psum(f"ps_q{u}") for u in range(2)]
        ps_kv = [psum(f"ps_kv{u}") for u in range(2)]
        ps_w = [psum(f"ps_w{u}") for u in range(2)]
        ps_vo = [psum(f"ps_vo{u}") for u in range(2)]

        raw_loaded = [sems(f"raw_loaded{u}") for u in range(2)]
        turned = sems("turned")
        q_turned = sems("q_turned")
        kv_turned = sems("kv_turned")
        multiplied = sems("multiplied")
        hi_done = sems("hi_done")
        lo_done = sems("lo_done")
        PAIRS = NH // 4

        wq_dram = hbm["L0_attn_q_b_w"].rearrange("r (i u h n) -> i u r h n", i=PAIRS, u=2, h=2)
        kvb_dram = hbm["L0_attn_kv_b_w"].rearrange("r (i u h n) -> i u r h n", i=PAIRS, u=2, h=2)
        o_dram = hbm["L0_attn_o_w"].rearrange("(i u h p) n -> i u p h n", i=PAIRS, u=2, h=2)

        def view(t):
            return t[:].rearrange("p (i u h n) -> p i u h n", i=PAIRS, u=2, h=2)

        w1hi, w1lo, w2hi, w2lo = (view(w[n]) for n in ("w1hi", "w1lo", "w2hi", "w2lo"))
        vohi, volo = (w[n][:].rearrange("p (i u) n -> p i u n", u=2) for n in ("vohi", "volo"))
        block = ctx.enter_context(nc.Block())

        @block.sync
        def _(sp):
            with sp.Fori(0, PAIRS) as i:
                done = sp.snap(i * 2)
                for u in range(2):
                    sp.wait_ge(lo_done, done + (u + 1))
                    sp.dma_start(raw_q1[u][:], wq_dram[i, u, 0:P]).then_inc(raw_loaded[u], 16)
                    sp.dma_start(raw_q2[u][0:64], wq_dram[i, u, P:QLR]).then_inc(raw_loaded[u], 16)
                    sp.dma_start(raw_q2[u][64:P], wq_dram[i, u, P:QLR]).then_inc(raw_loaded[u], 16)
                    sp.dma_start(raw_kv[u][:], kvb_dram[i, u]).then_inc(raw_loaded[u], 16)
                    sp.dma_start(raw_o[u][:], o_dram[i, u]).then_inc(raw_loaded[u], 16)

        @block.tensor
        def _(pe):
            with pe.Fori(0, PAIRS) as i:
                base = pe.snap(i * 2)
                loads = pe.snap(i * 80)
                for u in range(2):
                    pe.wait_ge(raw_loaded[u], loads + 80)
                    pe.wait_ge(lo_done, base + (u + 1))
                    for h in range(2):
                        nc.tensor.transpose(ps_q[u][:, 256 * h:256 * h + P], raw_q1[u][:, h, 0:DN], ident[:])
                        nc.tensor.transpose(ps_q[u][:, 256 * h + P:256 * h + 256], raw_q2[u][:, h, 0:DN], ident[:])
                        nc.tensor.transpose(ps_kv[u][:, 128 * h:128 * h + 64], raw_kv[u][:, h, 0:DN], ident[0:64, 0:64])
                        last = nc.tensor.transpose(ps_kv[u][:, 128 * h + 64:128 * h + 128], raw_kv[u][:, h, DN:DN + DV],
                                                   ident[0:64, 0:64])
                    last.then_inc(turned, 1)
                for u in range(2):
                    pe.wait_ge(q_turned, base + (u + 1))
                    pe.wait_ge(kv_turned, base + (u + 1))
                    for h in range(2):
                        for r in range(2):
                            nc.tensor.matmul(ps_w[u][:, 128 * h + 64 * r:128 * h + 64 * r + 64], q_t[u][:, h, r, :],
                                             kv_t[u][:, h, 0, :], start=True, stop=True)
                    for h in range(2):
                        last = nc.tensor.matmul(ps_vo[u][64 * h:64 * h + 64, 0:D], kv_t[u][:, h, 1, :], raw_o[u][:, h, :],
                                                start=True, stop=True)
                    last.then_inc(multiplied, 1)

        @block.scalar
        def _(act):
            with act.Fori(0, PAIRS) as i:
                base = act.snap(i * 2)
                for u in range(2):
                    act.wait_ge(turned, base + (u + 1))
                    nc.scalar.activation(q_t[u][:].rearrange("p h r n -> p (h r n)"), ps_q[u][:], ACT.Copy).then_inc(q_turned, 1)
                for u in range(2):
                    act.wait_ge(multiplied, base + (u + 1))
                    pw = ps_w[u][:, 0:256].rearrange("p (h r c) -> p h r c", h=2, r=2)
                    nc.scalar.activation(w1hi[:, i, u, :, 0:64], pw[:, :, 0, :], ACT.Copy)
                    nc.scalar.activation(w2hi[:, i, u, :, 0:64], pw[:, :, 1, :], ACT.Copy)
                    nc.scalar.activation(w1hi[:, i, u, :, 64:128], raw_q1[u][:, :, DN:DN + DR], ACT.Copy)
                    nc.scalar.activation(w2hi[:, i, u, :, 64:128], raw_q2[u][:, :, DN:DN + DR], ACT.Copy)
                    nc.scalar.activation(vohi[:, i, u, :], ps_vo[u][:, 0:D], ACT.Copy).then_inc(hi_done, 1)

        @block.vector
        def _(dve):
            dve.sem_inc(lo_done, 2)
            with dve.Fori(0, PAIRS) as i:
                base = dve.snap(i * 2)
                for u in range(2):
                    dve.wait_ge(turned, base + (u + 1))
                    nc.vector.tensor_copy(kv_t[u][:].rearrange("p h r n -> p (h r n)"), ps_kv[u][:, 0:256]).then_inc(kv_turned, 1)
                for u in range(2):
                    dve.wait_ge(hi_done, base + (u + 1))
                    pw = ps_w[u][:, 0:256].rearrange("p (h r c) -> p h r c", h=2, r=2)

                    def split(lo, x, hi):
                        return nc.vector.tensor_tensor(lo, x, hi.bitcast(F32), ALU.subtract)

                    split(w1lo[:, i, u, :, 0:64], pw[:, :, 0, :], w1hi[:, i, u, :, 0:64])
                    split(w2lo[:, i, u, :, 0:64], pw[:, :, 1, :], w2hi[:, i, u, :, 0:64])
                    split(w1lo[:, i, u, :, 64:128], raw_q1[u][:, :, DN:DN + DR], w1hi[:, i, u, :, 64:128])
                    split(w2lo[:, i, u, :, 64:128], raw_q2[u][:, :, DN:DN + DR], w2hi[:, i, u, :, 64:128])
                    split(volo[:, i, u, :], ps_vo[u][:, 0:D], vohi[:, i, u, :]).then_inc(lo_done, 1)


def start_constants(nc, sems, hbm, x_res, ident, mask, exponent):
    with ExitStack() as ctx:
        x_loaded, zeroed, made = sems("x_loaded"), sems("zeroed"), sems("made")
        block = ctx.enter_context(nc.Block())

        @block.sync
        def _(sp):
            sp.dma_start(x_res[:], hbm["L0_attn_hidden_states"].rearrange("b (j p) d -> p (b j) d", p=P)).then_inc(x_loaded, 16)
            sp.wait_ge(x_loaded, 16)

        @block.gpsimd
        def _(pool):
            nc.gpsimd.memset(ident[:], 0.0)
            nc.gpsimd.memset(exponent[:], -0.5)
            nc.gpsimd.memset(mask[:], 0.0).then_inc(zeroed, 1)
            pool.wait_ge(zeroed, 1)
            nc.gpsimd.affine_select(out=ident[:], in_=ident[:], compare_op=ALU.not_equal, fill=1.0, base=0,
                                    pattern=[[-1, P]], channel_multiplier=1)
            nc.gpsimd.affine_select(out=mask[:, 384:512], in_=mask[:, 384:512], compare_op=ALU.is_ge, fill=MASKED, base=0,
                                    pattern=[[-1, P]], channel_multiplier=1).then_inc(made, 1)
            pool.wait_ge(made, 1)


def latent_inputs(nc, sems, hbm, x_res, ident, exponent, scratch):
    with ExitStack() as ctx:
        def sb(name, shape, dt=F32):
            return ctx.enter_context(nc.sbuf_tensor("li_" + name, shape, dt))

        W = QLR + KVLR + DR
        wa = sb("wa", [P, KT, W])
        wa_hi, wa_lo = sb("wa_hi", [P, KT, W], F32R), sb("wa_lo", [P, KT, W], F32R)
        ln_w = sb("ln_w", [P, QLR + KVLR])
        rope = sb("rope", [P, 2, NT, DR])
        stats, mv = sb("stats", [P, NT, 6]), sb("mv", [P, NT, 2])
        var_eps, rstd = sb("var_eps", [P, NT]), sb("rstd", [P, NT])
        xn = sb("xn", [P, NT, D])
        xt_hi, xt_lo = sb("xt_hi", [P, NT, D], F32R), sb("xt_lo", [P, NT, D], F32R)
        square = sb("square", [P, NT, QLR + KVLR])
        ms, ms_eps, rms = sb("ms", [P, NT, 2]), sb("ms_eps", [P, NT, 2]), sb("rms", [P, NT, 2])
        qn, kv = sb("qn", [P, NT, 256]), sb("kv", [P, NT, P])
        rot_a, rot_b = sb("rot_a", [P, NT, DR]), sb("rot_b", [P, NT, DR])
        t_hi, t_lo = sb("t_hi", [P, 3, NT, P], F32R), sb("t_lo", [P, 3, NT, P], F32R)
        ps_t = [ctx.enter_context(nc.psum_tensor(f"li_ps_t{u}", [P, 512], F32)) for u in range(NT)]
        ps_p = [ctx.enter_context(nc.psum_tensor(f"li_ps_p{u}", [P, 512], F32)) for u in range(NT)]

        loaded, w_hi, w_lo = sems("loaded"), sems("w_hi"), sems("w_lo")
        bn, mean_var, eps_added, rstd_done, xn_done = (sems(n) for n in ("bn", "mean_var", "eps_added", "rstd_done", "xn_done"))
        xt_turned, xt_hi_done, xt_lo_done, projected = (sems(n) for n in ("xt_turned", "xt_hi_done", "xt_lo_done", "projected"))
        squared, ms_eps_added, rms_done, rotated, normed = (
            sems(n) for n in ("squared", "ms_eps_added", "rms_done", "rotated", "normed"))
        turned, hi_done, lo_done, stored, passed = (sems(n) for n in ("turned", "hi_done", "lo_done", "stored", "passed"))
        block = ctx.enter_context(nc.Block())
        N_LOADS, N_STORES = 6, 7

        @block.sync
        def _(sp):
            sp.dma_start(wa[:, :, 0:QLR], hbm["L0_attn_q_a_w"].rearrange("(k p) n -> p k n", p=P)).then_inc(loaded, 16)
            sp.dma_start(wa[:, :, QLR:W], hbm["L0_attn_kv_a_w"].rearrange("(k p) n -> p k n", p=P)).then_inc(loaded, 16)
            sp.dma_start(ln_w[:, 0:QLR], hbm["L0_attn_q_a_ln_w"].rearrange("(o n) -> o n", o=1).to_broadcast([P, QLR])).then_inc(loaded, 16)
            sp.dma_start(ln_w[:, QLR:], hbm["L0_attn_kv_a_ln_w"].rearrange("(o n) -> o n", o=1).to_broadcast([P, KVLR])).then_inc(loaded, 16)
            for k in range(2):
                sp.dma_start(rope[:, k], hbm["rope_latent"][k].rearrange("(j p) n -> p j n", p=P)).then_inc(loaded, 16)
            with sp.Fori(0, B) as b:
                done = sp.snap(b * NT)
                sp.wait_ge(hi_done, done + NT)
                flat = "p j n -> p (j n)"
                qs, kk = scratch["q_src"][b], scratch["k"][b]
                sp.dma_start(qs[:, 0], t_hi[:, 0].bitcast(F32).rearrange(flat)).then_inc(stored, 16)
                sp.dma_start(qs[0:64, 2], t_hi[0:64, 1].bitcast(F32).rearrange(flat)).then_inc(stored, 16)
                sp.dma_start(kk[:, 0], t_hi[:, 2].bitcast(F32).rearrange(flat)).then_inc(stored, 16)
                sp.wait_ge(lo_done, done + NT)
                sp.dma_start(qs[:, 1], t_lo[:, 0].bitcast(F32).rearrange(flat)).then_inc(stored, 16)
                sp.dma_start(qs[64:P, 2], t_lo[64:P, 1].bitcast(F32).rearrange(flat)).then_inc(stored, 16)
                sp.dma_start(kk[:, 1], t_lo[:, 2].bitcast(F32).rearrange(flat)).then_inc(stored, 16)
                sp.dma_start(scratch["v"][b], kv[:, :, 0:KVLR]).then_inc(stored, 16)
            sp.wait_ge(stored, 16 * N_STORES * (B + 1))

        @block.gpsimd
        def _(pool):
            pool.sem_inc(stored, 16 * N_STORES)
            with pool.Fori(0, B) as b:
                base = pool.snap(b * NT)
                for u in range(NT):
                    wait_alone(pool, mean_var, base + (u + 1), passed)
                    nc.gpsimd.tensor_scalar(var_eps[:, u:u + 1], mv[:, u, 1:2], LN_EPS, 1.0, ALU.add, ALU.mult).then_inc(eps_added, 1)
                    pool.wait_ge(eps_added, base + (u + 1))
                    nc.gpsimd.tensor_tensor(rstd[:, u:u + 1], var_eps[:, u:u + 1], exponent[:], ALU.pow).then_inc(rstd_done, 1)
                for u in range(NT):
                    wait_alone(pool, squared, base + (u + 1), passed)
                    nc.gpsimd.tensor_scalar(ms_eps[:, u, :], ms[:, u, :], MLA_EPS, 1.0, ALU.add, ALU.mult).then_inc(ms_eps_added, 1)
                    pool.wait_ge(ms_eps_added, base + (u + 1))
                    nc.gpsimd.tensor_tensor(rms[:, u, :], ms_eps[:, u, :], exponent[:].to_broadcast([P, 2]), ALU.pow).then_inc(rms_done, 1)

        @block.tensor
        def _(pe):
            pe.wait_ge(w_lo, 1)
            with pe.Fori(0, B) as b:
                base = pe.snap(b * NT)
                for u in range(NT):
                    pe.wait_ge(xn_done, base + (u + 1))
                    for k in range(KT):
                        last = nc.tensor.transpose(ps_t[u][:, P * k:P * k + P], xn[:, u, P * k:P * k + P], ident[:])
                    last.then_inc(xt_turned, 1)
                for u in range(NT):
                    pe.wait_ge(xt_lo_done, base + (u + 1))
                    n = 0
                    for k in range(KT):
                        for x, wt in ((xt_hi, wa_hi), (xt_hi, wa_lo), (xt_lo, wa_hi)):
                            last = nc.tensor.matmul(ps_p[u][:, 0:W], x[:, u, P * k:P * k + P], wt[:, k, :], start=(n == 0), stop=(n == 5))
                            n += 1
                    last.then_inc(projected, 1)
                for u in range(NT):
                    pe.wait_ge(normed, base + (u + 1))
                    nc.tensor.transpose(ps_t[u][:, 0:P], qn[:, u, 0:P], ident[:])
                    nc.tensor.transpose(ps_t[u][:, P:2 * P], qn[:, u, P:2 * P], ident[:])
                    nc.tensor.transpose(ps_t[u][:, 2 * P:3 * P], kv[:, u, :], ident[:]).then_inc(turned, 1)

        @block.scalar
        def _(act):
            act.wait_ge(loaded, 16 * N_LOADS)
            nc.scalar.activation(wa_hi[:], wa[:], ACT.Copy).then_inc(w_hi, 1)
            with act.Fori(0, B) as b:
                base = act.snap(b * NT)
                stores = act.snap(b * (16 * N_STORES))
                for u in range(NT):
                    act.wait_ge(xt_turned, base + (u + 1))
                    nc.scalar.activation(xt_hi[:, u, :], ps_t[u][:, 0:D], ACT.Copy).then_inc(xt_hi_done, 1)
                for u in range(NT):
                    act.wait_ge(projected, base + (u + 1))
                    nc.scalar.activation(square[:, u, 0:QLR], ps_p[u][:, 0:QLR], ACT.Square, scale=float(QLR) ** -0.5,
                                         accum_out=ms[:, u, 0:1])
                    nc.scalar.activation(square[:, u, QLR:], ps_p[u][:, QLR:QLR + KVLR], ACT.Square, scale=float(KVLR) ** -0.5,
                                         accum_out=ms[:, u, 1:2]).then_inc(squared, 1)
                act.wait_ge(stored, stores + 16 * N_STORES)
                for u in range(NT):
                    act.wait_ge(turned, base + (u + 1))
                    nc.scalar.activation(t_hi[:, :, u, :], ps_t[u][:, 0:3 * P].rearrange("p (k n) -> p k n", k=3), ACT.Copy)\
                        .then_inc(hi_done, 1)

        @block.vector
        def _(dve):
            dve.wait_ge(w_hi, 1)
            nc.vector.tensor_tensor(wa_lo[:], wa[:], wa_hi[:].bitcast(F32), ALU.subtract).then_inc(w_lo, 1)
            with dve.Fori(0, B) as b:
                base = dve.snap(b * NT)
                stores = dve.snap(b * (16 * N_STORES))
                xb = x_res[:].rearrange("p (b j) d -> p b j d", b=B)
                for u in range(NT):
                    nc.vector.bn_stats(stats[:, u, :], xb[:, b, u, :]).then_inc(bn, 1)
                for u in range(NT):
                    wait_alone(dve, bn, base + (u + 1), passed)
                    nc.vector.bn_aggr(mv[:, u, :], stats[:, u, :]).then_inc(mean_var, 1)
                for u in range(NT):
                    dve.wait_ge(rstd_done, base + (u + 1))
                    nc.vector.tensor_scalar(xn[:, u, :], xb[:, b, u, :], mv[:, u, 0:1], rstd[:, u:u + 1], ALU.subtract, ALU.mult)\
                        .then_inc(xn_done, 1)
                for u in range(NT):
                    dve.wait_ge(xt_hi_done, base + (u + 1))
                    nc.vector.tensor_tensor(xt_lo[:, u, :], ps_t[u][:, 0:D], xt_hi[:, u, :].bitcast(F32), ALU.subtract)\
                        .then_inc(xt_lo_done, 1)
                dve.wait_ge(stored, stores + 16 * N_STORES)
                for u in range(NT):
                    dve.wait_ge(rms_done, base + (u + 1))
                    q, c, kr = ps_p[u][:, 0:QLR], ps_p[u][:, QLR:QLR + KVLR], ps_p[u][:, QLR + KVLR:W]
                    nc.vector.tensor_tensor(rot_a[:, u, :], kr, rope[:, 0, u, :], ALU.mult)
                    nc.vector.tensor_tensor(rot_b[:, u, :].rearrange("p (t c) -> p t c", t=2),
                                            kr.rearrange("p (t c) -> p t c", t=2)[:, ::-1, :],
                                            rope[:, 1, u, :].rearrange("p (t c) -> p t c", t=2), ALU.mult).then_inc(rotated, 1)
                    nc.vector.scalar_tensor_tensor(out=qn[:, u, 0:P], in0=q[:, 0:P], scalar=rms[:, u, 0:1], in1=ln_w[:, 0:P],
                                                   op0=ALU.mult, op1=ALU.mult)
                    for k in range(2):
                        nc.vector.scalar_tensor_tensor(out=qn[:, u, P + 64 * k:P + 64 * k + 64], in0=q[:, P:QLR],
                                                       scalar=rms[:, u, 0:1], in1=ln_w[:, P:QLR], op0=ALU.mult, op1=ALU.mult)
                    nc.vector.scalar_tensor_tensor(out=kv[:, u, 0:KVLR], in0=c, scalar=rms[:, u, 1:2],
                                                   in1=ln_w[:, QLR:QLR + KVLR], op0=ALU.mult, op1=ALU.mult)
                    dve.wait_ge(rotated, base + (u + 1))
                    nc.vector.tensor_tensor(kv[:, u, KVLR:P], rot_a[:, u, :], rot_b[:, u, :], ALU.add).then_inc(normed, 1)
                for u in range(NT):
                    dve.wait_ge(hi_done, base + (u + 1))
                    nc.vector.tensor_tensor(t_lo[:, :, u, :], ps_t[u][:, 0:3 * P].rearrange("p (k n) -> p k n", k=3),
                                            t_hi[:, :, u, :].bitcast(F32), ALU.subtract).then_inc(lo_done, 1)


class Slot:

    def __init__(self, k, first=False, last=False):
        self.scores = not (last and k >= BODY)
        self.values = not (first and k == BODY) and not (last and k > BODY)
        self.unit = k - 3 if not first and not last else None
        self.turned_unit = k - 4 if not first and not last and k >= 4 else None
        self.last_unit = not first and not last and k == BODY + 2
        self.pair = (k - 3) // 2 if k % 2 and not first else None
        self.out = {6: 0, 10: 1}.get(k) if not first else None


SLOTS = range(3, BODY + 3)
FIRST_SLOTS = range(BODY, BODY + 3)


class Attention:

    def __init__(self, name, scale, q_slots, width, q_passes, k_slots, s_passes, out_hi, out_lo, scratch, rope):
        self.name, self.scale, self.q_slots, self.width = name, scale, q_slots, width
        self.q_passes, self.k_slots, self.s_passes = q_passes, k_slots, s_passes
        self.out_hi, self.out_lo, self.scratch, self.rope = out_hi, out_lo, scratch, rope


def attention(nc, sems, a, x_res, ident, mask):
    latent = a.width == 128
    with ExitStack() as ctx:
        def sb(name, shape, dt=F32):
            return ctx.enter_context(nc.sbuf_tensor(f"{a.name}_{name}", shape, dt))

        def psum(name):
            return ctx.enter_context(nc.psum_tensor(f"{a.name}_{name}", [P, 512], F32))

        q_src = sb("q_src", [P, a.q_slots, S], F32R)
        keys = [sb(f"keys{c}", [P, a.k_slots, S], F32R) for c in range(2)]
        values = [sb(f"values{c}", [P, NT, HD]) for c in range(2)]
        qt_hi, qt_lo = sb("qt_hi", [P, BODY, S], F32R), sb("qt_lo", [P, BODY, S], F32R)
        q_tok = [sb(f"q_tok{r}", [P, 4, P]) for r in range(Q_RING)]
        rot_a = [sb(f"rot_a{r}", [P, 4, DR]) for r in range(2)]
        rot_b = [sb(f"rot_b{r}", [P, 4, DR]) for r in range(2)]
        rope = sb("rope", [P, 2, NT, DR])
        probs = [sb(f"probs{r}", [P, P_ALL]) for r in range(2)]
        probs_t = [sb(f"probs_t{r}", [P, P_ALL]) for r in range(2)]
        neg_max = [sb(f"neg_max{r}", [P, NT]) for r in range(2)]
        total = [sb(f"total{r}", [P, NT]) for r in range(2)]
        inverse = [sb(f"inverse{r}", [P, NT]) for r in range(2)]
        ot_hi = [sb(f"ot_hi{r}", [P, S], F32R) for r in range(2)]
        ot_lo = [sb(f"ot_lo{r}", [P, S], F32R) for r in range(2)]
        ps_s = [psum(f"ps_s{r}") for r in range(2)]
        ps_t = [psum(f"ps_t{r}") for r in range(2)]
        ps_v, ps_q, ps_qt, ps_o = psum("ps_v"), psum("ps_q"), psum("ps_qt"), psum("ps_o")

        rope_loaded, q_src_loaded, passed = sems("rope_loaded"), sems("q_src_loaded"), sems("passed")
        k_loaded = [sems(f"k_loaded{c}") for c in range(2)]
        v_loaded = [sems(f"v_loaded{c}") for c in range(2)]
        scored, masked = sems("scored"), sems("masked")
        exped, inverted, scaled = sems("exped"), sems("inverted"), sems("scaled")
        turned, t_act, t_dve = sems("turned"), sems("t_act"), sems("t_dve")
        valued, o_hi_done, o_lo_done = sems("valued"), sems("o_hi_done"), sems("o_lo_done")
        out_done, added = sems("out_done"), sems("added")
        q_done, rope_read, nope_done, rope_added = sems("q_done"), sems("rope_read"), sems("nope_done"), sems("rope_added")
        q_turned, q_hi_done, q_lo_done = sems("q_turned"), sems("q_hi_done"), sems("q_lo_done")
        q_bank_read = nope_done if latent else rope_read
        block = ctx.enter_context(nc.Block())

        q_weights = [(slot, wt.rearrange("p (r c n) -> p r c n", r=ROUNDS, c=2)) for slot, wt in a.q_passes]
        out_w = [t[:].rearrange("p (r m) n -> p r m n", r=ROUNDS) for t in (a.out_hi, a.out_lo)]
        UQ = BODY

        def wait_q_tok(eng, u, unit):
            if u >= Q_RING:
                eng.wait_ge(q_turned, unit + (u - Q_RING + 1))
            elif not isinstance(unit, int):
                eng.wait_ge(q_turned, unit)

        @block.sync
        def _(sp):
            for k in range(2):
                sp.dma_start(rope[:, k], a.rope[k].rearrange("(j p) n -> p j n", p=P)).then_inc(rope_loaded, 16)
            sp.dma_start(q_src[:].bitcast(F32), a.scratch["q_src"][0]).then_inc(q_src_loaded, 16)

            def load_kv(c, b, r):
                kk, vv = (a.scratch["k"][b], a.scratch["v"][b]) if latent else \
                    (a.scratch["k"][b, r, c], a.scratch["v"][b, r, c])
                return kk, vv

            for c in range(2):
                kk, vv = load_kv(c, 0, 0)
                sp.dma_start(keys[c][:].bitcast(F32), kk).then_inc(k_loaded[c], 16)
                sp.dma_start(values[c][:], vv).then_inc(v_loaded[c], 16)

            def reload(done, b, r):
                for c in range(2):
                    kk, vv = load_kv(c, b, r)
                    sp.wait_ge(scored, done * 3 + 12 * (c + 1))
                    sp.dma_start(keys[c][:].bitcast(F32), kk).then_inc(k_loaded[c], 16)
                    sp.wait_ge(valued, done + 4 * (c + 1))
                    sp.dma_start(values[c][:], vv).then_inc(v_loaded[c], 16)

            with sp.Fori(0, B) as b:
                next_b = sp.snap((b + 1) & (B - 1))
                with sp.Fori(0, ROUNDS - 1) as r:
                    reload(sp.snap(b * (BODY * ROUNDS) + r * BODY), b, sp.snap(r + 1))
                done = sp.snap(b * (BODY * ROUNDS))
                wait_alone(sp, q_done, done + BODY * ROUNDS, passed)
                sp.dma_start(q_src[:].bitcast(F32), a.scratch["q_src"][next_b]).then_inc(q_src_loaded, 16)
                reload(sp.snap(b * (BODY * ROUNDS) + (ROUNDS - 1) * BODY), next_b, 0)
            sp.wait_ge(q_src_loaded, 16 * (B + 1))
            for c in range(2):
                sp.wait_ge(k_loaded[c], 16 * (N_ROUNDS + 1))
                sp.wait_ge(v_loaded[c], 16 * (N_ROUNDS + 1))

        @block.gpsimd
        def _(pool):
            pool.sem_inc(rope_added, 2)

            def rope_add(u, unit):
                pool.wait_ge(rope_read, unit + (u + 1) + (0 if latent else 1))
                wait_q_tok(pool, u, unit)
                if latent:
                    last = nc.gpsimd.tensor_tensor(q_tok[u % Q_RING][:, :, 64:P], rot_a[u % 2][:], rot_b[u % 2][:], ALU.add)
                else:
                    def twice(t):
                        return t[:].rearrange("p h (o n) -> p h o n", o=1).to_broadcast([P, 4, 2, HD])
                    last = nc.gpsimd.tensor_tensor(q_tok[u % Q_RING][:].rearrange("p h (o n) -> p h o n", o=2),
                                                   twice(rot_a[u % 2]), twice(rot_b[u % 2]), ALU.add)
                last.then_inc(rope_added, 1)

            for u in range(UQ):
                rope_add(u, 0)

            def scale(k, heads):
                wait_alone(pool, inverted, heads + (k + 1), passed)
                for q in (3, 0, 2, 1):
                    n = P * (q + 1)
                    pr = probs[k % 2][:, P_OFF[q]:P_OFF[q] + n]
                    last = nc.gpsimd.tensor_scalar(pr, pr, inverse[k % 2][:, q:q + 1], 1.0, ALU.mult, ALU.mult)
                last.then_inc(scaled, 1)

            def slot(s, k, heads, unit):
                if s.scores:
                    scale(k, heads)
                if s.unit is not None:
                    rope_add(s.unit, unit)

            for k in FIRST_SLOTS:
                slot(Slot(k, first=True), k, -BODY, None)
            with pool.Fori(0, N_ROUNDS - 1) as i:
                unit = pool.snap(i * UQ + UQ)
                heads = pool.snap(i * BODY)
                for k in SLOTS:
                    slot(Slot(k), k, heads, unit)
            for k in SLOTS:
                slot(Slot(k, last=True), k, BODY * (N_ROUNDS - 1), None)

        @block.tensor
        def _(pe):
            def project(u, unit, nxt, loads):
                if loads is not None:
                    pe.wait_ge(q_src_loaded, loads)
                pe.wait_ge(q_bank_read, unit + (u + 1))
                for n, (slot, wt) in enumerate(q_weights):
                    last = nc.tensor.matmul(ps_q[:, 0:4 * a.width], q_src[:, slot, P * (u % 4):P * (u % 4) + P],
                                            wt[:, nxt, u // 4, :], start=(n == 0), stop=(n == len(q_weights) - 1))
                last.then_inc(q_done, 1)

            def turn_queries(u, unit):
                pe.wait_ge(rope_added, unit + (u + 1) + 2)
                if latent:
                    pe.wait_ge(nope_done, unit + (u + 1) + 1)
                pe.wait_ge(q_lo_done, unit + (u + 1))
                for h in range(4):
                    last = nc.tensor.transpose(ps_qt[:, P * h:P * h + P], q_tok[u % Q_RING][:, h, :], ident[:])
                last.then_inc(q_turned, 1)

            def scores(k, n, heads, heads4, rounds16):
                if n == 0 and k % 4 == 0:
                    pe.wait_ge(q_lo_done, heads + (k + 4 + 1))
                    pe.wait_ge(k_loaded[k // 4 % 2], rounds16 + 16 * (k // BODY + 1))
                pe.wait_ge(masked, heads4 + (4 * k + 3 + n))
                for q, col in SCORE_UNITS[n]:
                    nk = P * (q + 1)
                    for m, (which, slot) in enumerate(a.s_passes):
                        qt = (qt_hi, qt_lo)[which]
                        last = nc.tensor.matmul(ps_s[(3 * k + n) % 2][:, col:col + nk], qt[:, k % BODY, P * q:P * q + P],
                                                keys[k // 4 % 2][:, slot, 0:nk], start=(m == 0), stop=(m == len(a.s_passes) - 1))
                last.then_inc(scored, 1)

            def turn_probs(k, n, heads, heads2):
                if n == 0:
                    pe.wait_ge(scaled, heads + (k + 1))
                if n == 0:
                    pe.wait_ge(t_dve, heads + (k + 1))
                else:
                    pe.wait_ge(t_act, heads2 + (2 * k + n))
                for j, col in TRANS_UNITS[n]:
                    for q in range(j, NT):
                        last = nc.tensor.transpose(ps_t[(3 * k + n) % 2][:, col + P * (q - j):col + P * (q - j) + P],
                                                   probs[k % 2][:, P_OFF[q] + P * j:P_OFF[q] + P * j + P], ident[:])
                last.then_inc(turned, 1)

            def apply(k, heads, heads2, pairs, rounds16):
                if k % 4 == 0:
                    pe.wait_ge(v_loaded[k // 4 % 2], rounds16 + 16 * (k // BODY + 1))
                if k % 2 == 0:
                    pe.wait_ge(o_lo_done, pairs + (k // 2 + 1))
                pe.wait_ge(t_act, heads2 + (2 * k + 3))
                pe.wait_ge(t_dve, heads + (k + 2))
                row = 64 * (k % 2)
                for j in range(NT):
                    n = S - P * j
                    last = nc.tensor.matmul(ps_v[row:row + 64, P * j:S], values[k // 4 % 2][:, j, :],
                                            probs_t[k % 2][:, PT_OFF[j]:PT_OFF[j] + n], start=(j == 0), stop=(j == NT - 1))
                last.then_inc(valued, 1)

            def project_out(c, half, r, pairs):
                pe.wait_ge(o_lo_done, pairs + (2 * c + 2 + 1))
                pe.wait_ge(added, pairs + (2 * c + half + 1))
                for t in range(2):
                    j = 2 * half + t
                    n = 0
                    for e in range(2):
                        for ot, wt in ((ot_hi, 0), (ot_hi, 1), (ot_lo, 0)):
                            last = nc.tensor.matmul(ps_o[:, D * t:D * t + D], ot[e][:, P * j:P * j + P],
                                                    out_w[wt][:, r, 2 * c + e, :], start=(n == 0), stop=(n == 5))
                            n += 1
                last.then_inc(out_done, 1)

            for u in range(UQ):
                project(u, 0, 0, 16 if u == 0 else None)
                if u:
                    turn_queries(u - 1, 0)
            turn_queries(UQ - 1, 0)

            def slot(s, k, r, nxt, loads, unit, heads, heads2, heads4, pairs, rounds16):
                if s.scores:
                    scores(k, 0, heads, heads4, rounds16)
                    scores(k, 1, heads, heads4, rounds16)
                if s.values:
                    turn_probs(k - 1, 0, heads, heads2)
                if s.scores:
                    scores(k, 2, heads, heads4, rounds16)
                if s.values:
                    turn_probs(k - 1, 1, heads, heads2)
                if s.unit is not None:
                    project(s.unit, unit, nxt, loads if s.unit == 0 else None)
                if s.values:
                    turn_probs(k - 1, 2, heads, heads2)
                if s.turned_unit is not None:
                    turn_queries(s.turned_unit, unit)
                if s.out is not None:
                    project_out(s.out, 0, r, pairs)
                if s.values:
                    apply(k - 1, heads, heads2, pairs, rounds16)
                if s.out is not None:
                    project_out(s.out, 1, r, pairs)
                if s.last_unit:
                    turn_queries(UQ - 1, unit)

            for k in FIRST_SLOTS:
                slot(Slot(k, first=True), k, None, None, None, None, -BODY, -2 * BODY, -4 * BODY, -BODY // 2, -16)
            with pe.Fori(0, N_ROUNDS - 1) as i:
                r = pe.snap(i & (ROUNDS - 1))
                nxt = pe.snap((i + 1) & (ROUNDS - 1))
                loads = pe.snap((((i + 1) >> 2) + 1) * 16)
                heads = pe.snap(i * BODY)
                unit = pe.snap(i * UQ + UQ)
                heads2 = pe.snap(i * (2 * BODY))
                heads4 = pe.snap(i * (4 * BODY))
                pairs = pe.snap(i * (BODY // 2))
                rounds16 = pe.snap(i * 16)
                for k in SLOTS:
                    slot(Slot(k), k, r, nxt, loads, unit, heads, heads2, heads4, pairs, rounds16)
            n = N_ROUNDS - 1
            for k in SLOTS:
                slot(Slot(k, last=True), k, ROUNDS - 1, None, None, None, n * BODY, n * 2 * BODY, n * 4 * BODY, n * BODY // 2, n * 16)

        @block.scalar
        def _(act):
            act.sem_inc(t_act, 1)

            def copy_nope(u, unit):
                if latent:
                    act.wait_ge(rope_read, unit + (u + 1))
                    wait_q_tok(act, u, unit)
                    nc.scalar.activation(q_tok[u % Q_RING][:, :, 0:64], ps_q[:].rearrange("p (h n) -> p h n", h=4)[:, :, 0:64],
                                         ACT.Copy).then_inc(nope_done, 1)

            def queries_hi(u, unit):
                act.wait_ge(q_turned, unit + (u + 1))
                h = 4 * (u // 4)
                nc.scalar.activation(qt_hi[:, h:h + 4, P * (u % 4):P * (u % 4) + P], ps_qt[:].rearrange("p (h n) -> p h n", h=4),
                                     ACT.Copy).then_inc(q_hi_done, 1)

            def exps(k, order, tiles_done):
                for q in order:
                    n = (3, 0, 2, 1).index(q)
                    act.wait_ge(masked, tiles_done + (4 * k + n + 1 + 4))
                    pr = probs[k % 2][:, P_OFF[q]:P_OFF[q] + P * (q + 1)]
                    last = nc.scalar.activation(pr, pr, ACT.Exp, scale=-1.0, bias=neg_max[k % 2][:, q:q + 1],
                                                accum_out=total[k % 2][:, q:q + 1])
                if q == 1:
                    last.then_inc(exped, 1)

            def copy_turned(k, n, heads3):
                act.wait_ge(turned, heads3 + (3 * k + n + 1))
                j = TRANS_UNITS[n][0][0]
                m = S - P * j
                nc.scalar.activation(probs_t[k % 2][:, PT_OFF[j]:PT_OFF[j] + m], ps_t[(3 * k + n) % 2][:, 0:m], ACT.Copy)\
                    .then_inc(t_act, 1)

            def values_hi(m, heads, pairs):
                act.wait_ge(valued, heads + (2 * m + 2))
                act.wait_ge(out_done, pairs + (m // 2 * 2 + 2))
                nc.scalar.activation(ot_hi[m % 2][:], ps_v[:], ACT.Copy).then_inc(o_hi_done, 1)

            for u in range(UQ):
                copy_nope(u, 0)
                if u:
                    queries_hi(u - 1, 0)
            queries_hi(UQ - 1, 0)

            def slot(s, k, unit, heads, heads3, tiles_done, pairs):
                if s.pair is not None:
                    values_hi(s.pair, heads, pairs)
                if s.scores:
                    exps(k, (3, 0, 2), tiles_done)
                if s.values:
                    copy_turned(k - 1, 0, heads3)
                if s.scores:
                    exps(k, (1,), tiles_done)
                if s.values:
                    copy_turned(k - 1, 2, heads3)
                if s.unit is not None:
                    copy_nope(s.unit, unit)
                if s.turned_unit is not None:
                    queries_hi(s.turned_unit, unit)
                if s.last_unit:
                    queries_hi(UQ - 1, unit)

            for k in FIRST_SLOTS:
                slot(Slot(k, first=True), k, None, -BODY, -3 * BODY, -4 * BODY, -BODY // 2)
            with act.Fori(0, N_ROUNDS - 1) as i:
                heads = act.snap(i * BODY)
                unit = act.snap(i * UQ + UQ)
                heads3 = act.snap(i * (3 * BODY))
                tiles_done = act.snap(i * (4 * BODY))
                pairs = act.snap(i * (BODY // 2))
                for k in SLOTS:
                    slot(Slot(k), k, unit, heads, heads3, tiles_done, pairs)
            n = N_ROUNDS - 1
            for k in SLOTS:
                slot(Slot(k, last=True), k, None, n * BODY, n * 3 * BODY, n * 4 * BODY, n * BODY // 2)

        @block.vector
        def _(dve):
            dve.sem_inc(masked, 4)
            dve.sem_inc(t_dve, 1)
            dve.sem_inc(o_lo_done, 1)
            dve.sem_inc(added, 1)
            dve.sem_inc(q_lo_done, 1)
            dve.sem_inc(out_done, 2)
            dve.sem_inc(q_bank_read, 1)
            dve.wait_ge(rope_loaded, 32)

            def rotate(u, unit):
                dve.wait_ge(q_done, unit + (u + 1))
                dve.wait_ge(rope_added, unit + (u + 1))
                x = ps_q[:, 0:4 * a.width].rearrange("p (h n) -> p h n", h=4)[:, :, a.width - DR:a.width]
                j = u % 4
                nc.vector.tensor_tensor(rot_a[u % 2][:], x, rope[:, 0, j:j + 1, :].to_broadcast([P, 4, DR]), ALU.mult)
                swapped = x.rearrange("p h (t c) -> p h t c", t=2)[:, :, ::-1, :]
                sines = rope[:, 1, j:j + 1, :].rearrange("p o (t c) -> p o t c", t=2).to_broadcast([P, 4, 2, HALF])
                nc.vector.tensor_tensor(rot_b[u % 2][:].rearrange("p h (t c) -> p h t c", t=2), swapped, sines, ALU.mult)\
                    .then_inc(rope_read, 1)

            def queries_lo(u, unit):
                dve.wait_ge(q_hi_done, unit + (u + 1))
                h = 4 * (u // 4)
                cols = slice(P * (u % 4), P * (u % 4) + P)
                nc.vector.tensor_tensor(qt_lo[:, h:h + 4, cols], ps_qt[:].rearrange("p (h n) -> p h n", h=4),
                                        qt_hi[:, h:h + 4, cols].bitcast(F32), ALU.subtract).then_inc(q_lo_done, 1)

            def mask_and_max(k, heads3):
                if not isinstance(heads3, int) or heads3 + 3 * k >= 6:
                    dve.wait_ge(turned, heads3 + 3 * (k - 1))
                for n, tiles in enumerate(SCORE_UNITS):
                    wait_alone(dve, scored, heads3 + (3 * k + n + 1), passed)
                    for q, col in tiles:
                        nk = P * (q + 1)
                        last = nc.vector.tensor_tensor_reduce(
                            out=probs[k % 2][:, P_OFF[q]:P_OFF[q] + nk], in0=ps_s[(3 * k + n) % 2][:, col:col + nk],
                            in1=mask[:, 512 - nk:512], scale=-a.scale, scalar=BIG, op0=ALU.add, op1=ALU.min,
                            accum_out=neg_max[k % 2][:, q:q + 1])
                        last.then_inc(masked, 1)

            def invert(k, heads):
                dve.wait_ge(exped, heads + (k + 1))
                nc.vector.reciprocal(inverse[k % 2][:], total[k % 2][:]).then_inc(inverted, 1)

            def copy_turned(k, heads3):
                dve.wait_ge(turned, heads3 + (3 * k + 2))
                o = probs_t[k % 2][:, PT_OFF[1]:PT_OFF[1] + 384]
                nc.vector.tensor_copy(o, ps_t[(3 * k + 1) % 2][:, 0:384])
                nc.vector.tensor_copy(probs_t[k % 2][:, PT_OFF[3]:PT_OFF[3] + P], ps_t[(3 * k + 1) % 2][:, 384:512]).then_inc(t_dve, 1)

            def values_lo(m, pairs):
                dve.wait_ge(o_hi_done, pairs + (m + 1))
                nc.vector.tensor_tensor(ot_lo[m % 2][:], ps_v[:], ot_hi[m % 2][:].bitcast(F32), ALU.subtract).then_inc(o_lo_done, 1)

            def add_out(c, half, b, pairs):
                dve.wait_ge(out_done, pairs + (2 * c + half + 1 + 2))
                xb = x_res[:].rearrange("p (b g t) d -> p b g (t d)", b=B, g=2)[:, b, half, :]
                nc.vector.tensor_tensor(xb, ps_o[:], xb, ALU.add).then_inc(added, 1)

            for u in range(UQ):
                rotate(u, 0)
                if u:
                    queries_lo(u - 1, 0)
            queries_lo(UQ - 1, 0)

            def slot(s, k, b, unit, heads, heads3, pairs):
                if s.scores:
                    mask_and_max(k, heads3)
                if s.values:
                    copy_turned(k - 1, heads3)
                if s.pair is not None:
                    values_lo(s.pair, pairs)
                if s.scores:
                    invert(k, heads)
                if s.unit is not None:
                    rotate(s.unit, unit)
                if s.turned_unit is not None:
                    queries_lo(s.turned_unit, unit)
                if s.out is not None:
                    add_out(s.out, 0, b, pairs)
                    add_out(s.out, 1, b, pairs)
                if s.last_unit:
                    queries_lo(UQ - 1, unit)

            for k in FIRST_SLOTS:
                slot(Slot(k, first=True), k, None, None, -BODY, -3 * BODY, -BODY // 2)
            with dve.Fori(0, N_ROUNDS - 1) as i:
                b = dve.snap((i >> 2) & (B - 1))
                heads = dve.snap(i * BODY)
                unit = dve.snap(i * UQ + UQ)
                heads3 = dve.snap(i * (3 * BODY))
                pairs = dve.snap(i * (BODY // 2))
                for k in SLOTS:
                    slot(Slot(k), k, b, unit, heads, heads3, pairs)
            n = N_ROUNDS - 1
            for k in SLOTS:
                slot(Slot(k, last=True), k, B - 1, None, n * BODY, n * 3 * BODY, n * BODY // 2)


def split_ffn_weights(nc, sems, hbm, w, wkv):
    with ExitStack() as ctx:
        raw = [ctx.enter_context(nc.sbuf_tensor(f"fw_raw{u}", [P, 2048], F32)) for u in range(3)]
        loaded = [sems(f"raw_loaded{u}") for u in range(3)]
        hi_done, lo_done = sems("hi_done"), sems("lo_done")
        wq = hbm["L0_ffn_wq"].rearrange("(k p) n -> k p n", p=P)
        wk = hbm["L0_ffn_wk"].rearrange("(k p) n -> k p n", p=P)
        wv = hbm["L0_ffn_wv"].rearrange("(k p) n -> k p n", p=P)
        wo = hbm["L0_ffn_wo"].rearrange("(m p) n -> p m n", p=P)
        jobs = [([(wk[k], 0, 512), (wv[k], 512, 1024)], wkv[0][:, k, :], wkv[1][:, k, :]) for k in range(KT)]
        jobs += [([(wq[k], 0, 2048)], w["wq_hi"][:, k, :], w["wq_lo"][:, k, :]) for k in range(KT)]
        for k in range(2):
            jobs.append(([(wo[:, 8 * k:8 * k + 8, :], 0, 2048)],
                         *(w[n][:].rearrange("p (k m) n -> p k (m n)", k=2)[:, k] for n in ("wo_hi", "wo_lo"))))
        block = ctx.enter_context(nc.Block())

        @block.sync
        def _(sp):
            for n, (parts, _, _) in enumerate(jobs):
                if n >= 3:
                    sp.wait_ge(lo_done, n - 2)
                for src, c0, c1 in parts:
                    dst = raw[n % 3][:, c0:c1]
                    if len(src.shape) == 3:
                        dst = dst.rearrange("p (m n) -> p m n", n=D)
                    sp.dma_start(dst, src).then_inc(loaded[n % 3], 16)

        @block.scalar
        def _(act):
            seen = [0, 0, 0]
            for n, (parts, hi, _) in enumerate(jobs):
                seen[n % 3] += 16 * len(parts)
                act.wait_ge(loaded[n % 3], seen[n % 3])
                nc.scalar.activation(hi, raw[n % 3][:, 0:parts[-1][2]], ACT.Copy).then_inc(hi_done, 1)

        @block.vector
        def _(dve):
            for n, (parts, hi, lo) in enumerate(jobs):
                dve.wait_ge(hi_done, n + 1)
                nc.vector.tensor_tensor(lo, raw[n % 3][:, 0:parts[-1][2]], hi.bitcast(F32), ALU.subtract).then_inc(lo_done, 1)


def ffn_inputs(nc, sems, hbm, x_res, ident, exponent, wkv, scratch):
    with ExitStack() as ctx:
        def sb(name, shape, dt=F32):
            return ctx.enter_context(nc.sbuf_tensor("fi_" + name, shape, dt))

        U = 2
        ROUNDS_IN = TILES // U
        ln_w = sb("ln_w", [P, D])
        rope = sb("rope", [P, 2, NT, DR])
        stats, mv = sb("stats", [P, U, 6]), sb("mv", [P, U, 2])
        var_eps, rstd = sb("var_eps", [P, U]), sb("rstd", [P, U])
        square, ms, ms_eps, rms = sb("square", [P, U, D]), sb("ms", [P, U]), sb("ms_eps", [P, U]), sb("rms", [P, U])
        h = sb("h", [P, U, D])
        ht_hi, ht_lo = sb("ht_hi", [P, U, KT, P], F32R), sb("ht_lo", [P, U, KT, P], F32R)
        rot_a, rot_b = sb("rot_a", [P, U, KVH, DR]), sb("rot_b", [P, U, KVH, DR])
        k_tok, v_tok = sb("k_tok", [P, U, KVH, 2, HD]), sb("v_tok", [P, U, KVH, HD])
        k_stack = sb("k_stack", [P, U, KVH, P], F32R)
        ps_t = [ctx.enter_context(nc.psum_tensor(f"fi_ps_t{u}", [P, 512], F32)) for u in range(U)]
        ps_k = [ctx.enter_context(nc.psum_tensor(f"fi_ps_k{u}", [P, 512], F32)) for u in range(U)]
        ps_v = [ctx.enter_context(nc.psum_tensor(f"fi_ps_v{u}", [P, 512], F32)) for u in range(U)]
        ps_kt = [ctx.enter_context(nc.psum_tensor(f"fi_ps_kt{g}", [P, 512], F32)) for g in range(2)]

        loaded, x_saved, bn, mean_var, eps_added, rstd_done = (
            sems(n) for n in ("loaded", "x_saved", "bn", "mean_var", "eps_added", "rstd_done"))
        xi_done, squared, ms_eps_added, rms_done, h_done = (
            sems(n) for n in ("xi_done", "squared", "ms_eps_added", "rms_done", "h_done"))
        turned, hi_done, lo_done, projected, rotated, added = (
            sems(n) for n in ("turned", "hi_done", "lo_done", "projected", "rotated", "added"))
        v_done, k_turned, k_hi_done, k_lo_done, stored, passed = (
            sems(n) for n in ("v_done", "k_turned", "k_hi_done", "k_lo_done", "stored", "passed"))
        block = ctx.enter_context(nc.Block())
        N_STORES = 4 * U

        @block.sync
        def _(sp):
            sp.dma_start(scratch["x1"], x_res[:]).then_inc(x_saved, 16)
            sp.dma_start(ln_w[:], hbm["L0_ffn_ln_w"].rearrange("(o n) -> o n", o=1).to_broadcast([P, D])).then_inc(loaded, 16)
            for k in range(2):
                sp.dma_start(rope[:, k], hbm["rope_ffn"][k].rearrange("(j p) n -> p j n", p=P)).then_inc(loaded, 16)
            with sp.Fori(0, B) as b:
                with sp.Fori(0, NT // U) as x:
                    done = sp.snap(b * NT + x * U)
                    for u in range(U):
                        qs = scratch["q_src"][b].rearrange("p k (x u n) -> p k x u n", x=2, u=2)[:, :, x, u, :]
                        kk = scratch["k"][b].rearrange("g p (x u n) -> p g x u n", x=2, u=2)[:, :, x, u, :]
                        vv = scratch["v"][b].rearrange("g p (x u) n -> p g x u n", x=2)[:, :, x, u, :]
                        sp.wait_ge(lo_done, done + (u + 1))
                        sp.dma_start(qs[:, 0:2], ht_hi[:, u].bitcast(F32)).then_inc(stored, 16)
                        sp.dma_start(qs[:, 2:4], ht_lo[:, u].bitcast(F32)).then_inc(stored, 16)
                        sp.wait_ge(v_done, done + (u + 1))
                        sp.dma_start(vv, v_tok[:, u]).then_inc(stored, 16)
                        sp.wait_ge(k_lo_done, done * 2 + (2 * (u + 1) + 2))
                        sp.dma_start(kk, k_stack[:, u].bitcast(F32)).then_inc(stored, 16)
            sp.wait_ge(stored, 16 * N_STORES * (ROUNDS_IN + 1))

        @block.gpsimd
        def _(pool):
            pool.sem_inc(stored, 16 * N_STORES)
            with pool.Fori(0, ROUNDS_IN) as i:
                base = pool.snap(i * U)
                for u in range(U):
                    wait_alone(pool, mean_var, base + (u + 1), passed)
                    nc.gpsimd.tensor_scalar(var_eps[:, u:u + 1], mv[:, u, 1:2], LN_EPS, 1.0, ALU.add, ALU.mult).then_inc(eps_added, 1)
                    pool.wait_ge(eps_added, base + (u + 1))
                    nc.gpsimd.tensor_tensor(rstd[:, u:u + 1], var_eps[:, u:u + 1], exponent[:], ALU.pow).then_inc(rstd_done, 1)
                for u in range(U):
                    wait_alone(pool, squared, base + (u + 1), passed)
                    nc.gpsimd.tensor_scalar(ms_eps[:, u:u + 1], ms[:, u:u + 1], FFN_EPS, 1.0, ALU.add, ALU.mult).then_inc(ms_eps_added, 1)
                    pool.wait_ge(ms_eps_added, base + (u + 1))
                    nc.gpsimd.tensor_tensor(rms[:, u:u + 1], ms_eps[:, u:u + 1], exponent[:], ALU.pow).then_inc(rms_done, 1)
                for u in range(U):
                    pool.wait_ge(rotated, base + (u + 1))

                    def twice(t):
                        return t[:, u].rearrange("p g (o n) -> p g o n", o=1).to_broadcast([P, KVH, 2, HD])
                    nc.gpsimd.tensor_tensor(k_tok[:, u], twice(rot_a), twice(rot_b), ALU.add).then_inc(added, 1)

        @block.tensor
        def _(pe):
            with pe.Fori(0, ROUNDS_IN) as i:
                base = pe.snap(i * U)
                halves = pe.snap(i * (2 * U))
                for u in range(U):
                    pe.wait_ge(h_done, base + (u + 1))
                    for k in range(KT):
                        last = nc.tensor.transpose(ps_t[u][:, P * k:P * k + P], h[:, u, P * k:P * k + P], ident[:])
                    last.then_inc(turned, 1)
                for u in range(U):
                    pe.wait_ge(lo_done, base + (u + 1))
                    for ps, c0 in ((ps_k[u], 0), (ps_v[u], 512)):
                        n = 0
                        for k in range(KT):
                            for x, wt in ((ht_hi, 0), (ht_hi, 1), (ht_lo, 0)):
                                last = nc.tensor.matmul(ps[:], x[:, u, k, :], wkv[wt][:, k, c0:c0 + 512], start=(n == 0), stop=(n == 5))
                                n += 1
                    last.then_inc(projected, 1)
                for u in range(U):
                    pe.wait_ge(added, base + (u + 1))
                    for g in range(2):
                        pe.wait_ge(k_lo_done, halves + (2 * u + g + 1))
                        for n in range(4):
                            last = nc.tensor.transpose(ps_kt[g][:, P * n:P * n + P],
                                                       k_tok[:, u, 4 * g + n].rearrange("p o n -> p (o n)"), ident[:])
                        last.then_inc(k_turned, 1)

        @block.scalar
        def _(act):
            with act.Fori(0, ROUNDS_IN) as i:
                base = act.snap(i * U)
                halves = act.snap(i * (2 * U))
                stores = act.snap(i * (16 * N_STORES))
                xr = x_res[:].rearrange("p (i u) d -> p i u d", u=U)
                for u in range(U):
                    act.wait_ge(xi_done, base + (u + 1))
                    nc.scalar.activation(square[:, u, :], xr[:, i, u, :], ACT.Square, scale=float(D) ** -0.5,
                                         accum_out=ms[:, u:u + 1]).then_inc(squared, 1)
                act.wait_ge(stored, stores + 16 * N_STORES)
                for u in range(U):
                    act.wait_ge(turned, base + (u + 1))
                    nc.scalar.activation(ht_hi[:, u].rearrange("p k n -> p (k n)"), ps_t[u][:, 0:D], ACT.Copy).then_inc(hi_done, 1)
                for u in range(U):
                    act.wait_ge(projected, base + (u + 1))
                    nc.scalar.activation(v_tok[:, u].rearrange("p g n -> p (g n)"), ps_v[u][:], ACT.Copy).then_inc(v_done, 1)
                for u in range(U):
                    for g in range(2):
                        act.wait_ge(k_turned, halves + (2 * u + g + 1))
                        nc.scalar.activation(k_stack[:, u, 4 * g:4 * g + 4].rearrange("p g n -> p (g n)"), ps_kt[g][:], ACT.Copy)\
                            .then_inc(k_hi_done, 1)

        @block.vector
        def _(dve):
            dve.sem_inc(k_lo_done, 2)
            dve.wait_ge(loaded, 48)
            dve.wait_ge(x_saved, 16)
            with dve.Fori(0, ROUNDS_IN) as i:
                base = dve.snap(i * U)
                halves = dve.snap(i * (2 * U))
                stores = dve.snap(i * (16 * N_STORES))
                x = dve.snap(i & 1)
                xr = x_res[:].rearrange("p (i u) d -> p i u d", u=U)
                table = rope[:].rearrange("p s (x u) n -> p s x u n", x=2)
                for u in range(U):
                    nc.vector.bn_stats(stats[:, u, :], xr[:, i, u, :]).then_inc(bn, 1)
                for u in range(U):
                    wait_alone(dve, bn, base + (u + 1), passed)
                    nc.vector.bn_aggr(mv[:, u, :], stats[:, u, :]).then_inc(mean_var, 1)
                for u in range(U):
                    dve.wait_ge(rstd_done, base + (u + 1))
                    nc.vector.tensor_scalar(xr[:, i, u, :], xr[:, i, u, :], mv[:, u, 0:1], rstd[:, u:u + 1], ALU.subtract, ALU.mult)\
                        .then_inc(xi_done, 1)
                for u in range(U):
                    dve.wait_ge(rms_done, base + (u + 1))
                    dve.wait_ge(xi_done, base + (u + 1))
                    nc.vector.scalar_tensor_tensor(out=h[:, u, :], in0=xr[:, i, u, :], scalar=rms[:, u:u + 1], in1=ln_w[:],
                                                   op0=ALU.mult, op1=ALU.mult).then_inc(h_done, 1)
                dve.wait_ge(stored, stores + 16 * N_STORES)
                for u in range(U):
                    dve.wait_ge(hi_done, base + (u + 1))
                    nc.vector.tensor_tensor(ht_lo[:, u].rearrange("p k n -> p (k n)"), ps_t[u][:, 0:D],
                                            ht_hi[:, u].bitcast(F32).rearrange("p k n -> p (k n)"), ALU.subtract).then_inc(lo_done, 1)
                for u in range(U):
                    dve.wait_ge(projected, base + (u + 1))
                    k3 = ps_k[u][:].rearrange("p (g n) -> p g n", g=KVH)
                    nc.vector.tensor_tensor(rot_a[:, u], k3, table[:, 0, x, u:u + 1, :].to_broadcast([P, KVH, DR]), ALU.mult)
                    nc.vector.tensor_tensor(rot_b[:, u].rearrange("p g (t c) -> p g t c", t=2),
                                            k3.rearrange("p g (t c) -> p g t c", t=2)[:, :, ::-1, :],
                                            table[:, 1, x, u:u + 1, :].rearrange("p o (t c) -> p o t c", t=2).to_broadcast([P, KVH, 2, HALF]),
                                            ALU.mult).then_inc(rotated, 1)
                for u in range(U):
                    for g in range(2):
                        dve.wait_ge(k_hi_done, halves + (2 * u + g + 1))
                        ks = k_stack[64:P, u, 4 * g:4 * g + 4].rearrange("p g n -> p (g n)")
                        nc.vector.tensor_tensor(ks, ps_kt[g][64:P, :], ks.bitcast(F32), ALU.subtract).then_inc(k_lo_done, 1)


def route(nc, sems, hbm, x_res, ident, exponent, gates, h_hi, h_lo, raw13, raw2, expert_loaded, scratch):
    with ExitStack() as ctx:
        def sb(name, shape, dt=F32):
            return ctx.enter_context(nc.sbuf_tensor("rt_" + name, shape, dt))

        U = NT
        ff_w, wg, numbers = sb("ff_w", [P, D]), sb("wg", [P, KT, E]), sb("numbers", [P, E])
        x1 = sb("x1", [P, TILES, D])
        square, ms, ms_eps, rms = sb("square", [P, U, D]), sb("ms", [P, U]), sb("ms_eps", [P, U]), sb("rms", [P, U])
        h, h_now = sb("h", [P, U, D]), sb("h_now", [P, U, D])
        logits, top, index = sb("logits", [P, U, E]), sb("top", [P, U, 8]), sb("index", [P, U, 8], U32)
        index_f, neg, e4, esum, einv, g4 = (sb(n, s) for n, s in (
            ("index_f", [P, U, TOPK]), ("neg", [P, U]), ("e4", [P, U, TOPK]), ("esum", [P, U]), ("einv", [P, U]), ("g4", [P, U, TOPK])))
        hot = sb("hot", [P, U, E, TOPK])
        ps_t = [ctx.enter_context(nc.psum_tensor(f"rt_ps_t{u}", [P, 512], F32)) for u in range(U)]
        ps_l = [ctx.enter_context(nc.psum_tensor(f"rt_ps_l{u}", [P, 512], F32)) for u in range(U)]
        names = ("loaded", "squared", "ms_eps_added", "rms_done", "h_done", "turned", "copied", "h_hi_done", "h_lo_done", "routed",
                 "logits_out", "top_done", "index_done", "index_cast", "neg_done", "exped", "inverted", "g4_done", "hot_done",
                 "numbered", "gated", "passed")
        (loaded, squared, ms_eps_added, rms_done, h_done, turned, copied, h_hi_done, h_lo_done, routed, logits_out, top_done,
         index_done, index_cast, neg_done, exped, inverted, g4_done, hot_done, numbered, gated, passed) = (sems(n) for n in names)
        block = ctx.enter_context(nc.Block())

        @block.sync
        def _(sp):
            sp.dma_start(ff_w[:], hbm["L0_ffn_ff_ln_w"].rearrange("(o n) -> o n", o=1).to_broadcast([P, D])).then_inc(loaded, 16)
            sp.dma_start(wg[:], hbm["L0_ffn_wg"].rearrange("(k p) n -> p k n", p=P)).then_inc(loaded, 16)
            sp.dma_start(x1[:], scratch["x1"]).then_inc(loaded, 16)
            for u in range(2):
                load_expert(sp, hbm, raw13[u], raw2[u], (0, u), expert_loaded[u])
            sp.wait_ge(loaded, 48)

        @block.gpsimd
        def _(pool):
            nc.gpsimd.iota(numbers[:], pattern=[[1, E]], base=0, channel_multiplier=0,
                           allow_small_or_imprecise_dtypes=True).then_inc(numbered, 1)
            with pool.Fori(0, TILES // U) as i:
                base = pool.snap(i * U)
                for u in range(U):
                    wait_alone(pool, squared, base + (u + 1), passed)
                    nc.gpsimd.tensor_scalar(ms_eps[:, u:u + 1], ms[:, u:u + 1], FFN_EPS, 1.0, ALU.add, ALU.mult).then_inc(ms_eps_added, 1)
                    pool.wait_ge(ms_eps_added, base + (u + 1))
                    nc.gpsimd.tensor_tensor(rms[:, u:u + 1], ms_eps[:, u:u + 1], exponent[:], ALU.pow).then_inc(rms_done, 1)

        @block.tensor
        def _(pe):
            pe.wait_ge(loaded, 48)
            with pe.Fori(0, TILES // U) as i:
                base = pe.snap(i * U)
                for u in range(U):
                    pe.wait_ge(h_done, base + (u + 1))
                    for k in range(KT):
                        last = nc.tensor.transpose(ps_t[u][:, P * k:P * k + P], h[:, u, P * k:P * k + P], ident[:])
                    last.then_inc(turned, 1)
                for u in range(U):
                    pe.wait_ge(copied, base + (u + 1))
                    for k in range(KT):
                        last = nc.tensor.matmul(ps_l[u][:, 0:E], h_now[:, u, P * k:P * k + P], wg[:, k, :], start=(k == 0), stop=(k == KT - 1))
                    last.then_inc(routed, 1)

        @block.scalar
        def _(act):
            with act.Fori(0, TILES // U) as i:
                base = act.snap(i * U)
                xr = x_res[:].rearrange("p (i u) d -> p i u d", u=U)
                hi = h_hi[:].rearrange("p k (i u n) -> p k i u n", u=U, n=P)
                for u in range(U):
                    nc.scalar.activation(square[:, u, :], xr[:, i, u, :], ACT.Square, scale=float(D) ** -0.5,
                                         accum_out=ms[:, u:u + 1]).then_inc(squared, 1)
                for u in range(U):
                    act.wait_ge(turned, base + (u + 1))
                    nc.scalar.activation(h_now[:, u, :], ps_t[u][:, 0:D], ACT.Copy).then_inc(copied, 1)
                    nc.scalar.activation(hi[:, :, i, u, :], ps_t[u][:, 0:D].rearrange("p (k n) -> p k n", k=KT), ACT.Copy)\
                        .then_inc(h_hi_done, 1)
                for u in range(U):
                    act.wait_ge(neg_done, base + (u + 1))
                    nc.scalar.activation(e4[:, u, :], top[:, u, 0:TOPK], ACT.Exp, bias=neg[:, u:u + 1],
                                         accum_out=esum[:, u:u + 1]).then_inc(exped, 1)

        @block.vector
        def _(dve):
            dve.wait_ge(loaded, 48)
            dve.wait_ge(numbered, 1)
            with dve.Fori(0, TILES // U) as i:
                base = dve.snap(i * U)
                base4 = dve.snap(i * (U * TOPK))
                xr = x_res[:].rearrange("p (i u) d -> p i u d", u=U)
                x1r = x1[:].rearrange("p (i u) d -> p i u d", u=U)
                gt = gates[:].rearrange("p (i u) e -> p i u e", u=U)
                hi, lo = (t[:].rearrange("p k (i u n) -> p k i u n", u=U, n=P) for t in (h_hi, h_lo))
                for u in range(U):
                    dve.wait_ge(rms_done, base + (u + 1))
                    nc.vector.scalar_tensor_tensor(out=h[:, u, :], in0=xr[:, i, u, :], scalar=rms[:, u:u + 1], in1=ff_w[:],
                                                   op0=ALU.mult, op1=ALU.mult).then_inc(h_done, 1)
                for u in range(U):
                    dve.wait_ge(h_done, base + (u + 1))
                    nc.vector.tensor_tensor(xr[:, i, u, :], xr[:, i, u, :], x1r[:, i, u, :], ALU.add)
                for u in range(U):
                    dve.wait_ge(h_hi_done, base + (u + 1))
                    nc.vector.tensor_tensor(lo[:, :, i, u, :], ps_t[u][:, 0:D].rearrange("p (k n) -> p k n", k=KT),
                                            hi[:, :, i, u, :].bitcast(F32), ALU.subtract).then_inc(h_lo_done, 1)
                for u in range(U):
                    dve.wait_ge(routed, base + (u + 1))
                    nc.vector.tensor_copy(logits[:, u, :], ps_l[u][:, 0:E]).then_inc(logits_out, 1)
                for u in range(U):
                    wait_alone(dve, logits_out, base + (u + 1), passed)
                    nc.vector.max(top[:, u, :], logits[:, u, :]).then_inc(top_done, 1)
                for u in range(U):
                    dve.wait_ge(top_done, base + (u + 1))
                    nc.vector.tensor_scalar(neg[:, u:u + 1], top[:, u, 0:1], -1.0, None, ALU.mult).then_inc(neg_done, 1)
                    nc.vector.max_index(index[:, u, :], top[:, u, :], logits[:, u, :]).then_inc(index_done, 1)
                for u in range(U):
                    dve.wait_ge(index_done, base + (u + 1))
                    nc.vector.tensor_copy(index_f[:, u, :], index[:, u, 0:TOPK]).then_inc(index_cast, 1)
                for u in range(U):
                    dve.wait_ge(exped, base + (u + 1))
                    nc.vector.reciprocal(einv[:, u:u + 1], esum[:, u:u + 1]).then_inc(inverted, 1)
                for u in range(U):
                    dve.wait_ge(inverted, base + (u + 1))
                    nc.vector.tensor_scalar(g4[:, u, :], e4[:, u, :], einv[:, u:u + 1], None, ALU.mult).then_inc(g4_done, 1)
                for u in range(U):
                    dve.wait_ge(g4_done, base + (u + 1))
                    dve.wait_ge(index_cast, base + (u + 1))
                    for k in range(TOPK):
                        nc.vector.tensor_scalar(hot[:, u, :, k], numbers[:], index_f[:, u, k:k + 1], g4[:, u, k:k + 1],
                                                ALU.is_equal, ALU.mult).then_inc(hot_done, 1)
                for u in range(U):
                    dve.wait_ge(hot_done, base4 + TOPK * (u + 1))
                    nc.vector.tensor_reduce(gt[:, i, u, :], hot[:, u], AX_X, ALU.add).then_inc(gated, 1)


def expert_loads(hbm, name, rows):
    return hbm[name].rearrange("(i u) (k p) h -> i u p k h", u=2, p=P)[rows]


def load_expert(sp, hbm, raw13, raw2, rows, loaded):
    for n, name in enumerate(("L0_ffn_w1", "L0_ffn_w3")):
        sp.dma_start(raw13[:, :, H * n:H * n + H], expert_loads(hbm, name, rows)).then_inc(loaded, 16)
    sp.dma_start(raw2[:], expert_loads(hbm, "L0_ffn_w2", rows)).then_inc(loaded, 16)


def experts_dense(nc, sems, hbm, x_res, gates, h_hi, h_lo, raw13, raw2, loaded, out):
    with ExitStack() as ctx:
        def sb(name, shape, dt=F32):
            return ctx.enter_context(nc.sbuf_tensor("ex_" + name, shape, dt))

        U, G, C = 2, B, H // P
        w13 = [[sb(f"w13_{part}{u}", [P, KT, 2 * H], F32R) for part in ("hi", "lo")] for u in range(U)]
        w2 = [[sb(f"w2_{part}{u}", [P, KT, D], F32R) for part in ("hi", "lo")] for u in range(U)]
        silu = [sb(f"silu{c}", [P, S]) for c in range(C)]
        a = [sb(f"a{c}", [P, S]) for c in range(C)]
        a_hi = [[sb(f"a_hi{r}{c}", [P, S], F32R) for c in range(C)] for r in range(2)]
        a_lo = [[sb(f"a_lo{r}{c}", [P, S], F32R) for c in range(C)] for r in range(2)]
        ps_g, ps_u = ([ctx.enter_context(nc.psum_tensor(f"ex_{n}{c}", [P, S], F32)) for c in range(C)] for n in ("ps_g", "ps_u"))
        ps_y = [ctx.enter_context(nc.psum_tensor(f"ex_ps_y{r}", [P, 512], F32)) for r in range(4)]
        names = ("w_hi", "w_lo", "up", "silued", "mixed", "a_hi_done", "a_lo_done", "down", "added", "stored")
        w_hi, w_lo, up, silued, mixed, a_hi_done, a_lo_done, down, added, stored = (sems(n) for n in names)
        block = ctx.enter_context(nc.Block())
        STEPS = U * G
        ROUNDS_E = E // U
        PASSES = ((0, 0), (0, 1), (1, 0))

        @block.sync
        def _(sp):
            with sp.Fori(0, ROUNDS_E - 1) as i:
                split = sp.snap(i * U)
                for u in range(U):
                    sp.wait_ge(w_lo, split + (u + 1))
                    load_expert(sp, hbm, raw13[u], raw2[u], (i + 1, u), loaded[u])
            sp.wait_ge(added, 4 * G * E + 8)
            sp.dma_start(out.rearrange("b (j p) d -> p (b j) d", p=P), x_res[:]).then_inc(stored, 16)
            sp.wait_ge(stored, 16)

        @block.tensor
        def _(pe):
            def gate_up(s, c, base2, experts):
                u, g = s // G, s % G
                if g == 0 and c == 0:
                    pe.wait_ge(w_lo, experts + (u + 1))
                pe.wait_ge(mixed, base2 + (2 * s + c + 1))
                for ps, c0 in ((ps_g[c], P * c), (ps_u[c], H + P * c)):
                    n = 0
                    for k in range(KT):
                        for wt, x in PASSES:
                            last = nc.tensor.matmul(ps[:], w13[u][wt][:, k, c0:c0 + P], (h_hi, h_lo)[x][:, k, S * g:S * g + S],
                                                    start=(n == 0), stop=(n == 3 * KT - 1))
                            n += 1
                last.then_inc(up, 1)

            def project(s, base2, base4):
                pe.wait_ge(a_lo_done, base2 + (2 * s + 2))
                for half in range(2):
                    pe.wait_ge(added, base4 + (4 * s + 2 * half + 2))
                    for t in (2 * half, 2 * half + 1):
                        n = 0
                        for k in range(C):
                            for x, wt in PASSES:
                                last = nc.tensor.matmul(ps_y[2 * (s % 2) + half][:, D * (t % 2):D * (t % 2) + D],
                                                        (a_hi, a_lo)[x][s % 2][k][:, P * t:P * t + P],
                                                        w2[s // G % 2][wt][:, k, :], start=(n == 0), stop=(n == 3 * C - 1))
                                n += 1
                    last.then_inc(down, 1)

            gate_up(0, 0, 0, 0)
            gate_up(0, 1, 0, 0)
            with pe.Fori(0, ROUNDS_E - 1) as i:
                base2 = pe.snap(i * (2 * STEPS))
                base4 = pe.snap(i * (4 * STEPS))
                experts = pe.snap(i * U)
                for s in range(1, STEPS + 1):
                    gate_up_of = s % STEPS
                    ahead = (2 * STEPS, U) if s == STEPS else (0, 0)
                    gate_up(gate_up_of, 0, base2 + ahead[0], experts + ahead[1])
                    gate_up(gate_up_of, 1, base2 + ahead[0], experts + ahead[1])
                    project(s - 1, base2, base4)
            n = ROUNDS_E - 1
            for s in range(1, STEPS + 1):
                if s < STEPS:
                    gate_up(s, 0, n * 2 * STEPS, n * U)
                    gate_up(s, 1, n * 2 * STEPS, n * U)
                project(s - 1, n * 2 * STEPS, n * 4 * STEPS)

        @block.scalar
        def _(act):
            def split_hi(u, loads, downs):
                act.wait_ge(loaded[u], loads)
                if downs is not None:
                    act.wait_ge(down, downs)
                nc.scalar.activation(w13[u][0][:], raw13[u][:], ACT.Copy)
                nc.scalar.activation(w2[u][0][:], raw2[u][:], ACT.Copy).then_inc(w_hi, 1)

            def step(s, base2):
                for c in range(C):
                    act.wait_ge(up, base2 + (2 * s + c + 1))
                    nc.scalar.activation(silu[c][:], ps_g[c][:], ACT.Silu).then_inc(silued, 1)
                for c in range(C):
                    act.wait_ge(mixed, base2 + (2 * s + c + 1 + 2))
                    if c == 0:
                        act.wait_ge(down, base2 + (2 * s - 2 + 4))
                    nc.scalar.activation(a_hi[s % 2][c][:], a[c][:], ACT.Copy).then_inc(a_hi_done, 1)

            def round_of(base2, loads, last):
                for s in range(STEPS):
                    step(s, base2)
                    if s == 2:
                        split_hi(1, loads + 48, base2 + 4)
                    if s == G + 2 and not last:
                        split_hi(0, loads + 96, base2 + (2 * G + 4))

            split_hi(0, 48, None)
            with act.Fori(0, ROUNDS_E - 1) as i:
                round_of(act.snap(i * (2 * STEPS)), act.snap(i * 48), False)
            round_of((ROUNDS_E - 1) * 2 * STEPS, (ROUNDS_E - 1) * 48, True)

        @block.vector
        def _(dve):
            dve.sem_inc(mixed, 2)
            dve.sem_inc(added, 8)
            dve.sem_inc(down, 4)

            def split_lo(u, splits):
                dve.wait_ge(w_hi, splits)
                nc.vector.tensor_tensor(w13[u][1][:], raw13[u][:], w13[u][0][:].bitcast(F32), ALU.subtract)
                nc.vector.tensor_tensor(w2[u][1][:], raw2[u][:], w2[u][0][:].bitcast(F32), ALU.subtract).then_inc(w_lo, 1)

            def add(s, base2, i):
                u, g = s // G, s % G
                for t in range(NT):
                    if t % 2 == 0:
                        dve.wait_ge(down, base2 + (2 * s + t // 2 + 1 + 4))
                    j = NT * g + t
                    gt = gates[:].rearrange("p t (i u) -> p t i u", u=U)[:, j, i, u:u + 1]
                    nc.vector.scalar_tensor_tensor(out=x_res[:, j, :], in0=ps_y[2 * (s % 2) + t // 2][:, D * (t % 2):D * (t % 2) + D],
                                                   scalar=gt, in1=x_res[:, j, :], op0=ALU.mult, op1=ALU.add).then_inc(added, 1)

            def step(s, base2):
                for c in range(C):
                    dve.wait_ge(silued, base2 + (2 * s + c + 1))
                    if not isinstance(base2, int) or base2 + s > 0:
                        dve.wait_ge(a_lo_done, base2 + (2 * s + c - 1))
                    nc.vector.tensor_tensor(a[c][:], ps_u[c][:], silu[c][:], ALU.mult).then_inc(mixed, 1)
                for c in range(C):
                    dve.wait_ge(a_hi_done, base2 + (2 * s + c + 1))
                    nc.vector.tensor_tensor(a_lo[s % 2][c][:], a[c][:], a_hi[s % 2][c][:].bitcast(F32), ALU.subtract)\
                        .then_inc(a_lo_done, 1)

            def round_of(i, base2, splits, last):
                for s in range(1, STEPS + 1):
                    if s < STEPS:
                        step(s, base2)
                    elif not last:
                        step(0, base2 + 2 * STEPS)
                    if s == 2:
                        split_lo(1, splits + 2)
                    if s == G + 2 and not last:
                        split_lo(0, splits + 3)
                    add(s - 1, base2, i)

            split_lo(0, 1)
            step(0, 0)
            with dve.Fori(0, ROUNDS_E - 1) as i:
                round_of(i, dve.snap(i * (2 * STEPS)), dve.snap(i * U), False)
            round_of(ROUNDS_E - 1, (ROUNDS_E - 1) * 2 * STEPS, (ROUNDS_E - 1) * U, True)


def build(nc, hbm, out, upto=9):
    with ExitStack() as ctx:
        def sb(name, shape, dt=F32, c=ctx):
            return c.enter_context(nc.sbuf_tensor(name, shape, dt))

        def dram(name, shape):
            return nc.dram_tensor("scratch_" + name, shape, F32, kind="Internal").ap()

        x_res = sb("x_res", [P, TILES, D])
        ident, mask, exponent = sb("ident", [P, P]), sb("mask", [P, S]), sb("exponent", [P, 1])
        start_constants(nc, Sems(nc, ctx, "sc"), hbm, x_res, ident, mask, exponent)

        with ExitStack() as layer:
            w = {n: sb(n, [P, NH * P], F32R, layer) for n in ("w1hi", "w1lo", "w2hi", "w2lo")}
            w |= {n: sb(n, [P, NH // 2, D], F32R, layer) for n in ("vohi", "volo")}
            latent_scratch = {"q_src": dram("lq", [B, P, 3, S]), "k": dram("lk", [B, P, 2, S]), "v": dram("lv", [B, P, NT, KVLR])}
            prepare_latent_weights(nc, Sems(nc, ctx, "lw"), hbm, w, ident)
            latent_inputs(nc, Sems(nc, ctx, "li"), hbm, x_res, ident, exponent, latent_scratch)
            q_passes = [(0, w["w1hi"][:]), (0, w["w1lo"][:]), (1, w["w1hi"][:]), (2, w["w2hi"][:]), (2, w["w2lo"][:])]
            latent = Attention("la", float(DN + DR) ** -0.5, 3, P, q_passes, 2, [(0, 0), (0, 1), (1, 0)],
                               w["vohi"], w["volo"], latent_scratch, hbm["rope_latent"])
            attention(nc, Sems(nc, ctx, "la"), latent, x_res, ident, mask)
        if upto >= 2:
            with ExitStack() as layer:
                w = {n: sb(n, [P, KT, NH * HD], F32R, layer) for n in ("wq_hi", "wq_lo")}
                w |= {n: sb(n, [P, NH // 2, D], F32R, layer) for n in ("wo_hi", "wo_lo")}
                ffn_scratch = {"q_src": dram("fq", [B, P, 4, S]), "k": dram("fk", [B, KVH, P, S]),
                               "v": dram("fv", [B, KVH, P, NT, HD]), "x1": dram("x1", [P, TILES, D])}
                with ExitStack() as part:
                    wkv = [sb(n, [P, KT, 2 * KVH * HD], F32R, part) for n in ("wkv_hi", "wkv_lo")]
                    split_ffn_weights(nc, Sems(nc, ctx, "fw"), hbm, w, wkv)
                    ffn_inputs(nc, Sems(nc, ctx, "fi"), hbm, x_res, ident, exponent, wkv, ffn_scratch)
                q_passes = [p for k in range(KT) for p in ((k, w["wq_hi"][:, k, :]), (k, w["wq_lo"][:, k, :]), (2 + k, w["wq_hi"][:, k, :]))]
                views = dict(ffn_scratch, k=ffn_scratch["k"].rearrange("b (r c) p (o s) -> b r c p o s", r=ROUNDS, o=1),
                             v=ffn_scratch["v"].rearrange("b (r c) p j n -> b r c p j n", r=ROUNDS))
                grouped = Attention("ga", float(HD) ** -0.5, 4, HD, q_passes, 1, [(0, 0), (1, 0)],
                                    w["wo_hi"], w["wo_lo"], views, hbm["rope_ffn"])
                attention(nc, Sems(nc, ctx, "ga"), grouped, x_res, ident, mask)
        if upto >= 3:
            h_hi, h_lo = sb("h_hi", [P, KT, B * S], F32R), sb("h_lo", [P, KT, B * S], F32R)
            gates = sb("gates", [P, TILES, E])
            raw13, raw2 = ([sb(f"{n}_{u}", [P, KT, width]) for u in range(2)] for n, width in (("raw13", 2 * H), ("raw2", D)))
            loaded = [ctx.enter_context(nc.semaphore(f"expert_loaded{u}")) for u in range(2)]
            route(nc, Sems(nc, ctx, "rt"), hbm, x_res, ident, exponent, gates, h_hi, h_lo, raw13, raw2, loaded, ffn_scratch)
            experts_dense(nc, Sems(nc, ctx, "ex"), hbm, x_res, gates, h_hi, h_lo, raw13, raw2, loaded, out)
        else:
            stored = ctx.enter_context(nc.semaphore("stored"))
            block = ctx.enter_context(nc.Block())

            @block.sync
            def _(sp):
                sp.dma_start(out.rearrange("b (j p) d -> p (b j) d", p=P), x_res[:]).then_inc(stored, 16)
                sp.wait_ge(stored, 16)


_INS = ["L0_attn_hidden_states", "L0_attn_q_a_w", "L0_attn_q_a_ln_w", "L0_attn_q_b_w", "L0_attn_kv_a_w", "L0_attn_kv_a_ln_w",
        "L0_attn_kv_b_w", "L0_attn_o_w", "L0_ffn_ln_w", "L0_ffn_ff_ln_w", "L0_ffn_wq", "L0_ffn_wk", "L0_ffn_wv", "L0_ffn_wo",
        "L0_ffn_wg", "L0_ffn_w1", "L0_ffn_w3", "L0_ffn_w2"]


def rope_table(base):
    half = np.arange(HALF, dtype=np.float32) / np.float32(HALF)
    angle = np.arange(S, dtype=np.float32)[:, None] * (np.float32(1.0) / np.float32(base) ** half)
    cos, sin = np.cos(angle), np.sin(angle)
    return np.stack([np.concatenate([cos, cos], 1), np.concatenate([-sin, sin], 1)]).astype(np.float32)


def kernel(**inputs):
    import concourse.bacc as bacc
    from concourse.bass_utils import run_bass_kernel_spmd

    nc = bacc.Bacc("TRN2", target_bir_lowering=False, num_devices=1)
    arrays = {n: np.ascontiguousarray(inputs[n]) for n in _INS}
    arrays |= {"rope_latent": rope_table(10000.0), "rope_ffn": rope_table(150000.0)}
    hbm = {n: nc.dram_tensor("in_" + n, a.shape, mybir.dt.from_np(a.dtype), kind="ExternalInput").ap() for n, a in arrays.items()}
    out = nc.dram_tensor("out_x", (B, S, D), F32, kind="ExternalOutput").ap()
    build(nc, hbm, out)
    r = run_bass_kernel_spmd(nc, [{"in_" + n: a for n, a in arrays.items()}], core_ids=[0])
    return r.results[0]["out_x"]
```

```python
from contextlib import ExitStack

import numpy as np

import concourse.bass as bass
from concourse import mybir

F32 = mybir.dt.float32
F32R = mybir.dt.float32r
U32 = mybir.dt.uint32
ALU = mybir.AluOpType
ACT = mybir.ActivationFunctionType
AX_X = mybir.AxisListType.X

P = 128
B, S, D = 4, 512, 256
NT = S // P
TILES = B * NT
KT = D // P
NH = 32
QLR, KVLR, DR, DN, DV = 192, 64, 64, 128, 128
HD, KVH = 64, 8
E, TOPK, H = 16, 4, 256
HALF = 32
BODY = 8
Q_RING = 2
ROUNDS = NH // BODY
N_ROUNDS = B * ROUNDS
MASKED = -1.0e30
BIG = 3.0e38
LN_EPS, MLA_EPS, FFN_EPS = 1e-5, 1e-6, 1e-5

P_OFF = [0, 128, 384, 768]
P_ALL = 1280
SCORE_UNITS = [[(3, 0)], [(0, 0), (2, 128)], [(1, 0)]]
SUM_COL = {3: 0, 0: 1, 2: 2, 1: 3}
PT_OFF = [0, 512, 1024, 896]
TRANS_UNITS = [[(0, 0)], [(1, 0), (3, 384)], [(2, 0)]]


def wait_alone(eng, sem, value, passed):
    eng.wait_ge(sem, value)
    eng.sem_inc(passed, 1)


class Sems:

    def __init__(self, nc, ctx, prefix):
        self.nc, self.ctx, self.prefix = nc, ctx, prefix

    def __call__(self, name):
        return self.ctx.enter_context(self.nc.semaphore(f"{self.prefix}_{name}"))


def prepare_latent_weights(nc, sems, hbm, w, ident, x_res):
    with ExitStack() as ctx:
        def sb(name, shape, dt=F32):
            return ctx.enter_context(nc.sbuf_tensor("lw_" + name, shape, dt))

        def psum(name):
            return ctx.enter_context(nc.psum_tensor("lw_" + name, [P, 512], F32))

        U = 8
        G = 4
        L = 2
        TRIPS = NH // 2 // U
        raw_q1 = [sb(f"raw_q1{n}", [P, L, 2, DN + DR]) for n in range(U // L)]
        raw_q2 = [sb(f"raw_q2{n}", [P, L, 2, DN + DR]) for n in range(U // L)]
        raw_kv = [sb(f"raw_kv{n}", [KVLR, L, 2, DN + DV]) for n in range(U // L)]
        raw_o = [sb(f"raw_o{n}", [P, L, 2, D]) for n in range(U // L)]
        q_t = [sb(f"q_t{u}", [P, 2, 2, P]) for u in range(G)]
        kv_t = [sb(f"kv_t{u}", [P, 2, 2, KVLR]) for u in range(G)]
        ps_q = [psum(f"ps_q{u}") for u in range(G)]
        ps_kv = [psum(f"ps_kv{u}") for u in range(G)]

        raw_loaded, x_loaded = [sems(f"raw_loaded{n}") for n in range(U // L)], sems("x_loaded")
        turned = sems("turned")
        q_turned = sems("q_turned")
        kv_turned = sems("kv_turned")
        multiplied = sems("multiplied")
        hi_done = sems("hi_done")
        lo_done = sems("lo_done")

        wq_dram = hbm["L0_attn_q_b_w"].rearrange("r (i k m) -> i k r m", i=TRIPS, k=U // L)
        kvb_dram = hbm["L0_attn_kv_b_w"].rearrange("r (i k m) -> i k r m", i=TRIPS, k=U // L)
        o_dram = hbm["L0_attn_o_w"].rearrange("(i k h p) n -> i k p h n", i=TRIPS, k=U // L, p=P)

        def view(t):
            return t[:].rearrange("p (i u h n) -> p i u h n", i=TRIPS, u=U, h=2)

        w1hi, w1lo, w2hi, w2lo = (view(w[n]) for n in ("w1hi", "w1lo", "w2hi", "w2lo"))
        vohi, volo = (w[n][:].rearrange("p (i u) n -> p i u n", u=U) for n in ("vohi", "volo"))
        block = ctx.enter_context(nc.Block())

        @block.sync
        def _(sp):
            with sp.Fori(0, TRIPS) as i:
                done = sp.snap(i * U)
                for n in range(U // L):
                    sp.wait_ge(lo_done, done + L * (n + 1))
                    q1, q2, kv = (t[n][:].rearrange("p l h n -> p (l h n)") for t in (raw_q1, raw_q2, raw_kv))
                    sp.dma_start(q1, wq_dram[i, n, 0:P]).then_inc(raw_loaded[n], 16)
                    sp.dma_start(q2[0:64], wq_dram[i, n, P:QLR]).then_inc(raw_loaded[n], 16)
                    sp.dma_start(q2[64:P], wq_dram[i, n, P:QLR]).then_inc(raw_loaded[n], 16)
                    sp.dma_start(kv, kvb_dram[i, n]).then_inc(raw_loaded[n], 16)
                    sp.dma_start(raw_o[n][:].rearrange("p l h n -> p (l h) n"), o_dram[i, n]).then_inc(raw_loaded[n], 16)
            sp.dma_start(x_res[:], hbm["L0_attn_hidden_states"].rearrange("b (j p) d -> p (b j) d", p=P)).then_inc(x_loaded, 16)
            sp.wait_ge(x_loaded, 16)

        @block.tensor
        def _(pe):
            with pe.Fori(0, TRIPS) as i:
                base = pe.snap(i * U)
                loads = pe.snap(i * 80)
                for g in range(0, U, G):
                    for u in range(g, g + G):
                        n, m, c = u // L, u % L, u % G
                        if m == 0:
                            pe.wait_ge(raw_loaded[n], loads + 80)
                        pe.wait_ge(lo_done, base + (u + 1 + U - G))
                        for h in range(2):
                            nc.tensor.transpose(ps_q[c][:, 256 * h:256 * h + P], raw_q1[n][:, m, h, 0:DN], ident[:])
                            nc.tensor.transpose(ps_q[c][:, 256 * h + P:256 * h + 256], raw_q2[n][:, m, h, 0:DN], ident[:])
                            nc.tensor.transpose(ps_kv[c][:, 128 * h:128 * h + 64], raw_kv[n][:, m, h, 0:DN], ident[0:64, 0:64])
                            last = nc.tensor.transpose(ps_kv[c][:, 128 * h + 64:128 * h + 128], raw_kv[n][:, m, h, DN:DN + DV],
                                                       ident[0:64, 0:64])
                        last.then_inc(turned, 1)
                    for u in range(g, g + G):
                        n, m, c = u // L, u % L, u % G
                        pe.wait_ge(q_turned, base + (u + 1))
                        pe.wait_ge(kv_turned, base + (u + 1))
                        for h in range(2):
                            for r in range(2):
                                nc.tensor.matmul(ps_kv[c][:, 256 + 128 * h + 64 * r:256 + 128 * h + 64 * r + 64], q_t[c][:, h, r, :],
                                                 kv_t[c][:, h, 0, :], start=True, stop=True)
                        for h in range(2):
                            last = nc.tensor.matmul(ps_q[c][64 * h:64 * h + 64, 0:D], kv_t[c][:, h, 1, :], raw_o[n][:, m, h, :],
                                                    start=True, stop=True)
                        last.then_inc(multiplied, 1)

        @block.scalar
        def _(act):
            with act.Fori(0, TRIPS) as i:
                base = act.snap(i * U)
                for g in range(0, U, G):
                    for u in range(g, g + G):
                        act.wait_ge(turned, base + (u + 1))
                        nc.scalar.activation(q_t[u % G][:].rearrange("p h r n -> p (h r n)"), ps_q[u % G][:], ACT.Copy).then_inc(q_turned, 1)
                    for u in range(g, g + G):
                        n, m, c = u // L, u % L, u % G
                        act.wait_ge(multiplied, base + (u + 1))
                        pw = ps_kv[c][:, 256:512].rearrange("p (h r c) -> p h r c", h=2, r=2)
                        nc.scalar.activation(w1hi[:, i, u, :, 0:64], pw[:, :, 0, :], ACT.Copy)
                        nc.scalar.activation(w2hi[:, i, u, :, 0:64], pw[:, :, 1, :], ACT.Copy)
                        nc.scalar.activation(w1hi[:, i, u, :, 64:128], raw_q1[n][:, m, :, DN:DN + DR], ACT.Copy)
                        nc.scalar.activation(w2hi[:, i, u, :, 64:128], raw_q2[n][:, m, :, DN:DN + DR], ACT.Copy)
                        nc.scalar.activation(vohi[:, i, u, :], ps_q[c][:, 0:D], ACT.Copy).then_inc(hi_done, 1)

        @block.vector
        def _(dve):
            dve.sem_inc(lo_done, U)

            def split(lo, x, hi):
                return nc.vector.tensor_tensor(lo, x, hi.bitcast(F32), ALU.subtract)

            with dve.Fori(0, TRIPS) as i:
                base = dve.snap(i * U)
                for g in range(0, U, G):
                    for u in range(g, g + G):
                        dve.wait_ge(turned, base + (u + 1))
                        nc.vector.tensor_copy(kv_t[u % G][:].rearrange("p h r n -> p (h r n)"), ps_kv[u % G][:, 0:256]).then_inc(kv_turned, 1)
                    for u in range(g, g + G):
                        n, m, c = u // L, u % L, u % G
                        dve.wait_ge(hi_done, base + (u + 1))
                        pw = ps_kv[c][:, 256:512].rearrange("p (h r c) -> p h r c", h=2, r=2)
                        split(w1lo[:, i, u, :, 0:64], pw[:, :, 0, :], w1hi[:, i, u, :, 0:64])
                        split(w2lo[:, i, u, :, 0:64], pw[:, :, 1, :], w2hi[:, i, u, :, 0:64])
                        split(w1lo[:, i, u, :, 64:128], raw_q1[n][:, m, :, DN:DN + DR], w1hi[:, i, u, :, 64:128])
                        split(w2lo[:, i, u, :, 64:128], raw_q2[n][:, m, :, DN:DN + DR], w2hi[:, i, u, :, 64:128])
                        split(volo[:, i, u, :], ps_q[c][:, 0:D], vohi[:, i, u, :]).then_inc(lo_done, 1)


def start_constants(nc, sems, ident, mask, exponent):
    with ExitStack() as ctx:
        zeroed, made = sems("zeroed"), sems("made")
        block = ctx.enter_context(nc.Block())

        @block.gpsimd
        def _(pool):
            nc.gpsimd.memset(ident[:], 0.0)
            nc.gpsimd.memset(exponent[:], -0.5)
            nc.gpsimd.memset(mask[:], 0.0).then_inc(zeroed, 1)
            pool.wait_ge(zeroed, 1)
            nc.gpsimd.affine_select(out=ident[:], in_=ident[:], compare_op=ALU.not_equal, fill=1.0, base=0,
                                    pattern=[[-1, P]], channel_multiplier=1)
            nc.gpsimd.affine_select(out=mask[:, 384:512], in_=mask[:, 384:512], compare_op=ALU.is_ge, fill=MASKED, base=0,
                                    pattern=[[-1, P]], channel_multiplier=1).then_inc(made, 1)
            pool.wait_ge(made, 1)


def latent_inputs(nc, sems, hbm, x_res, ident, exponent, scratch):
    with ExitStack() as ctx:
        def sb(name, shape, dt=F32):
            return ctx.enter_context(nc.sbuf_tensor("li_" + name, shape, dt))

        W = QLR + KVLR + DR
        wa = sb("wa", [P, KT, W])
        wa_hi, wa_lo = sb("wa_hi", [P, KT, W], F32R), sb("wa_lo", [P, KT, W], F32R)
        ln_w = sb("ln_w", [P, QLR + KVLR])
        rope = sb("rope", [P, 2, NT, DR])
        stats, mv = sb("stats", [P, NT, 6]), sb("mv", [P, NT, 2])
        var_eps, rstd = sb("var_eps", [P, NT]), sb("rstd", [P, NT])
        xn = sb("xn", [P, NT, D])
        xt_hi, xt_lo = sb("xt_hi", [P, NT, D], F32R), sb("xt_lo", [P, NT, D], F32R)
        square = sb("square", [P, NT, QLR + KVLR])
        ms, ms_eps, rms = sb("ms", [P, NT, 2]), sb("ms_eps", [P, NT, 2]), sb("rms", [P, NT, 2])
        qn, kv = sb("qn", [P, NT, 256]), sb("kv", [P, NT, P])
        rot_a, rot_b = sb("rot_a", [P, NT, DR]), sb("rot_b", [P, NT, DR])
        t_hi, t_lo = sb("t_hi", [P, 3, NT, P], F32R), sb("t_lo", [P, 3, NT, P], F32R)
        ps_t = [ctx.enter_context(nc.psum_tensor(f"li_ps_t{u}", [P, 512], F32)) for u in range(NT)]
        ps_p = [ctx.enter_context(nc.psum_tensor(f"li_ps_p{u}", [P, 512], F32)) for u in range(NT)]

        loaded, w_hi, w_lo = sems("loaded"), sems("w_hi"), sems("w_lo")
        bn, mean_var, eps_added, rstd_done, xn_done = (sems(n) for n in ("bn", "mean_var", "eps_added", "rstd_done", "xn_done"))
        xt_turned, xt_hi_done, xt_lo_done, projected = (sems(n) for n in ("xt_turned", "xt_hi_done", "xt_lo_done", "projected"))
        squared, ms_eps_added, rms_done, rotated, normed = (
            sems(n) for n in ("squared", "ms_eps_added", "rms_done", "rotated", "normed"))
        turned, hi_done, lo_done, stored, passed = (sems(n) for n in ("turned", "hi_done", "lo_done", "stored", "passed"))
        block = ctx.enter_context(nc.Block())
        N_LOADS, N_STORES = 6, 7

        @block.sync
        def _(sp):
            sp.dma_start(wa[:, :, 0:QLR], hbm["L0_attn_q_a_w"].rearrange("(k p) n -> p k n", p=P)).then_inc(loaded, 16)
            sp.dma_start(wa[:, :, QLR:W], hbm["L0_attn_kv_a_w"].rearrange("(k p) n -> p k n", p=P)).then_inc(loaded, 16)
            sp.dma_start(ln_w[:, 0:QLR], hbm["L0_attn_q_a_ln_w"].rearrange("(o n) -> o n", o=1).to_broadcast([P, QLR])).then_inc(loaded, 16)
            sp.dma_start(ln_w[:, QLR:], hbm["L0_attn_kv_a_ln_w"].rearrange("(o n) -> o n", o=1).to_broadcast([P, KVLR])).then_inc(loaded, 16)
            for k in range(2):
                sp.dma_start(rope[:, k], hbm["rope_latent"][k].rearrange("(j p) n -> p j n", p=P)).then_inc(loaded, 16)
            with sp.Fori(0, B) as b:
                done = sp.snap(b * NT)
                sp.wait_ge(hi_done, done + NT)
                flat = "p j n -> p (j n)"
                qs, kk = scratch["q_src"][b], scratch["k"][b]
                sp.dma_start(qs[:, 0], t_hi[:, 0].bitcast(F32).rearrange(flat)).then_inc(stored, 16)
                sp.dma_start(qs[0:64, 2], t_hi[0:64, 1].bitcast(F32).rearrange(flat)).then_inc(stored, 16)
                sp.dma_start(kk[:, 0], t_hi[:, 2].bitcast(F32).rearrange(flat)).then_inc(stored, 16)
                sp.wait_ge(lo_done, done + 2 * NT)
                sp.dma_start(qs[:, 1], t_lo[:, 0].bitcast(F32).rearrange(flat)).then_inc(stored, 16)
                sp.dma_start(qs[64:P, 2], t_lo[64:P, 1].bitcast(F32).rearrange(flat)).then_inc(stored, 16)
                sp.dma_start(kk[:, 1], t_lo[:, 2].bitcast(F32).rearrange(flat)).then_inc(stored, 16)
                sp.dma_start(scratch["v"][b], kv[:, :, 0:KVLR]).then_inc(stored, 16)
            sp.wait_ge(stored, 16 * N_STORES * (B + 1))

        @block.gpsimd
        def _(pool):
            pool.sem_inc(stored, 16 * N_STORES)

            def layer_norm(base):
                for u in range(NT):
                    wait_alone(pool, mean_var, base + (u + 1), passed)
                    nc.gpsimd.tensor_scalar(var_eps[:, u:u + 1], mv[:, u, 1:2], LN_EPS, 1.0, ALU.add, ALU.mult).then_inc(eps_added, 1)
                    pool.wait_ge(eps_added, base + (u + 1))
                    nc.gpsimd.tensor_tensor(rstd[:, u:u + 1], var_eps[:, u:u + 1], exponent[:], ALU.pow).then_inc(rstd_done, 1)

            def rms_norms(base):
                for u in range(NT):
                    wait_alone(pool, squared, base + (u + 1), passed)
                    nc.gpsimd.tensor_scalar(ms_eps[:, u, :], ms[:, u, :], MLA_EPS, 1.0, ALU.add, ALU.mult).then_inc(ms_eps_added, 1)
                    pool.wait_ge(ms_eps_added, base + (u + 1))
                    nc.gpsimd.tensor_tensor(rms[:, u, :], ms_eps[:, u, :], exponent[:].to_broadcast([P, 2]), ALU.pow).then_inc(rms_done, 1)

            layer_norm(0)
            with pool.Fori(0, B - 1) as b:
                base = pool.snap(b * NT)
                layer_norm(base + NT)
                rms_norms(base)
            rms_norms((B - 1) * NT)

        @block.tensor
        def _(pe):
            pe.wait_ge(w_lo, 1)
            with pe.Fori(0, B) as b:
                base = pe.snap(b * NT)
                for u in range(NT):
                    pe.wait_ge(xn_done, base + (u + 1))
                    pe.wait_ge(lo_done, base + (u + 1))
                    for k in range(KT):
                        last = nc.tensor.transpose(ps_t[u][:, P * k:P * k + P], xn[:, u, P * k:P * k + P], ident[:])
                    last.then_inc(xt_turned, 1)
                for u in range(NT):
                    pe.wait_ge(xt_lo_done, base + (u + 1))
                    n = 0
                    for k in range(KT):
                        for x, wt in ((xt_hi, wa_hi), (xt_hi, wa_lo), (xt_lo, wa_hi)):
                            last = nc.tensor.matmul(ps_p[u][:, 0:W], x[:, u, P * k:P * k + P], wt[:, k, :], start=(n == 0), stop=(n == 5))
                            n += 1
                    last.then_inc(projected, 1)
                for u in range(NT):
                    pe.wait_ge(normed, base + (u + 1))
                    nc.tensor.transpose(ps_t[u][:, 0:P], qn[:, u, 0:P], ident[:])
                    nc.tensor.transpose(ps_t[u][:, P:2 * P], qn[:, u, P:2 * P], ident[:])
                    nc.tensor.transpose(ps_t[u][:, 2 * P:3 * P], kv[:, u, :], ident[:]).then_inc(turned, 1)

        @block.scalar
        def _(act):
            act.wait_ge(loaded, 16 * N_LOADS)
            nc.scalar.activation(wa_hi[:], wa[:], ACT.Copy).then_inc(w_hi, 1)
            with act.Fori(0, B) as b:
                base = act.snap(b * NT)
                stores = act.snap(b * (16 * N_STORES))
                for u in range(NT):
                    act.wait_ge(xt_turned, base + (u + 1))
                    nc.scalar.activation(xt_hi[:, u, :], ps_t[u][:, 0:D], ACT.Copy).then_inc(xt_hi_done, 1)
                for u in range(NT):
                    act.wait_ge(projected, base + (u + 1))
                    nc.scalar.activation(square[:, u, 0:QLR], ps_p[u][:, 0:QLR], ACT.Square, scale=float(QLR) ** -0.5,
                                         accum_out=ms[:, u, 0:1])
                    nc.scalar.activation(square[:, u, QLR:], ps_p[u][:, QLR:QLR + KVLR], ACT.Square, scale=float(KVLR) ** -0.5,
                                         accum_out=ms[:, u, 1:2]).then_inc(squared, 1)
                act.wait_ge(stored, stores + 16 * N_STORES)
                for u in range(NT):
                    act.wait_ge(turned, base + (u + 1))
                    nc.scalar.activation(t_hi[:, :, u, :], ps_t[u][:, 0:3 * P].rearrange("p (k n) -> p k n", k=3), ACT.Copy)\
                        .then_inc(hi_done, 1)

        @block.vector
        def _(dve):
            dve.wait_ge(w_hi, 1)
            nc.vector.tensor_tensor(wa_lo[:], wa[:], wa_hi[:].bitcast(F32), ALU.subtract).then_inc(w_lo, 1)
            dve.sem_inc(lo_done, NT)
            xb = x_res[:].rearrange("p (b j) d -> p b j d", b=B)

            def statistics(b, base):
                for u in range(NT):
                    nc.vector.bn_stats(stats[:, u, :], xb[:, b, u, :]).then_inc(bn, 1)
                for u in range(NT):
                    wait_alone(dve, bn, base + (u + 1), passed)
                    nc.vector.bn_aggr(mv[:, u, :], stats[:, u, :]).then_inc(mean_var, 1)

            def layer_norm(b, base):
                for u in range(NT):
                    dve.wait_ge(rstd_done, base + (u + 1))
                    nc.vector.tensor_scalar(xn[:, u, :], xb[:, b, u, :], mv[:, u, 0:1], rstd[:, u:u + 1], ALU.subtract, ALU.mult)\
                        .then_inc(xn_done, 1)

            def batch(b, base, stores, more):
                for u in range(NT):
                    dve.wait_ge(xt_hi_done, base + (u + 1))
                    nc.vector.tensor_tensor(xt_lo[:, u, :], ps_t[u][:, 0:D], xt_hi[:, u, :].bitcast(F32), ALU.subtract)\
                        .then_inc(xt_lo_done, 1)
                if more:
                    statistics(b + 1, base + NT)
                    layer_norm(b + 1, base + NT)
                dve.wait_ge(stored, stores + 16 * N_STORES)
                for u in range(NT):
                    dve.wait_ge(rms_done, base + (u + 1))
                    q, c, kr = ps_p[u][:, 0:QLR], ps_p[u][:, QLR:QLR + KVLR], ps_p[u][:, QLR + KVLR:W]
                    nc.vector.tensor_tensor(rot_a[:, u, :], kr, rope[:, 0, u, :], ALU.mult)
                    nc.vector.tensor_tensor(rot_b[:, u, :].rearrange("p (t c) -> p t c", t=2),
                                            kr.rearrange("p (t c) -> p t c", t=2)[:, ::-1, :],
                                            rope[:, 1, u, :].rearrange("p (t c) -> p t c", t=2), ALU.mult).then_inc(rotated, 1)
                    nc.vector.scalar_tensor_tensor(out=qn[:, u, 0:QLR], in0=q, scalar=rms[:, u, 0:1], in1=ln_w[:, 0:QLR],
                                                   op0=ALU.mult, op1=ALU.mult)
                    nc.vector.scalar_tensor_tensor(out=qn[:, u, QLR:2 * P], in0=q[:, P:QLR], scalar=rms[:, u, 0:1],
                                                   in1=ln_w[:, P:QLR], op0=ALU.mult, op1=ALU.mult)
                    nc.vector.scalar_tensor_tensor(out=kv[:, u, 0:KVLR], in0=c, scalar=rms[:, u, 1:2],
                                                   in1=ln_w[:, QLR:QLR + KVLR], op0=ALU.mult, op1=ALU.mult)
                    dve.wait_ge(rotated, base + (u + 1))
                    nc.vector.tensor_tensor(kv[:, u, KVLR:P], rot_a[:, u, :], rot_b[:, u, :], ALU.add).then_inc(normed, 1)
                for u in range(NT):
                    dve.wait_ge(hi_done, base + (u + 1))
                    nc.vector.tensor_tensor(t_lo[:, :, u, :], ps_t[u][:, 0:3 * P].rearrange("p (k n) -> p k n", k=3),
                                            t_hi[:, :, u, :].bitcast(F32), ALU.subtract).then_inc(lo_done, 1)

            statistics(0, 0)
            layer_norm(0, 0)
            with dve.Fori(0, B - 1) as b:
                batch(b, dve.snap(b * NT), dve.snap(b * (16 * N_STORES)), True)
            batch(B - 1, (B - 1) * NT, (B - 1) * 16 * N_STORES, False)


class Slot:

    def __init__(self, k, first=False, last=False):
        self.scores = not (last and k >= BODY)
        self.values = not (first and k == BODY) and not (last and k > BODY)
        self.unit = k - 3 if not first and not last else None
        self.turned_unit = k - 4 if not first and (not last or k == 3) else None
        self.pair = (k - 3) // 2 if k % 2 and not first else None
        self.out = {6: 0, 10: 1}.get(k) if not first else None


SLOTS = range(3, BODY + 3)
FIRST_SLOTS = range(BODY, BODY + 3)


class Attention:

    def __init__(self, name, scale, q_slots, width, q_passes, k_slots, s_passes, out_hi, out_lo, scratch, rope):
        self.name, self.scale, self.q_slots, self.width = name, scale, q_slots, width
        self.q_passes, self.k_slots, self.s_passes = q_passes, k_slots, s_passes
        self.out_hi, self.out_lo, self.scratch, self.rope = out_hi, out_lo, scratch, rope


def attention(nc, sems, a, x_res, ident, mask):
    latent = a.width == 128
    with ExitStack() as ctx:
        def sb(name, shape, dt=F32):
            return ctx.enter_context(nc.sbuf_tensor(f"{a.name}_{name}", shape, dt))

        def psum(name):
            return ctx.enter_context(nc.psum_tensor(f"{a.name}_{name}", [P, 512], F32))

        q_src = sb("q_src", [P, a.q_slots, S], F32R)
        keys = [sb(f"keys{c}", [P, a.k_slots, S], F32R) for c in range(2)]
        values = [sb(f"values{c}", [P, NT, HD]) for c in range(2)]
        qt_hi, qt_lo = sb("qt_hi", [P, BODY, S], F32R), sb("qt_lo", [P, BODY, S], F32R)
        q_tok = [sb(f"q_tok{r}", [P, 4, P]) for r in range(Q_RING)]
        rot_a = [sb(f"rot_a{r}", [P, 4, DR]) for r in range(2)]
        rot_b = [sb(f"rot_b{r}", [P, 4, DR]) for r in range(2)]
        rope = sb("rope", [P, 2, NT, DR])
        probs = [sb(f"probs{r}", [P, P_ALL]) for r in range(2)]
        probs_t = [sb(f"probs_t{r}", [P, P_ALL]) for r in range(2)]
        neg_max = [sb(f"neg_max{r}", [P, NT]) for r in range(2)]
        total = [sb(f"total{r}", [P, NT]) for r in range(2)]
        inverse = [sb(f"inverse{r}", [P, NT]) for r in range(2)]
        ot_hi = [sb(f"ot_hi{r}", [P, S], F32R) for r in range(2)]
        ot_lo = [sb(f"ot_lo{r}", [P, S], F32R) for r in range(2)]
        ps_s = [psum(f"ps_s{r}") for r in range(2)]
        ps_t = [psum(f"ps_t{r}") for r in range(2)]
        ps_v, ps_q, ps_qt, ps_o = psum("ps_v"), psum("ps_q"), psum("ps_qt"), psum("ps_o")

        rope_loaded, q_src_loaded, passed = sems("rope_loaded"), sems("q_src_loaded"), sems("passed")
        k_loaded = [sems(f"k_loaded{c}") for c in range(2)]
        v_loaded = [sems(f"v_loaded{c}") for c in range(2)]
        scored, masked = sems("scored"), sems("masked")
        exped, inverted, scaled = sems("exped"), sems("inverted"), sems("scaled")
        turned, t_act, t_dve = sems("turned"), sems("t_act"), sems("t_dve")
        valued, o_hi_done, o_lo_done = sems("valued"), sems("o_hi_done"), sems("o_lo_done")
        out_done, added = sems("out_done"), sems("added")
        q_done, rope_read, nope_done, rope_added = sems("q_done"), sems("rope_read"), sems("nope_done"), sems("rope_added")
        q_turned, q_hi_done, q_lo_done = sems("q_turned"), sems("q_hi_done"), sems("q_lo_done")
        q_bank_read = nope_done if latent else rope_read
        block = ctx.enter_context(nc.Block())

        q_weights = [(slot, wt.rearrange("p (r c n) -> p r c n", r=ROUNDS, c=2)) for slot, wt in a.q_passes]
        out_w = [t.rearrange("p (r m) n -> p r m n", r=ROUNDS) for t in (a.out_hi, a.out_lo)]
        UQ = BODY

        def unit_banks(u, unit):
            return (ps_o, ps_v) if isinstance(unit, int) and unit == 0 and u % 2 else (ps_q, ps_qt)

        def wait_q_tok(eng, u, unit):
            if u >= Q_RING or not isinstance(unit, int):
                eng.wait_ge(q_turned, unit + (u - Q_RING + 1))

        @block.sync
        def _(sp):
            sp.dma_start(q_src[:].bitcast(F32), a.scratch["q_src"][0]).then_inc(q_src_loaded, 16)
            for k in range(2):
                sp.dma_start(rope[:, k], a.rope[k].rearrange("(j p) n -> p j n", p=P)).then_inc(rope_loaded, 16)

            def load_kv(c, b, r):
                kk, vv = (a.scratch["k"][b], a.scratch["v"][b]) if latent else \
                    (a.scratch["k"][b, r, c], a.scratch["v"][b, r, c])
                return kk, vv

            for c in range(2):
                kk, vv = load_kv(c, 0, 0)
                sp.dma_start(keys[c][:].bitcast(F32), kk).then_inc(k_loaded[c], 16)
                sp.dma_start(values[c][:], vv).then_inc(v_loaded[c], 16)

            def reload(done, b, r):
                for c in range(2):
                    kk, vv = load_kv(c, b, r)
                    sp.wait_ge(scored, done * 3 + 12 * (c + 1))
                    sp.dma_start(keys[c][:].bitcast(F32), kk).then_inc(k_loaded[c], 16)
                    sp.wait_ge(valued, done + 4 * (c + 1))
                    sp.dma_start(values[c][:], vv).then_inc(v_loaded[c], 16)

            with sp.Fori(0, B) as b:
                next_b = sp.snap((b + 1) & (B - 1))
                with sp.Fori(0, ROUNDS - 1) as r:
                    reload(sp.snap(b * (BODY * ROUNDS) + r * BODY), b, sp.snap(r + 1))
                done = sp.snap(b * (BODY * ROUNDS))
                wait_alone(sp, q_done, done + BODY * ROUNDS, passed)
                sp.dma_start(q_src[:].bitcast(F32), a.scratch["q_src"][next_b]).then_inc(q_src_loaded, 16)
                reload(sp.snap(b * (BODY * ROUNDS) + (ROUNDS - 1) * BODY), next_b, 0)
            sp.wait_ge(q_src_loaded, 16 * (B + 1))
            for c in range(2):
                sp.wait_ge(k_loaded[c], 16 * (N_ROUNDS + 1))
                sp.wait_ge(v_loaded[c], 16 * (N_ROUNDS + 1))

        @block.gpsimd
        def _(pool):
            pool.sem_inc(rope_added, 2)

            def rope_add(u, unit):
                pool.wait_ge(rope_read, unit + (u + 1) + (0 if latent else 1))
                wait_q_tok(pool, u, unit)
                if latent:
                    last = nc.gpsimd.tensor_tensor(q_tok[u % Q_RING][:, :, 64:P], rot_a[u % 2][:], rot_b[u % 2][:], ALU.add)
                else:
                    def twice(t):
                        return t[:].rearrange("p h (o n) -> p h o n", o=1).to_broadcast([P, 4, 2, HD])
                    last = nc.gpsimd.tensor_tensor(q_tok[u % Q_RING][:].rearrange("p h (o n) -> p h o n", o=2),
                                                   twice(rot_a[u % 2]), twice(rot_b[u % 2]), ALU.add)
                last.then_inc(rope_added, 1)

            for u in range(UQ):
                rope_add(u, 0)

            def scale(k, heads2):
                for part, tiles in enumerate(((3, 0), (2, 1))):
                    wait_alone(pool, inverted, heads2 + (2 * k + part + 1), passed)
                    for q in tiles:
                        c = SUM_COL[q]
                        pr = probs[k % 2][:, P_OFF[q]:P_OFF[q] + P * (q + 1)]
                        last = nc.gpsimd.tensor_scalar(pr, pr, inverse[k % 2][:, c:c + 1], 1.0, ALU.mult, ALU.mult)
                last.then_inc(scaled, 1)

            def slot(s, k, heads2, unit):
                if s.scores:
                    scale(k, heads2)
                if s.unit is not None:
                    rope_add(s.unit, unit)

            for k in FIRST_SLOTS:
                slot(Slot(k, first=True), k, -2 * BODY, None)
            with pool.Fori(0, N_ROUNDS - 1) as i:
                unit = pool.snap(i * UQ + UQ)
                heads2 = pool.snap(i * (2 * BODY))
                for k in SLOTS:
                    slot(Slot(k), k, heads2, unit)
            for k in SLOTS:
                slot(Slot(k, last=True), k, 2 * BODY * (N_ROUNDS - 1), None)

        @block.tensor
        def _(pe):
            def project(u, unit, nxt, loads):
                if loads is not None:
                    pe.wait_ge(q_src_loaded, loads)
                if not isinstance(unit, int):
                    pe.wait_ge(q_bank_read, unit + (u + 1))
                elif u >= 2:
                    pe.wait_ge(q_bank_read, u)
                bank, _ = unit_banks(u, unit)
                for n, (slot, wt) in enumerate(q_weights):
                    last = nc.tensor.matmul(bank[:, 0:4 * a.width], q_src[:, slot, P * (u % 4):P * (u % 4) + P],
                                            wt[:, nxt, u // 4, :], start=(n == 0), stop=(n == len(q_weights) - 1))
                last.then_inc(q_done, 1)

            def turn_queries(u, unit):
                pe.wait_ge(rope_added, unit + (u + 1) + 2)
                if latent:
                    pe.wait_ge(nope_done, unit + (u + 1) + 1)
                if not isinstance(unit, int) or unit > 0:
                    pe.wait_ge(q_lo_done, unit + (u + 1))
                elif u >= 2:
                    pe.wait_ge(q_lo_done, u)
                _, bank = unit_banks(u, unit)
                for h in range(4):
                    last = nc.tensor.transpose(bank[:, P * h:P * h + P], q_tok[u % Q_RING][:, h, :], ident[:])
                last.then_inc(q_turned, 1)

            def scores(k, n, heads, heads4, rounds16):
                if n == 0 and k % 4 == 0:
                    pe.wait_ge(q_lo_done, heads + (k + 4 + 1))
                    pe.wait_ge(k_loaded[k // 4 % 2], rounds16 + 16 * (k // BODY + 1))
                pe.wait_ge(masked, heads4 + (4 * k + 3 + n))
                for q, col in SCORE_UNITS[n]:
                    nk = P * (q + 1)
                    for m, (which, slot) in enumerate(a.s_passes):
                        qt = (qt_hi, qt_lo)[which]
                        last = nc.tensor.matmul(ps_s[(3 * k + n) % 2][:, col:col + nk], qt[:, k % BODY, P * q:P * q + P],
                                                keys[k // 4 % 2][:, slot, 0:nk], start=(m == 0), stop=(m == len(a.s_passes) - 1))
                last.then_inc(scored, 1)

            def turn_probs(k, n, heads, heads2):
                if n == 0:
                    pe.wait_ge(scaled, heads + (k + 1))
                if n == 0:
                    pe.wait_ge(t_dve, heads + (k + 1))
                else:
                    pe.wait_ge(t_act, heads2 + (2 * k + n))
                for j, col in TRANS_UNITS[n]:
                    for q in range(j, NT):
                        last = nc.tensor.transpose(ps_t[(3 * k + n) % 2][:, col + P * (q - j):col + P * (q - j) + P],
                                                   probs[k % 2][:, P_OFF[q] + P * j:P_OFF[q] + P * j + P], ident[:])
                last.then_inc(turned, 1)

            def apply(k, heads, heads2, pairs, rounds16):
                if k % 4 == 0:
                    pe.wait_ge(v_loaded[k // 4 % 2], rounds16 + 16 * (k // BODY + 1))
                if k % 2 == 0:
                    pe.wait_ge(o_lo_done, pairs + (k // 2 + 1))
                pe.wait_ge(t_act, heads2 + (2 * k + 3))
                pe.wait_ge(t_dve, heads + (k + 2))
                row = 64 * (k % 2)
                for j in range(NT):
                    n = S - P * j
                    last = nc.tensor.matmul(ps_v[row:row + 64, P * j:S], values[k // 4 % 2][:, j, :],
                                            probs_t[k % 2][:, PT_OFF[j]:PT_OFF[j] + n], start=(j == 0), stop=(j == NT - 1))
                last.then_inc(valued, 1)

            def project_out(c, half, r, pairs):
                pe.wait_ge(o_lo_done, pairs + (2 * c + 2 + 1))
                pe.wait_ge(added, pairs + (2 * c + half + 1))
                for t in range(2):
                    j = 2 * half + t
                    n = 0
                    for e in range(2):
                        for ot, wt in ((ot_hi, 0), (ot_hi, 1), (ot_lo, 0)):
                            last = nc.tensor.matmul(ps_o[:, D * t:D * t + D], ot[e][:, P * j:P * j + P],
                                                    out_w[wt][:, r, 2 * c + e, :], start=(n == 0), stop=(n == 5))
                            n += 1
                last.then_inc(out_done, 1)

            for u in range(UQ):
                project(u, 0, 0, 16 if u == 0 else None)
                if u:
                    turn_queries(u - 1, 0)

            def slot(s, k, r, nxt, loads, unit, heads, heads2, heads4, pairs, rounds16):
                if s.scores:
                    scores(k, 0, heads, heads4, rounds16)
                    scores(k, 1, heads, heads4, rounds16)
                if s.values:
                    turn_probs(k - 1, 0, heads, heads2)
                if s.out is not None:
                    project_out(s.out, 0, r, pairs)
                if s.scores:
                    scores(k, 2, heads, heads4, rounds16)
                if s.values:
                    turn_probs(k - 1, 1, heads, heads2)
                if s.turned_unit is not None:
                    turn_queries(s.turned_unit, unit)
                if s.values:
                    turn_probs(k - 1, 2, heads, heads2)
                if s.unit is not None:
                    project(s.unit, unit, nxt, loads if s.unit == 0 else None)
                if s.out is not None:
                    project_out(s.out, 1, r, pairs)
                if s.values:
                    apply(k - 1, heads, heads2, pairs, rounds16)

            for k in FIRST_SLOTS:
                if k == BODY + 1:
                    pe.wait_ge(q_lo_done, UQ)
                slot(Slot(k, first=True), k, None, None, None, None, -BODY, -2 * BODY, -4 * BODY, -BODY // 2, -16)
            with pe.Fori(0, N_ROUNDS - 1) as i:
                r = pe.snap(i & (ROUNDS - 1))
                nxt = pe.snap((i + 1) & (ROUNDS - 1))
                loads = pe.snap((((i + 1) >> 2) + 1) * 16)
                heads = pe.snap(i * BODY)
                unit = pe.snap(i * UQ + UQ)
                heads2 = pe.snap(i * (2 * BODY))
                heads4 = pe.snap(i * (4 * BODY))
                pairs = pe.snap(i * (BODY // 2))
                rounds16 = pe.snap(i * 16)
                for k in SLOTS:
                    slot(Slot(k), k, r, nxt, loads, unit, heads, heads2, heads4, pairs, rounds16)
            n = N_ROUNDS - 1
            for k in SLOTS:
                slot(Slot(k, last=True), k, ROUNDS - 1, None, None, n * UQ + UQ, n * BODY, n * 2 * BODY, n * 4 * BODY, n * BODY // 2, n * 16)

        @block.scalar
        def _(act):
            act.sem_inc(t_act, 1)

            def copy_nope(u, unit):
                if latent:
                    act.wait_ge(rope_read, unit + (u + 1))
                    wait_q_tok(act, u, unit)
                    nc.scalar.activation(q_tok[u % Q_RING][:, :, 0:64], unit_banks(u, unit)[0][:].rearrange("p (h n) -> p h n", h=4)[:, :, 0:64],
                                         ACT.Copy).then_inc(nope_done, 1)

            def queries_hi(u, unit):
                act.wait_ge(q_turned, unit + (u + 1))
                h = 4 * (u % UQ // 4)
                nc.scalar.activation(qt_hi[:, h:h + 4, P * (u % 4):P * (u % 4) + P],
                                     unit_banks(u, unit)[1][:].rearrange("p (h n) -> p h n", h=4), ACT.Copy).then_inc(q_hi_done, 1)

            def exps(k, order, tiles_done):
                for q in order:
                    n = (3, 0, 2, 1).index(q)
                    act.wait_ge(masked, tiles_done + (4 * k + n + 1 + 4))
                    pr = probs[k % 2][:, P_OFF[q]:P_OFF[q] + P * (q + 1)]
                    last = nc.scalar.activation(pr, pr, ACT.Exp, scale=-1.0, bias=neg_max[k % 2][:, q:q + 1],
                                                accum_out=total[k % 2][:, SUM_COL[q]:SUM_COL[q] + 1])
                if q in (0, 1):
                    last.then_inc(exped, 1)

            def copy_turned(k, n, heads3):
                act.wait_ge(turned, heads3 + (3 * k + n + 1))
                j = TRANS_UNITS[n][0][0]
                m = S - P * j
                nc.scalar.activation(probs_t[k % 2][:, PT_OFF[j]:PT_OFF[j] + m], ps_t[(3 * k + n) % 2][:, 0:m], ACT.Copy)\
                    .then_inc(t_act, 1)

            def values_hi(m, heads, pairs):
                act.wait_ge(valued, heads + (2 * m + 2))
                act.wait_ge(out_done, pairs + (m // 2 * 2 + 2))
                nc.scalar.activation(ot_hi[m % 2][:], ps_v[:], ACT.Copy).then_inc(o_hi_done, 1)

            for u in range(UQ):
                copy_nope(u, 0)
                if u:
                    queries_hi(u - 1, 0)

            def slot(s, k, unit, heads, heads3, tiles_done, pairs):
                if s.pair is not None:
                    values_hi(s.pair, heads, pairs)
                if s.scores:
                    exps(k, (3,), tiles_done)
                if s.values:
                    copy_turned(k - 1, 0, heads3)
                if s.scores:
                    exps(k, (0,), tiles_done)
                    exps(k, (2,), tiles_done)
                if s.values:
                    copy_turned(k - 1, 2, heads3)
                if s.turned_unit is not None:
                    queries_hi(s.turned_unit, unit)
                if s.scores:
                    exps(k, (1,), tiles_done)
                if s.unit is not None:
                    copy_nope(s.unit, unit)

            for k in FIRST_SLOTS:
                slot(Slot(k, first=True), k, None, -BODY, -3 * BODY, -4 * BODY, -BODY // 2)
            with act.Fori(0, N_ROUNDS - 1) as i:
                heads = act.snap(i * BODY)
                unit = act.snap(i * UQ + UQ)
                heads3 = act.snap(i * (3 * BODY))
                tiles_done = act.snap(i * (4 * BODY))
                pairs = act.snap(i * (BODY // 2))
                for k in SLOTS:
                    slot(Slot(k), k, unit, heads, heads3, tiles_done, pairs)
            n = N_ROUNDS - 1
            for k in SLOTS:
                slot(Slot(k, last=True), k, n * UQ + UQ, n * BODY, n * 3 * BODY, n * 4 * BODY, n * BODY // 2)

        @block.vector
        def _(dve):
            dve.sem_inc(masked, 4)
            dve.sem_inc(t_dve, 1)
            dve.sem_inc(o_lo_done, 1)
            dve.sem_inc(added, 1)
            dve.sem_inc(q_lo_done, 1)
            dve.sem_inc(out_done, 2)
            dve.sem_inc(q_bank_read, 1)
            dve.wait_ge(rope_loaded, 32)

            def rotate(u, unit):
                dve.wait_ge(q_done, unit + (u + 1))
                dve.wait_ge(rope_added, unit + (u + 1))
                x = unit_banks(u, unit)[0][:, 0:4 * a.width].rearrange("p (h n) -> p h n", h=4)[:, :, a.width - DR:a.width]
                j = u % 4
                nc.vector.tensor_tensor(rot_a[u % 2][:], x, rope[:, 0, j:j + 1, :].to_broadcast([P, 4, DR]), ALU.mult)
                swapped = x.rearrange("p h (t c) -> p h t c", t=2)[:, :, ::-1, :]
                sines = rope[:, 1, j:j + 1, :].rearrange("p o (t c) -> p o t c", t=2).to_broadcast([P, 4, 2, HALF])
                nc.vector.tensor_tensor(rot_b[u % 2][:].rearrange("p h (t c) -> p h t c", t=2), swapped, sines, ALU.mult)\
                    .then_inc(rope_read, 1)

            def queries_lo(u, unit):
                dve.wait_ge(q_hi_done, unit + (u + 1))
                h = 4 * (u % UQ // 4)
                cols = slice(P * (u % 4), P * (u % 4) + P)
                nc.vector.tensor_tensor(qt_lo[:, h:h + 4, cols], unit_banks(u, unit)[1][:].rearrange("p (h n) -> p h n", h=4),
                                        qt_hi[:, h:h + 4, cols].bitcast(F32), ALU.subtract).then_inc(q_lo_done, 1)

            def mask_and_max(k, n, heads3):
                if n == 0 and (not isinstance(heads3, int) or heads3 + 3 * k >= 6):
                    dve.wait_ge(turned, heads3 + 3 * (k - 1))
                wait_alone(dve, scored, heads3 + (3 * k + n + 1), passed)
                for q, col in SCORE_UNITS[n]:
                    nk = P * (q + 1)
                    nc.vector.tensor_tensor_reduce(
                        out=probs[k % 2][:, P_OFF[q]:P_OFF[q] + nk], in0=ps_s[(3 * k + n) % 2][:, col:col + nk],
                        in1=mask[:, 512 - nk:512], scale=-a.scale, scalar=BIG, op0=ALU.add, op1=ALU.min,
                        accum_out=neg_max[k % 2][:, q:q + 1]).then_inc(masked, 1)

            def invert(k, part, heads2):
                dve.wait_ge(exped, heads2 + (2 * k + part + 1))
                cols = slice(2 * part, 2 * part + 2)
                nc.vector.reciprocal(inverse[k % 2][:, cols], total[k % 2][:, cols]).then_inc(inverted, 1)

            def copy_turned(k, heads3):
                dve.wait_ge(turned, heads3 + (3 * k + 2))
                o = probs_t[k % 2][:, PT_OFF[1]:PT_OFF[1] + 512]
                nc.vector.tensor_copy(o, ps_t[(3 * k + 1) % 2][:]).then_inc(t_dve, 1)

            def values_lo(m, pairs):
                dve.wait_ge(o_hi_done, pairs + (m + 1))
                nc.vector.tensor_tensor(ot_lo[m % 2][:], ps_v[:], ot_hi[m % 2][:].bitcast(F32), ALU.subtract).then_inc(o_lo_done, 1)

            def add_out(c, half, b, pairs):
                dve.wait_ge(out_done, pairs + (2 * c + half + 1 + 2))
                xb = x_res[:].rearrange("p (b g t) d -> p b g (t d)", b=B, g=2)[:, b, half, :]
                nc.vector.tensor_tensor(xb, ps_o[:], xb, ALU.add).then_inc(added, 1)

            for u in range(UQ):
                rotate(u, 0)
                if u:
                    queries_lo(u - 1, 0)

            def slot(s, k, b, unit, heads2, heads3, pairs):
                if s.scores:
                    mask_and_max(k, 0, heads3)
                if s.pair is not None:
                    values_lo(s.pair, pairs)
                if s.scores:
                    mask_and_max(k, 1, heads3)
                if s.out is not None:
                    add_out(s.out, 0, b, pairs)
                if s.scores:
                    mask_and_max(k, 2, heads3)
                if s.values:
                    copy_turned(k - 1, heads3)
                if s.scores:
                    invert(k, 0, heads2)
                if s.unit is not None:
                    rotate(s.unit, unit)
                if s.scores:
                    invert(k, 1, heads2)
                if s.turned_unit is not None:
                    queries_lo(s.turned_unit, unit)
                if s.out is not None:
                    add_out(s.out, 1, b, pairs)

            for k in FIRST_SLOTS:
                slot(Slot(k, first=True), k, None, None, -2 * BODY, -3 * BODY, -BODY // 2)
            with dve.Fori(0, N_ROUNDS - 1) as i:
                b = dve.snap((i >> 2) & (B - 1))
                heads2 = dve.snap(i * (2 * BODY))
                unit = dve.snap(i * UQ + UQ)
                heads3 = dve.snap(i * (3 * BODY))
                pairs = dve.snap(i * (BODY // 2))
                for k in SLOTS:
                    slot(Slot(k), k, b, unit, heads2, heads3, pairs)
            n = N_ROUNDS - 1
            for k in SLOTS:
                slot(Slot(k, last=True), k, B - 1, n * UQ + UQ, n * 2 * BODY, n * 3 * BODY, n * BODY // 2)


def ffn_inputs(nc, sems, hbm, x_res, ident, exponent, w_hi, w_lo, scratch):
    with ExitStack() as ctx:
        def sb(name, shape, dt=F32):
            return ctx.enter_context(nc.sbuf_tensor("fi_" + name, shape, dt))

        U = NT
        wide = 2 * KVH * HD
        raw_kv, raw = sb("raw_kv", [P, KT, wide]), sb("raw", [P, 4, 2048])
        wkv = [sb(n, [P, KT, wide], F32R) for n in ("wkv_hi", "wkv_lo")]
        ln_w = sb("ln_w", [P, D])
        rope = sb("rope", [P, 2, NT, DR])
        stats, mv = sb("stats", [P, U, 6]), sb("mv", [P, U, 2])
        var_eps, rstd = sb("var_eps", [P, U]), sb("rstd", [P, U])
        square, ms, ms_eps, rms = sb("square", [P, U, D]), sb("ms", [P, U]), sb("ms_eps", [P, U]), sb("rms", [P, U])
        h = sb("h", [P, U, D])
        ht_hi, ht_lo = sb("ht_hi", [P, KT, U, P], F32R), sb("ht_lo", [P, KT, U, P], F32R)
        rot_a, rot_b = sb("rot_a", [P, 2, KVH, DR]), sb("rot_b", [P, 2, KVH, DR])
        k_tok, v_tok = sb("k_tok", [P, U, KVH, 2, HD]), sb("v_tok", [P, KVH, U, HD])
        k_stack = sb("k_stack", [P, KVH, U, P], F32R)
        ps_k = [ctx.enter_context(nc.psum_tensor(f"fi_ps_k{u}", [P, 512], F32)) for u in range(U)]
        ps_v = [ctx.enter_context(nc.psum_tensor(f"fi_ps_v{u}", [P, 512], F32)) for u in range(U)]

        loaded, kv_loaded, raw_loaded, x_saved, bn, mean_var, eps_added, rstd_done = (
            sems(n) for n in ("loaded", "kv_loaded", "raw_loaded", "x_saved", "bn", "mean_var", "eps_added", "rstd_done"))
        kv_hi_done, kv_lo_done, w_hi_done, w_lo_done = (sems(n) for n in ("kv_hi_done", "kv_lo_done", "w_hi_done", "w_lo_done"))
        xi_done, squared, ms_eps_added, rms_done, h_done = (
            sems(n) for n in ("xi_done", "squared", "ms_eps_added", "rms_done", "h_done"))
        turned, hi_done, lo_done, projected, rotated, added = (
            sems(n) for n in ("turned", "hi_done", "lo_done", "projected", "rotated", "added"))
        v_done, k_turned, k_hi_done, k_lo_done, passed = (sems(n) for n in ("v_done", "k_turned", "k_hi_done", "k_lo_done", "passed"))
        q_stored, v_stored, k_stored = (sems(n) for n in ("q_stored", "v_stored", "k_stored"))
        block = ctx.enter_context(nc.Block())

        @block.sync
        def _(sp):
            sp.dma_start(raw_kv[:, :, 0:wide // 2], hbm["L0_ffn_wk"].rearrange("(k p) n -> p k n", p=P)).then_inc(kv_loaded, 16)
            sp.dma_start(raw_kv[:, :, wide // 2:wide], hbm["L0_ffn_wv"].rearrange("(k p) n -> p k n", p=P)).then_inc(kv_loaded, 16)
            sp.dma_start(scratch["x1"], x_res[:]).then_inc(x_saved, 16)
            sp.dma_start(ln_w[:], hbm["L0_ffn_ln_w"].rearrange("(o n) -> o n", o=1).to_broadcast([P, D])).then_inc(loaded, 16)
            for k in range(2):
                sp.dma_start(rope[:, k], hbm["rope_ffn"][k].rearrange("(j p) n -> p j n", p=P)).then_inc(loaded, 16)
            sp.dma_start(raw[:, 0:2], hbm["L0_ffn_wq"].rearrange("(k p) n -> p k n", p=P)).then_inc(raw_loaded, 16)
            wo = hbm["L0_ffn_wo"].rearrange("(m p) n -> p m n", p=P)
            sp.dma_start(raw[:, 2:4].rearrange("p k (m n) -> p (k m) n", n=D), wo).then_inc(raw_loaded, 16)
            with sp.Fori(0, B) as b:
                done = sp.snap(b * NT)
                flat = "p k u n -> p k (u n)"
                sp.wait_ge(lo_done, done + NT)
                sp.dma_start(scratch["q_src"][b][:, 0:2], ht_hi[:].bitcast(F32).rearrange(flat)).then_inc(q_stored, 16)
                sp.dma_start(scratch["q_src"][b][:, 2:4], ht_lo[:].bitcast(F32).rearrange(flat)).then_inc(q_stored, 16)
                sp.wait_ge(v_done, done + NT)
                sp.dma_start(scratch["v"][b].rearrange("g p j n -> p g (j n)"), v_tok[:].rearrange("p g j n -> p g (j n)")).then_inc(v_stored, 16)
                for half in range(2):
                    sp.wait_ge(k_lo_done, done * 2 + (NT * (half + 1) + 2 * NT))
                    sp.dma_start(scratch["k"][b].rearrange("g p (x s) -> p g x s", x=2)[:, :, half, :],
                                 k_stack[:, :, 2 * half:2 * half + 2, :].bitcast(F32).rearrange(flat)).then_inc(k_stored, 16)
            sp.wait_ge(q_stored, 32 * (B + 1))
            sp.wait_ge(v_stored, 16 * (B + 1))
            sp.wait_ge(k_stored, 32 * (B + 1))

        @block.gpsimd
        def _(pool):
            pool.sem_inc(q_stored, 32)
            pool.sem_inc(v_stored, 16)
            pool.sem_inc(k_stored, 32)

            def layer_norm(base):
                for u in range(U):
                    wait_alone(pool, mean_var, base + (u + 1), passed)
                    nc.gpsimd.tensor_scalar(var_eps[:, u:u + 1], mv[:, u, 1:2], LN_EPS, 1.0, ALU.add, ALU.mult).then_inc(eps_added, 1)
                    pool.wait_ge(eps_added, base + (u + 1))
                    nc.gpsimd.tensor_tensor(rstd[:, u:u + 1], var_eps[:, u:u + 1], exponent[:], ALU.pow).then_inc(rstd_done, 1)

            def rms_norm(base):
                for u in range(U):
                    wait_alone(pool, squared, base + (u + 1), passed)
                    nc.gpsimd.tensor_scalar(ms_eps[:, u:u + 1], ms[:, u:u + 1], FFN_EPS, 1.0, ALU.add, ALU.mult).then_inc(ms_eps_added, 1)
                    pool.wait_ge(ms_eps_added, base + (u + 1))
                    nc.gpsimd.tensor_tensor(rms[:, u:u + 1], ms_eps[:, u:u + 1], exponent[:], ALU.pow).then_inc(rms_done, 1)

            def twice(t):
                return t.rearrange("p g (o n) -> p g o n", o=1).to_broadcast([P, KVH, 2, HD])

            def add_rotated(tiles, base):
                for u in tiles:
                    pool.wait_ge(rotated, base + (u + 1))
                    nc.gpsimd.tensor_tensor(k_tok[:, u], twice(rot_a[:, u % 2]), twice(rot_b[:, u % 2]), ALU.add).then_inc(added, 1)

            layer_norm(0)
            rms_norm(0)
            with pool.Fori(0, B - 1) as i:
                base = pool.snap(i * U)
                layer_norm(base + U)
                add_rotated((0, 1), base)
                rms_norm(base + U)
                add_rotated((2, 3), base)
            add_rotated(range(U), (B - 1) * U)

        @block.tensor
        def _(pe):
            pe.wait_ge(kv_lo_done, 1)
            with pe.Fori(0, B) as i:
                base = pe.snap(i * U)
                for u in range(U):
                    pe.wait_ge(h_done, base + (u + 1))
                    pe.wait_ge(k_lo_done, base * 2 + (2 * u + 2))
                    for k in range(KT):
                        last = nc.tensor.transpose(ps_k[u][:, P * k:P * k + P], h[:, u, P * k:P * k + P], ident[:])
                    last.then_inc(turned, 1)
                for u in range(U):
                    pe.wait_ge(lo_done, base + (u + 1))
                    for ps, c0 in ((ps_k[u], 0), (ps_v[u], wide // 2)):
                        n = 0
                        for k in range(KT):
                            for x, wt in ((ht_hi, 0), (ht_hi, 1), (ht_lo, 0)):
                                last = nc.tensor.matmul(ps[:], x[:, k, u, :], wkv[wt][:, k, c0:c0 + 512], start=(n == 0), stop=(n == 5))
                                n += 1
                    last.then_inc(projected, 1)
                for u in range(U):
                    pe.wait_ge(added, base + (u + 1))
                    pe.wait_ge(v_done, base + (u + 1))
                    for g, ps in enumerate((ps_k[u], ps_v[u])):
                        for n in range(4):
                            last = nc.tensor.transpose(ps[:, P * n:P * n + P],
                                                       k_tok[:, u, 4 * g + n].rearrange("p o n -> p (o n)"), ident[:])
                        last.then_inc(k_turned, 1)

        @block.scalar
        def _(act):
            act.wait_ge(kv_loaded, 32)
            nc.scalar.activation(wkv[0][:], raw_kv[:], ACT.Copy).then_inc(kv_hi_done, 1)
            xr = x_res[:].rearrange("p (i u) d -> p i u d", u=U)

            def squares(i, base):
                for u in range(U):
                    act.wait_ge(xi_done, base + (u + 1))
                    nc.scalar.activation(square[:, u, :], xr[:, i, u, :], ACT.Square, scale=float(D) ** -0.5,
                                         accum_out=ms[:, u:u + 1]).then_inc(squared, 1)

            def copy_values(tiles, base):
                for u in tiles:
                    act.wait_ge(projected, base + (u + 1))
                    nc.scalar.activation(v_tok[:, :, u, :], ps_v[u][:].rearrange("p (g n) -> p g n", g=KVH), ACT.Copy).then_inc(v_done, 1)

            def batch(i, base, halves, i16, i32, more):
                act.wait_ge(q_stored, i32 + 32)
                for u in range(U):
                    act.wait_ge(turned, base + (u + 1))
                    nc.scalar.activation(ht_hi[:, :, u, :], ps_k[u][:, 0:D].rearrange("p (k n) -> p k n", k=KT), ACT.Copy)\
                        .then_inc(hi_done, 1)
                act.wait_ge(v_stored, i16 + 16)
                copy_values((0, 1), base)
                if more:
                    squares(i + 1, base + U)
                copy_values((2, 3), base)
                act.wait_ge(raw_loaded, 32)
                nc.scalar.activation(w_hi[:, i, :], raw[:, i, :], ACT.Copy).then_inc(w_hi_done, 1)
                act.wait_ge(k_stored, i32 + 32)
                for u in range(U):
                    for g, ps in enumerate((ps_k[u], ps_v[u])):
                        act.wait_ge(k_turned, halves + (2 * u + g + 1))
                        nc.scalar.activation(k_stack[:, 4 * g:4 * g + 4, u, :], ps[:].rearrange("p (g n) -> p g n", g=4), ACT.Copy)\
                            .then_inc(k_hi_done, 1)

            squares(0, 0)
            with act.Fori(0, B - 1) as i:
                batch(i, act.snap(i * U), act.snap(i * (2 * U)), act.snap(i * 16), act.snap(i * 32), True)
            n = B - 1
            batch(n, n * U, n * 2 * U, n * 16, n * 32, False)

        @block.vector
        def _(dve):
            dve.wait_ge(kv_hi_done, 1)
            nc.vector.tensor_tensor(wkv[1][:], raw_kv[:], wkv[0][:].bitcast(F32), ALU.subtract).then_inc(kv_lo_done, 1)
            dve.sem_inc(k_lo_done, 2 * U)
            xr = x_res[:].rearrange("p (i u) d -> p i u d", u=U)

            def statistics(i, base):
                for u in range(U):
                    nc.vector.bn_stats(stats[:, u, :], xr[:, i, u, :]).then_inc(bn, 1)
                for u in range(U):
                    wait_alone(dve, bn, base + (u + 1), passed)
                    nc.vector.bn_aggr(mv[:, u, :], stats[:, u, :]).then_inc(mean_var, 1)

            def layer_norm(i, base):
                dve.wait_ge(x_saved, 16)
                for u in range(U):
                    dve.wait_ge(rstd_done, base + (u + 1))
                    nc.vector.tensor_scalar(xr[:, i, u, :], xr[:, i, u, :], mv[:, u, 0:1], rstd[:, u:u + 1], ALU.subtract, ALU.mult)\
                        .then_inc(xi_done, 1)

            def rms_norm(i, base):
                for u in range(U):
                    dve.wait_ge(rms_done, base + (u + 1))
                    dve.wait_ge(xi_done, base + (u + 1))
                    nc.vector.scalar_tensor_tensor(out=h[:, u, :], in0=xr[:, i, u, :], scalar=rms[:, u:u + 1], in1=ln_w[:],
                                                   op0=ALU.mult, op1=ALU.mult).then_inc(h_done, 1)

            def rotate(tiles, base):
                for u in tiles:
                    dve.wait_ge(projected, base + (u + 1))
                    if u >= 2:
                        dve.wait_ge(added, base + (u - 1))
                    k3 = ps_k[u][:].rearrange("p (g n) -> p g n", g=KVH)
                    nc.vector.tensor_tensor(rot_a[:, u % 2], k3, rope[:, 0, u:u + 1, :].to_broadcast([P, KVH, DR]), ALU.mult)
                    nc.vector.tensor_tensor(rot_b[:, u % 2].rearrange("p g (t c) -> p g t c", t=2),
                                            k3.rearrange("p g (t c) -> p g t c", t=2)[:, :, ::-1, :],
                                            rope[:, 1, u:u + 1, :].rearrange("p o (t c) -> p o t c", t=2).to_broadcast([P, KVH, 2, HALF]),
                                            ALU.mult).then_inc(rotated, 1)

            def batch(i, base, halves, i32, more):
                dve.wait_ge(q_stored, i32 + 32)
                for u in range(U):
                    dve.wait_ge(hi_done, base + (u + 1))
                    nc.vector.tensor_tensor(ht_lo[:, :, u, :], ps_k[u][:, 0:D].rearrange("p (k n) -> p k n", k=KT),
                                            ht_hi[:, :, u, :].bitcast(F32), ALU.subtract).then_inc(lo_done, 1)
                if more:
                    statistics(i + 1, base + U)
                rotate((0,), base)
                if more:
                    layer_norm(i + 1, base + U)
                rotate((1, 2), base)
                if more:
                    rms_norm(i + 1, base + U)
                rotate((3,), base)
                dve.wait_ge(w_hi_done, i + 1)
                nc.vector.tensor_tensor(w_lo[:, i, :], raw[:, i, :], w_hi[:, i, :].bitcast(F32), ALU.subtract).then_inc(w_lo_done, 1)
                for u in range(U):
                    for g, ps in enumerate((ps_k[u], ps_v[u])):
                        dve.wait_ge(k_hi_done, halves + (2 * u + g + 1))
                        ks = k_stack[64:P, 4 * g:4 * g + 4, u, :]
                        nc.vector.tensor_tensor(ks, ps[64:P, :].rearrange("p (g n) -> p g n", g=4), ks.bitcast(F32), ALU.subtract)\
                            .then_inc(k_lo_done, 1)

            statistics(0, 0)
            layer_norm(0, 0)
            dve.wait_ge(loaded, 48)
            rms_norm(0, 0)
            with dve.Fori(0, B - 1) as i:
                batch(i, dve.snap(i * U), dve.snap(i * (2 * U)), dve.snap(i * 32), True)
            n = B - 1
            batch(n, n * U, n * 2 * U, n * 32, False)


def route(nc, sems, hbm, x_res, ident, exponent, gates, h_hi, h_lo, raw13, raw2, expert_loaded, scratch):
    with ExitStack() as ctx:
        def sb(name, shape, dt=F32):
            return ctx.enter_context(nc.sbuf_tensor("rt_" + name, shape, dt))

        U = NT
        ff_w, wg, numbers = sb("ff_w", [P, D]), sb("wg", [P, KT, E]), sb("numbers", [P, E])
        x1 = sb("x1", [P, TILES, D])
        square, ms, ms_eps, rms = sb("square", [P, U, D]), sb("ms", [P, U]), sb("ms_eps", [P, U]), sb("rms", [P, U])
        h, h_now = sb("h", [P, U, D]), sb("h_now", [P, U, D])
        logits, top, index = sb("logits", [P, U, E]), sb("top", [P, U, 8]), sb("index", [P, U, 8], U32)
        index_f, neg, e4, esum, einv, g4 = (sb(n, s) for n, s in (
            ("index_f", [P, U, TOPK]), ("neg", [P, U]), ("e4", [P, U, TOPK]), ("esum", [P, U]), ("einv", [P, U]), ("g4", [P, U, TOPK])))
        hot = sb("hot", [P, U, E, TOPK])
        ps_t = [ctx.enter_context(nc.psum_tensor(f"rt_ps_t{u}", [P, 512], F32)) for u in range(U)]
        ps_l = [ctx.enter_context(nc.psum_tensor(f"rt_ps_l{u}", [P, 512], F32)) for u in range(U)]
        names = ("loaded", "squared", "ms_eps_added", "rms_done", "h_done", "turned", "copied", "h_hi_done", "h_lo_done", "routed",
                 "logits_out", "top_done", "index_done", "index_cast", "neg_done", "exped", "inverted", "g4_done", "hot_done",
                 "numbered", "gated", "x1_loaded", "x1_added", "passed")
        (loaded, squared, ms_eps_added, rms_done, h_done, turned, copied, h_hi_done, h_lo_done, routed, logits_out, top_done,
         index_done, index_cast, neg_done, exped, inverted, g4_done, hot_done, numbered, gated, x1_loaded, x1_added, passed) = (sems(n) for n in names)
        block = ctx.enter_context(nc.Block())

        @block.sync
        def _(sp):
            sp.dma_start(ff_w[:], hbm["L0_ffn_ff_ln_w"].rearrange("(o n) -> o n", o=1).to_broadcast([P, D])).then_inc(loaded, 16)
            sp.dma_start(wg[:], hbm["L0_ffn_wg"].rearrange("(k p) n -> p k n", p=P)).then_inc(loaded, 16)
            sp.dma_start(x1[:], scratch["x1"]).then_inc(x1_loaded, 16)
            for u in range(2):
                load_expert(sp, hbm, raw13[u], raw2[u], (0, u), expert_loaded[u])
            sp.wait_ge(x1_loaded, 16)

        @block.gpsimd
        def _(pool):
            nc.gpsimd.iota(numbers[:], pattern=[[1, E]], base=0, channel_multiplier=0,
                           allow_small_or_imprecise_dtypes=True).then_inc(numbered, 1)
            with pool.Fori(0, TILES // U) as i:
                base = pool.snap(i * U)
                xr, x1r = (t[:].rearrange("p (i n) d -> p i (n d)", n=U) for t in (x_res, x1))
                for u in range(U):
                    wait_alone(pool, squared, base + (u + 1), passed)
                    nc.gpsimd.tensor_scalar(ms_eps[:, u:u + 1], ms[:, u:u + 1], FFN_EPS, 1.0, ALU.add, ALU.mult).then_inc(ms_eps_added, 1)
                    pool.wait_ge(ms_eps_added, base + (u + 1))
                    nc.gpsimd.tensor_tensor(rms[:, u:u + 1], ms_eps[:, u:u + 1], exponent[:], ALU.pow).then_inc(rms_done, 1)
                pool.wait_ge(x1_loaded, 16)
                pool.wait_ge(h_done, base + U)
                nc.gpsimd.tensor_tensor(xr[:, i, :], xr[:, i, :], x1r[:, i, :], ALU.add).then_inc(x1_added, 1)

        @block.tensor
        def _(pe):
            pe.wait_ge(loaded, 32)
            with pe.Fori(0, TILES // U) as i:
                base = pe.snap(i * U)
                for u in range(U):
                    pe.wait_ge(h_done, base + (u + 1))
                    for k in range(KT):
                        last = nc.tensor.transpose(ps_t[u][:, P * k:P * k + P], h[:, u, P * k:P * k + P], ident[:])
                    last.then_inc(turned, 1)
                for u in range(U):
                    pe.wait_ge(copied, base + (u + 1))
                    for k in range(KT):
                        last = nc.tensor.matmul(ps_l[u][:, 0:E], h_now[:, u, P * k:P * k + P], wg[:, k, :], start=(k == 0), stop=(k == KT - 1))
                    last.then_inc(routed, 1)

        @block.scalar
        def _(act):
            xr = x_res[:].rearrange("p (i u) d -> p i u d", u=U)
            hi = h_hi[:].rearrange("p k (i u n) -> p k i u n", u=U, n=P)
            ROUNDS_R = TILES // U

            def squares(i):
                for u in range(U):
                    nc.scalar.activation(square[:, u, :], xr[:, i, u, :], ACT.Square, scale=float(D) ** -0.5,
                                         accum_out=ms[:, u:u + 1]).then_inc(squared, 1)

            def tiles(i, base, more):
                for u in range(U):
                    act.wait_ge(turned, base + (u + 1))
                    nc.scalar.activation(h_now[:, u, :], ps_t[u][:, 0:D], ACT.Copy).then_inc(copied, 1)
                    nc.scalar.activation(hi[:, :, i, u, :], ps_t[u][:, 0:D].rearrange("p (k n) -> p k n", k=KT), ACT.Copy)\
                        .then_inc(h_hi_done, 1)
                if more:
                    squares(i + 1)
                for u in range(U):
                    act.wait_ge(neg_done, i + 1)
                    nc.scalar.activation(e4[:, u, :], top[:, u, 0:TOPK], ACT.Exp, bias=neg[:, u:u + 1],
                                         accum_out=esum[:, u:u + 1]).then_inc(exped, 1)

            squares(0)
            with act.Fori(0, ROUNDS_R - 1) as i:
                tiles(i, act.snap(i * U), True)
            tiles(ROUNDS_R - 1, (ROUNDS_R - 1) * U, False)

        @block.vector
        def _(dve):
            dve.wait_ge(loaded, 32)
            dve.wait_ge(numbered, 1)
            xr = x_res[:].rearrange("p (i u) d -> p i u d", u=U)
            gt = gates[:].rearrange("p (i u) e -> p i u e", u=U)
            hi, lo = (t[:].rearrange("p k (i u n) -> p k i u n", u=U, n=P) for t in (h_hi, h_lo))

            def rms_norm(i, base):
                for u in range(U):
                    dve.wait_ge(rms_done, base + (u + 1))
                    nc.vector.scalar_tensor_tensor(out=h[:, u, :], in0=xr[:, i, u, :], scalar=rms[:, u:u + 1], in1=ff_w[:],
                                                   op0=ALU.mult, op1=ALU.mult).then_inc(h_done, 1)

            def tiles(i, base, base4, more):
                for u in range(U):
                    dve.wait_ge(h_hi_done, base + (u + 1))
                    nc.vector.tensor_tensor(lo[:, :, i, u, :], ps_t[u][:, 0:D].rearrange("p (k n) -> p k n", k=KT),
                                            hi[:, :, i, u, :].bitcast(F32), ALU.subtract).then_inc(h_lo_done, 1)
                for u in range(U):
                    dve.wait_ge(routed, base + (u + 1))
                    nc.vector.tensor_copy(logits[:, u, :], ps_l[u][:, 0:E]).then_inc(logits_out, 1)
                for u in range(U):
                    wait_alone(dve, logits_out, base + (u + 1), passed)
                    nc.vector.max(top[:, u, :], logits[:, u, :]).then_inc(top_done, 1)
                dve.wait_ge(top_done, base + U)
                nc.vector.tensor_scalar(neg[:], top[:, :, 0], -1.0, None, ALU.mult).then_inc(neg_done, 1)
                for u in range(U):
                    nc.vector.max_index(index[:, u, :], top[:, u, :], logits[:, u, :]).then_inc(index_done, 1)
                if more:
                    rms_norm(i + 1, base + U)
                dve.wait_ge(index_done, base + U)
                nc.vector.tensor_copy(index_f[:], index[:, :, 0:TOPK]).then_inc(index_cast, 1)
                dve.wait_ge(exped, base + U)
                nc.vector.reciprocal(einv[:], esum[:]).then_inc(inverted, 1)
                dve.wait_ge(inverted, i + 1)
                nc.vector.tensor_tensor(g4[:], e4[:], einv[:].rearrange("p (u o) -> p u o", o=1).to_broadcast([P, U, TOPK]), ALU.mult)\
                    .then_inc(g4_done, 1)
                dve.wait_ge(g4_done, i + 1)
                dve.wait_ge(index_cast, i + 1)
                for u in range(U):
                    for k in range(TOPK):
                        nc.vector.tensor_scalar(hot[:, u, :, k], numbers[:], index_f[:, u, k:k + 1], g4[:, u, k:k + 1],
                                                ALU.is_equal, ALU.mult).then_inc(hot_done, 1)
                dve.wait_ge(hot_done, base4 + TOPK * U)
                nc.vector.tensor_reduce(gt[:, i], hot[:], AX_X, ALU.add).then_inc(gated, 1)

            rms_norm(0, 0)
            with dve.Fori(0, TILES // U - 1) as i:
                tiles(i, dve.snap(i * U), dve.snap(i * (U * TOPK)), True)
            n = TILES // U - 1
            tiles(n, n * U, n * U * TOPK, False)


def expert_loads(hbm, name, rows):
    return hbm[name].rearrange("(i u) (k p) h -> i u p k h", u=2, p=P)[rows]


def load_expert(sp, hbm, raw13, raw2, rows, loaded):
    for n, name in enumerate(("L0_ffn_w1", "L0_ffn_w3")):
        sp.dma_start(raw13[:, :, H * n:H * n + H], expert_loads(hbm, name, rows)).then_inc(loaded, 16)
    sp.dma_start(raw2[:], expert_loads(hbm, "L0_ffn_w2", rows)).then_inc(loaded, 16)


def experts_dense(nc, sems, hbm, x_res, gates, h_hi, h_lo, raw13, raw2, loaded, out):
    with ExitStack() as ctx:
        def sb(name, shape, dt=F32):
            return ctx.enter_context(nc.sbuf_tensor("ex_" + name, shape, dt))

        U, G, C = 2, B, H // P
        w13 = [[sb(f"w13_{part}{u}", [P, KT, 2 * H], F32R) for part in ("hi", "lo")] for u in range(U)]
        w2 = [[sb(f"w2_{part}{u}", [P, KT, D], F32R) for part in ("hi", "lo")] for u in range(U)]
        silu = [sb(f"silu{c}", [P, S]) for c in range(C)]
        a = [sb(f"a{c}", [P, S]) for c in range(C)]
        a_hi = [[sb(f"a_hi{r}{c}", [P, S], F32R) for c in range(C)] for r in range(2)]
        a_lo = [[sb(f"a_lo{r}{c}", [P, S], F32R) for c in range(C)] for r in range(2)]
        ps_g, ps_u = ([ctx.enter_context(nc.psum_tensor(f"ex_{n}{c}", [P, S], F32)) for c in range(C)] for n in ("ps_g", "ps_u"))
        ps_y = [ctx.enter_context(nc.psum_tensor(f"ex_ps_y{r}", [P, 512], F32)) for r in range(4)]
        names = ("w_hi", "w_lo", "up", "silued", "mixed", "a_hi_done", "a_lo_done", "down", "added", "stored")
        w_hi, w_lo, up, silued, mixed, a_hi_done, a_lo_done, down, added, stored = (sems(n) for n in names)
        block = ctx.enter_context(nc.Block())
        STEPS = U * G
        ROUNDS_E = E // U
        PASSES = ((0, 0), (0, 1), (1, 0))

        @block.sync
        def _(sp):
            with sp.Fori(0, ROUNDS_E - 1) as i:
                split = sp.snap(i * U)
                for u in range(U):
                    sp.wait_ge(w_lo, split + (u + 1))
                    load_expert(sp, hbm, raw13[u], raw2[u], (i + 1, u), loaded[u])
            for g in range(G):
                sp.wait_ge(added, NT * G * (E - 1) + NT * (g + 1) + 8)
                sp.dma_start(out[g].rearrange("(j p) d -> p j d", p=P), x_res[:, NT * g:NT * g + NT, :]).then_inc(stored, 16)
            sp.wait_ge(stored, 16 * G)

        @block.tensor
        def _(pe):
            def gate_up(s, c, base2, experts):
                u, g = s // G, s % G
                if g == 0 and c == 0:
                    pe.wait_ge(w_lo, experts + (u + 1))
                pe.wait_ge(mixed, base2 + (2 * s + c + 1))
                for ps, c0 in ((ps_g[c], P * c), (ps_u[c], H + P * c)):
                    n = 0
                    for k in range(KT):
                        for wt, x in PASSES:
                            last = nc.tensor.matmul(ps[:], w13[u][wt][:, k, c0:c0 + P], (h_hi, h_lo)[x][:, k, S * g:S * g + S],
                                                    start=(n == 0), stop=(n == 3 * KT - 1))
                            n += 1
                last.then_inc(up, 1)

            def project(s, base2, base4):
                pe.wait_ge(a_lo_done, base2 + (2 * s + 2))
                for half in range(2):
                    pe.wait_ge(added, base4 + (4 * s + 2 * half + 2))
                    for t in (2 * half, 2 * half + 1):
                        n = 0
                        for k in range(C):
                            for x, wt in PASSES:
                                last = nc.tensor.matmul(ps_y[2 * (s % 2) + half][:, D * (t % 2):D * (t % 2) + D],
                                                        (a_hi, a_lo)[x][s % 2][k][:, P * t:P * t + P],
                                                        w2[s // G % 2][wt][:, k, :], start=(n == 0), stop=(n == 3 * C - 1))
                                n += 1
                    last.then_inc(down, 1)

            gate_up(0, 0, 0, 0)
            gate_up(0, 1, 0, 0)
            with pe.Fori(0, ROUNDS_E - 1) as i:
                base2 = pe.snap(i * (2 * STEPS))
                base4 = pe.snap(i * (4 * STEPS))
                experts = pe.snap(i * U)
                for s in range(1, STEPS + 1):
                    gate_up_of = s % STEPS
                    ahead = (2 * STEPS, U) if s == STEPS else (0, 0)
                    gate_up(gate_up_of, 0, base2 + ahead[0], experts + ahead[1])
                    gate_up(gate_up_of, 1, base2 + ahead[0], experts + ahead[1])
                    project(s - 1, base2, base4)
            n = ROUNDS_E - 1
            for s in range(1, STEPS + 1):
                if s < STEPS:
                    gate_up(s, 0, n * 2 * STEPS, n * U)
                    gate_up(s, 1, n * 2 * STEPS, n * U)
                project(s - 1, n * 2 * STEPS, n * 4 * STEPS)

        @block.scalar
        def _(act):
            def split_hi(u, loads, downs):
                act.wait_ge(loaded[u], loads)
                if downs is not None:
                    act.wait_ge(down, downs)
                nc.scalar.activation(w13[u][0][:], raw13[u][:], ACT.Copy)
                nc.scalar.activation(w2[u][0][:], raw2[u][:], ACT.Copy).then_inc(w_hi, 1)

            def step(s, base2):
                for c in range(C):
                    act.wait_ge(up, base2 + (2 * s + c + 1))
                    nc.scalar.activation(silu[c][:], ps_g[c][:], ACT.Silu).then_inc(silued, 1)
                for c in range(C):
                    act.wait_ge(mixed, base2 + (2 * s + c + 1 + 2))
                    if c == 0:
                        act.wait_ge(down, base2 + (2 * s - 2 + 4))
                    nc.scalar.activation(a_hi[s % 2][c][:], a[c][:], ACT.Copy).then_inc(a_hi_done, 1)

            def round_of(base2, loads, last):
                for s in range(STEPS):
                    step(s, base2)
                    if s == 2:
                        split_hi(1, loads + 48, base2 + 4)
                    if s == G + 2 and not last:
                        split_hi(0, loads + 96, base2 + (2 * G + 4))

            split_hi(0, 48, None)
            with act.Fori(0, ROUNDS_E - 1) as i:
                round_of(act.snap(i * (2 * STEPS)), act.snap(i * 48), False)
            round_of((ROUNDS_E - 1) * 2 * STEPS, (ROUNDS_E - 1) * 48, True)

        @block.vector
        def _(dve):
            dve.sem_inc(mixed, 2)
            dve.sem_inc(added, 8)
            dve.sem_inc(down, 4)

            def split_lo(u, splits):
                dve.wait_ge(w_hi, splits)
                nc.vector.tensor_tensor(w13[u][1][:], raw13[u][:], w13[u][0][:].bitcast(F32), ALU.subtract)
                nc.vector.tensor_tensor(w2[u][1][:], raw2[u][:], w2[u][0][:].bitcast(F32), ALU.subtract).then_inc(w_lo, 1)

            def add(s, base2, i):
                u, g = s // G, s % G
                for t in range(NT):
                    if t % 2 == 0:
                        dve.wait_ge(down, base2 + (2 * s + t // 2 + 1 + 4))
                    j = NT * g + t
                    gt = gates[:].rearrange("p t (i u) -> p t i u", u=U)[:, j, i, u:u + 1]
                    nc.vector.scalar_tensor_tensor(out=x_res[:, j, :], in0=ps_y[2 * (s % 2) + t // 2][:, D * (t % 2):D * (t % 2) + D],
                                                   scalar=gt, in1=x_res[:, j, :], op0=ALU.mult, op1=ALU.add).then_inc(added, 1)

            def step(s, base2):
                for c in range(C):
                    dve.wait_ge(silued, base2 + (2 * s + c + 1))
                    if not isinstance(base2, int) or base2 + s > 0:
                        dve.wait_ge(a_lo_done, base2 + (2 * s + c - 1))
                    nc.vector.tensor_tensor(a[c][:], ps_u[c][:], silu[c][:], ALU.mult).then_inc(mixed, 1)
                for c in range(C):
                    dve.wait_ge(a_hi_done, base2 + (2 * s + c + 1))
                    nc.vector.tensor_tensor(a_lo[s % 2][c][:], a[c][:], a_hi[s % 2][c][:].bitcast(F32), ALU.subtract)\
                        .then_inc(a_lo_done, 1)

            def round_of(i, base2, splits, last):
                for s in range(1, STEPS + 1):
                    if s < STEPS:
                        step(s, base2)
                    elif not last:
                        step(0, base2 + 2 * STEPS)
                    if s == 2:
                        split_lo(1, splits + 2)
                    if s == G + 2 and not last:
                        split_lo(0, splits + 3)
                    add(s - 1, base2, i)

            split_lo(0, 1)
            step(0, 0)
            with dve.Fori(0, ROUNDS_E - 1) as i:
                round_of(i, dve.snap(i * (2 * STEPS)), dve.snap(i * U), False)
            round_of(ROUNDS_E - 1, (ROUNDS_E - 1) * 2 * STEPS, (ROUNDS_E - 1) * U, True)


def build(nc, hbm, out, upto=9):
    with ExitStack() as ctx:
        def sb(name, shape, dt=F32, c=ctx):
            return c.enter_context(nc.sbuf_tensor(name, shape, dt))

        def dram(name, shape):
            return nc.dram_tensor("scratch_" + name, shape, F32, kind="Internal").ap()

        x_res = sb("x_res", [P, TILES, D])
        ident, mask, exponent = sb("ident", [P, P]), sb("mask", [P, S]), sb("exponent", [P, 1])
        start_constants(nc, Sems(nc, ctx, "sc"), ident, mask, exponent)

        with ExitStack() as layer:
            w = {n: sb(n, [P, NH * P], F32R, layer) for n in ("w1hi", "w1lo", "w2hi", "w2lo")}
            w |= {n: sb(n, [P, NH // 2, D], F32R, layer) for n in ("vohi", "volo")}
            latent_scratch = {"q_src": dram("lq", [B, P, 3, S]), "k": dram("lk", [B, P, 2, S]), "v": dram("lv", [B, P, NT, KVLR])}
            prepare_latent_weights(nc, Sems(nc, ctx, "lw"), hbm, w, ident, x_res)
            latent_inputs(nc, Sems(nc, ctx, "li"), hbm, x_res, ident, exponent, latent_scratch)
            q_passes = [(0, w["w1hi"][:]), (0, w["w1lo"][:]), (1, w["w1hi"][:]), (2, w["w2hi"][:]), (2, w["w2lo"][:])]
            latent = Attention("la", float(DN + DR) ** -0.5, 3, P, q_passes, 2, [(0, 0), (0, 1), (1, 0)],
                               w["vohi"][:], w["volo"][:], latent_scratch, hbm["rope_latent"])
            attention(nc, Sems(nc, ctx, "la"), latent, x_res, ident, mask)
        if upto >= 2:
            with ExitStack() as layer:
                w_hi, w_lo = (sb(n, [P, 4, NH * HD], F32R, layer) for n in ("wqo_hi", "wqo_lo"))
                ffn_scratch = {"q_src": dram("fq", [B, P, 4, S]), "k": dram("fk", [B, KVH, P, S]),
                               "v": dram("fv", [B, KVH, P, NT, HD]), "x1": dram("x1", [P, TILES, D])}
                ffn_inputs(nc, Sems(nc, ctx, "fi"), hbm, x_res, ident, exponent, w_hi, w_lo, ffn_scratch)
                q_passes = [p for k in range(KT) for p in ((k, w_hi[:, k, :]), (k, w_lo[:, k, :]), (2 + k, w_hi[:, k, :]))]
                views = dict(ffn_scratch, k=ffn_scratch["k"].rearrange("b (r c) p (o s) -> b r c p o s", r=ROUNDS, o=1),
                             v=ffn_scratch["v"].rearrange("b (r c) p j n -> b r c p j n", r=ROUNDS))
                grouped = Attention("ga", float(HD) ** -0.5, 4, HD, q_passes, 1, [(0, 0), (1, 0)],
                                    *(t[:, 2:4, :].rearrange("p k (m n) -> p (k m) n", n=D) for t in (w_hi, w_lo)), views, hbm["rope_ffn"])
                attention(nc, Sems(nc, ctx, "ga"), grouped, x_res, ident, mask)
        if upto >= 3:
            h_hi, h_lo = sb("h_hi", [P, KT, B * S], F32R), sb("h_lo", [P, KT, B * S], F32R)
            gates = sb("gates", [P, TILES, E])
            raw13, raw2 = ([sb(f"{n}_{u}", [P, KT, width]) for u in range(2)] for n, width in (("raw13", 2 * H), ("raw2", D)))
            loaded = [ctx.enter_context(nc.semaphore(f"expert_loaded{u}")) for u in range(2)]
            route(nc, Sems(nc, ctx, "rt"), hbm, x_res, ident, exponent, gates, h_hi, h_lo, raw13, raw2, loaded, ffn_scratch)
            experts_dense(nc, Sems(nc, ctx, "ex"), hbm, x_res, gates, h_hi, h_lo, raw13, raw2, loaded, out)
        else:
            stored = ctx.enter_context(nc.semaphore("stored"))
            block = ctx.enter_context(nc.Block())

            @block.sync
            def _(sp):
                sp.dma_start(out.rearrange("b (j p) d -> p (b j) d", p=P), x_res[:]).then_inc(stored, 16)
                sp.wait_ge(stored, 16)


_INS = ["L0_attn_hidden_states", "L0_attn_q_a_w", "L0_attn_q_a_ln_w", "L0_attn_q_b_w", "L0_attn_kv_a_w", "L0_attn_kv_a_ln_w",
        "L0_attn_kv_b_w", "L0_attn_o_w", "L0_ffn_ln_w", "L0_ffn_ff_ln_w", "L0_ffn_wq", "L0_ffn_wk", "L0_ffn_wv", "L0_ffn_wo",
        "L0_ffn_wg", "L0_ffn_w1", "L0_ffn_w3", "L0_ffn_w2"]


def rope_table(base):
    half = np.arange(HALF, dtype=np.float32) / np.float32(HALF)
    angle = np.arange(S, dtype=np.float32)[:, None] * (np.float32(1.0) / np.float32(base) ** half)
    cos, sin = np.cos(angle), np.sin(angle)
    return np.stack([np.concatenate([cos, cos], 1), np.concatenate([-sin, sin], 1)]).astype(np.float32)


def kernel(**inputs):
    import concourse.bacc as bacc
    from concourse.bass_utils import run_bass_kernel_spmd

    nc = bacc.Bacc("TRN2", target_bir_lowering=False, num_devices=1)
    arrays = {n: np.ascontiguousarray(inputs[n]) for n in _INS}
    arrays |= {"rope_latent": rope_table(10000.0), "rope_ffn": rope_table(150000.0)}
    hbm = {n: nc.dram_tensor("in_" + n, a.shape, mybir.dt.from_np(a.dtype), kind="ExternalInput").ap() for n, a in arrays.items()}
    out = nc.dram_tensor("out_x", (B, S, D), F32, kind="ExternalOutput").ap()
    build(nc, hbm, out)
    r = run_bass_kernel_spmd(nc, [{"in_" + n: a for n, a in arrays.items()}], core_ids=[0])
    return r.results[0]["out_x"]
```
